# Optimizing a Trainium2 kernel written in Bass

```python
import numpy as np
import jax
import jax.numpy as jnp

def _softmax(x, axis=-1):
    return jax.nn.softmax(x, axis=axis)

def _gelu(x):
    return jax.nn.gelu(x, approximate=True)

def _silu(x):
    return jax.nn.silu(x)

def _sigmoid(x):
    return jax.nn.sigmoid(x)

def _layernorm(x, axis=-1, eps=1e-05):
    m = jnp.mean(x, axis=axis, keepdims=True)
    v = jnp.var(x, axis=axis, keepdims=True)
    return (x - m) / jnp.sqrt(v + eps)

def _scatter_add(tgt, idx, src, axis=0):
    return tgt.at[idx].add(src)

def _segment_sum(src, seg, n):
    return jax.ops.segment_sum(src, seg, n)
kernel_name = 'mk_sandwich_d2_jaxref_r8_bbd82f'

def setup_inputs(seed: int=0):
    np.random.seed(seed)
    _w = jnp.asarray

    def _L0_attn_setup():
        import math
        import jax, jax.numpy as jnp
        import numpy as np
        D_MODEL = 128
        N_HEAD = 16
        HEAD_DIM = D_MODEL // N_HEAD
        B, T = (2, 256)

        def _layernorm(x, g, b, eps=1e-05):
            mu = jnp.mean(x, axis=-1, keepdims=True)
            var = jnp.mean(jnp.square(x - mu), axis=-1, keepdims=True)
            return (x - mu) * jax.lax.rsqrt(var + eps) * g + b

        def _l2norm(x, eps=1e-12):
            n = jnp.sqrt(jnp.sum(jnp.square(x), axis=-1, keepdims=True))
            return x / jnp.maximum(n, eps)

        def _rope(x, times):
            half = x.shape[-1] // 2
            freqs = jnp.exp(-jnp.arange(half, dtype=x.dtype) * (math.log(10000.0) / half))
            theta = times[:, None] * freqs[None, :]
            cos = jnp.cos(theta)[None, :, None, :]
            sin = jnp.sin(theta)[None, :, None, :]
            xr = x.reshape(*x.shape[:-1], half, 2)
            x1, x2 = (xr[..., 0], xr[..., 1])
            r1 = x1 * cos - x2 * sin
            r2 = x1 * sin + x2 * cos
            return jnp.stack([r1, r2], axis=-1).reshape(x.shape)
        key = jax.random.key(seed)
        ks = jax.random.split(key, 16)
        s = 0.02
        f32 = jnp.float32
        inp = {'x': jax.random.normal(ks[0], (B, T, D_MODEL), f32), 'Wq': jax.random.normal(ks[1], (D_MODEL, D_MODEL), f32) * s, 'Wk': jax.random.normal(ks[2], (D_MODEL, D_MODEL), f32) * s, 'Wv': jax.random.normal(ks[3], (D_MODEL, D_MODEL), f32) * s, 'gate_w': jax.random.normal(ks[4], (D_MODEL, D_MODEL), f32) * s, 'gate_b': jnp.zeros((D_MODEL,), f32), 'p_w': jax.random.normal(ks[5], (D_MODEL, D_MODEL), f32) * s, 'p_b': jnp.zeros((D_MODEL,), f32), 'out_w': jax.random.normal(ks[6], (D_MODEL, D_MODEL), f32) * s, 'out_b': jnp.zeros((D_MODEL,), f32), 'clock_w': jax.random.normal(ks[7], (D_MODEL, N_HEAD), f32) * s, 'clock_b': jnp.zeros((N_HEAD,), f32), 'ln1_g': jnp.ones((D_MODEL,), f32), 'ln1_b': jnp.zeros((D_MODEL,), f32), 'ln2_g': jnp.ones((D_MODEL,), f32), 'ln2_b': jnp.zeros((D_MODEL,), f32), 'mlp_w1': jax.random.normal(ks[8], (D_MODEL, 4 * D_MODEL), f32) * s, 'mlp_b1': jnp.zeros((4 * D_MODEL,), f32), 'mlp_w2': jax.random.normal(ks[9], (4 * D_MODEL, D_MODEL), f32) * s, 'mlp_b2': jnp.zeros((D_MODEL,), f32)}
        return inp
    _L0_attn_in = _L0_attn_setup()

    def _L0_ffn_setup():
        import jax, jax.numpy as jnp
        import numpy as np
        B, S, D, F, E = (8, 128, 128, 512, 8)
        EPS = 1e-05
        key = jax.random.key(seed)
        ks = jax.random.split(key, 4)
        s = 0.02
        return {'input_features': jax.random.normal(ks[0], (B, S, D), jnp.float32), 'centroids': jax.random.normal(ks[1], (E, D), jnp.float32) * 0.1, 'ln_g': jnp.ones((E, D), jnp.float32), 'ln_b': jnp.zeros((E, D), jnp.float32), 'w1': jax.random.normal(ks[2], (E, D, F), jnp.float32) * s, 'b1': jnp.zeros((E, F), jnp.float32), 'w2': jax.random.normal(ks[3], (E, F, D), jnp.float32) * s, 'b2': jnp.zeros((E, D), jnp.float32)}
    _L0_ffn_in = _L0_ffn_setup()

    def _L1_attn_setup():
        import jax, jax.numpy as jnp
        import numpy as np
        BATCH, L, D_MODEL = (2, 128, 128)
        D_STATE, D_CONV, EXPAND = (16, 4, 2)
        D_INNER = EXPAND * D_MODEL
        DT_RANK = max(1, -(-D_MODEL // 16))

        def _forward(x, W_in, conv_w, conv_b, W_x, W_dt, b_dt, A_log, D, W_out):
            xv = x @ W_in
            xc = jnp.transpose(xv, (0, 2, 1))
            xc = jax.lax.conv_general_dilated(xc, conv_w, window_strides=(1,), padding=[(D_CONV - 1, 0)], dimension_numbers=('NCH', 'OIH', 'NCH'), feature_group_count=D_INNER)
            xv = jnp.transpose(xc, (0, 2, 1)) + conv_b
            xv = jax.nn.silu(xv)
            ssm = xv @ W_x
            dt_raw = ssm[..., :DT_RANK]
            Bp = ssm[..., DT_RANK:DT_RANK + D_STATE]
            Cp = ssm[..., DT_RANK + D_STATE:]
            delta = jax.nn.softplus(dt_raw @ W_dt + b_dt)
            A = -jnp.exp(A_log)
            dA = jnp.exp(delta[..., None] * A)
            dBx = delta[..., None] * Bp[:, :, None, :] * xv[..., None]

            def comb(c1, c2):
                a1, b1 = c1
                a2, b2 = c2
                return (a1 * a2, a2 * b1 + b2)
            _, h = jax.lax.associative_scan(comb, (dA, dBx), axis=1)
            y = jnp.einsum('bldn,bln->bld', h, Cp)
            y = y + xv * D
            return y @ W_out
        key = jax.random.key(seed)
        ks = jax.random.split(key, 10)
        s = 0.02
        x = jax.random.normal(ks[0], (BATCH, L, D_MODEL), jnp.float32)
        W_in = jax.random.normal(ks[1], (D_MODEL, D_INNER), jnp.float32) * s
        conv_w = jax.random.normal(ks[2], (D_INNER, 1, D_CONV), jnp.float32) * s
        conv_b = jax.random.normal(ks[3], (D_INNER,), jnp.float32) * s
        W_x = jax.random.normal(ks[4], (D_INNER, DT_RANK + 2 * D_STATE), jnp.float32) * s
        W_dt = jax.random.normal(ks[5], (DT_RANK, D_INNER), jnp.float32) * s
        b_dt = jax.random.normal(ks[6], (D_INNER,), jnp.float32) * s
        A_log = jnp.log(jnp.broadcast_to(jnp.arange(1, D_STATE + 1, dtype=jnp.float32), (D_INNER, D_STATE)))
        D = jnp.ones((D_INNER,), jnp.float32)
        W_out = jax.random.normal(ks[7], (D_INNER, D_MODEL), jnp.float32) * s
        return {'x': x, 'W_in': W_in, 'conv_w': conv_w, 'conv_b': conv_b, 'W_x': W_x, 'W_dt': W_dt, 'b_dt': b_dt, 'A_log': A_log, 'D': D, 'W_out': W_out}
    _L1_attn_in = _L1_attn_setup()

    def _L1_ffn_setup():
        import jax, jax.numpy as jnp
        import numpy as np
        B, S, DIM = (4, 512, 128)
        BASE_COUPLING = 0.1
        NUM_CYCLES = 3

        def _gelu(x):
            return jax.nn.gelu(x, approximate=False)

        def _coupling_net(h, w1, b1, w2, b2, w3, b3, w4, b4):
            h = _gelu(h @ w1 + b1)
            h = _gelu(h @ w2 + b2)
            h = _gelu(h @ w3 + b3)
            return jax.nn.sigmoid(h @ w4 + b4)

        def _global_net(h, w1, b1, w2, b2, w3, b3):
            h = _gelu(h @ w1 + b1)
            h = _gelu(h @ w2 + b2)
            return jax.nn.sigmoid(h @ w3 + b3)

        def _twist(x):
            o_r, o_i, p_r, p_i = jnp.split(x, 4, axis=-1)
            return jnp.concatenate([p_r, -p_i, -o_r, o_i], axis=-1)
        key = jax.random.key(seed)
        ks = jax.random.split(key, 9)
        d = DIM

        def w(k, fan_in, fan_out):
            return jax.random.normal(k, (fan_in, fan_out), dtype=jnp.float32) / np.sqrt(fan_in).astype(np.float32)
        inp = {'x': jax.random.normal(ks[0], (B, S, d), dtype=jnp.float32)}
        cn_dims = [(d, d), (d, d // 2), (d // 2, d // 4), (d // 4, 1)]
        for i, (a, b) in enumerate(cn_dims):
            inp[f'cn_w{i + 1}'] = w(ks[1 + i], a, b)
            inp[f'cn_b{i + 1}'] = jnp.zeros((b,), dtype=jnp.float32)
        gc_dims = [(d, d // 2), (d // 2, d // 4), (d // 4, 1)]
        for i, (a, b) in enumerate(gc_dims):
            inp[f'gc_w{i + 1}'] = w(ks[5 + i], a, b)
            inp[f'gc_b{i + 1}'] = jnp.zeros((b,), dtype=jnp.float32)
        inp['adaptive_range'] = jnp.full((1,), 0.2, dtype=jnp.float32)
        return inp
    _L1_ffn_in = _L1_ffn_setup()
    _d = {'L0_attn_x': _L0_attn_in['x'], 'L0_attn_Wq': _L0_attn_in['Wq'], 'L0_attn_Wk': _L0_attn_in['Wk'], 'L0_attn_Wv': _L0_attn_in['Wv'], 'L0_attn_gate_w': _L0_attn_in['gate_w'], 'L0_attn_gate_b': _L0_attn_in['gate_b'], 'L0_attn_p_w': _L0_attn_in['p_w'], 'L0_attn_p_b': _L0_attn_in['p_b'], 'L0_attn_out_w': _L0_attn_in['out_w'], 'L0_attn_out_b': _L0_attn_in['out_b'], 'L0_attn_clock_w': _L0_attn_in['clock_w'], 'L0_attn_clock_b': _L0_attn_in['clock_b'], 'L0_attn_ln1_g': _L0_attn_in['ln1_g'], 'L0_attn_ln1_b': _L0_attn_in['ln1_b'], 'L0_attn_ln2_g': _L0_attn_in['ln2_g'], 'L0_attn_ln2_b': _L0_attn_in['ln2_b'], 'L0_attn_mlp_w1': _L0_attn_in['mlp_w1'], 'L0_attn_mlp_b1': _L0_attn_in['mlp_b1'], 'L0_attn_mlp_w2': _L0_attn_in['mlp_w2'], 'L0_attn_mlp_b2': _L0_attn_in['mlp_b2'], 'L0_ffn_centroids': _L0_ffn_in['centroids'], 'L0_ffn_ln_g': _L0_ffn_in['ln_g'], 'L0_ffn_ln_b': _L0_ffn_in['ln_b'], 'L0_ffn_w1': _L0_ffn_in['w1'], 'L0_ffn_b1': _L0_ffn_in['b1'], 'L0_ffn_w2': _L0_ffn_in['w2'], 'L0_ffn_b2': _L0_ffn_in['b2'], 'L1_attn_W_in': _L1_attn_in['W_in'], 'L1_attn_conv_w': _L1_attn_in['conv_w'], 'L1_attn_conv_b': _L1_attn_in['conv_b'], 'L1_attn_W_x': _L1_attn_in['W_x'], 'L1_attn_W_dt': _L1_attn_in['W_dt'], 'L1_attn_b_dt': _L1_attn_in['b_dt'], 'L1_attn_A_log': _L1_attn_in['A_log'], 'L1_attn_D': _L1_attn_in['D'], 'L1_attn_W_out': _L1_attn_in['W_out'], 'L1_ffn_cn_w1': _L1_ffn_in['cn_w1'], 'L1_ffn_cn_b1': _L1_ffn_in['cn_b1'], 'L1_ffn_cn_w2': _L1_ffn_in['cn_w2'], 'L1_ffn_cn_b2': _L1_ffn_in['cn_b2'], 'L1_ffn_cn_w3': _L1_ffn_in['cn_w3'], 'L1_ffn_cn_b3': _L1_ffn_in['cn_b3'], 'L1_ffn_cn_w4': _L1_ffn_in['cn_w4'], 'L1_ffn_cn_b4': _L1_ffn_in['cn_b4'], 'L1_ffn_gc_w1': _L1_ffn_in['gc_w1'], 'L1_ffn_gc_b1': _L1_ffn_in['gc_b1'], 'L1_ffn_gc_w2': _L1_ffn_in['gc_w2'], 'L1_ffn_gc_b2': _L1_ffn_in['gc_b2'], 'L1_ffn_gc_w3': _L1_ffn_in['gc_w3'], 'L1_ffn_gc_b3': _L1_ffn_in['gc_b3'], 'L1_ffn_adaptive_range': _L1_ffn_in['adaptive_range']}
    _x0 = _d['L0_attn_x']
    _d['L0_attn_x'] = jax.random.normal(jax.random.fold_in(jax.random.key(seed), 1), (32, 256, 128), dtype=_x0.dtype)
    del _x0
    return _d

def reference(L0_attn_x, L0_attn_Wq, L0_attn_Wk, L0_attn_Wv, L0_attn_gate_w, L0_attn_gate_b, L0_attn_p_w, L0_attn_p_b, L0_attn_out_w, L0_attn_out_b, L0_attn_clock_w, L0_attn_clock_b, L0_attn_ln1_g, L0_attn_ln1_b, L0_attn_ln2_g, L0_attn_ln2_b, L0_attn_mlp_w1, L0_attn_mlp_b1, L0_attn_mlp_w2, L0_attn_mlp_b2, L0_ffn_centroids, L0_ffn_ln_g, L0_ffn_ln_b, L0_ffn_w1, L0_ffn_b1, L0_ffn_w2, L0_ffn_b2, L1_attn_W_in, L1_attn_conv_w, L1_attn_conv_b, L1_attn_W_x, L1_attn_W_dt, L1_attn_b_dt, L1_attn_A_log, L1_attn_D, L1_attn_W_out, L1_ffn_cn_w1, L1_ffn_cn_b1, L1_ffn_cn_w2, L1_ffn_cn_b2, L1_ffn_cn_w3, L1_ffn_cn_b3, L1_ffn_cn_w4, L1_ffn_cn_b4, L1_ffn_gc_w1, L1_ffn_gc_b1, L1_ffn_gc_w2, L1_ffn_gc_b2, L1_ffn_gc_w3, L1_ffn_gc_b3, L1_ffn_adaptive_range):

    def _L0_attn_ref(x, Wq, Wk, Wv, gate_w, gate_b, p_w, p_b, out_w, out_b, clock_w, clock_b, ln1_g, ln1_b, ln2_g, ln2_b, mlp_w1, mlp_b1, mlp_w2, mlp_b2):
        import math
        import jax, jax.numpy as jnp
        import numpy as np
        D_MODEL = 128
        N_HEAD = 16
        HEAD_DIM = D_MODEL // N_HEAD
        B, T = (2, 256)

        def _layernorm(x, g, b, eps=1e-05):
            mu = jnp.mean(x, axis=-1, keepdims=True)
            var = jnp.mean(jnp.square(x - mu), axis=-1, keepdims=True)
            return (x - mu) * jax.lax.rsqrt(var + eps) * g + b

        def _l2norm(x, eps=1e-12):
            n = jnp.sqrt(jnp.sum(jnp.square(x), axis=-1, keepdims=True))
            return x / jnp.maximum(n, eps)

        def _rope(x, times):
            half = x.shape[-1] // 2
            freqs = jnp.exp(-jnp.arange(half, dtype=x.dtype) * (math.log(10000.0) / half))
            theta = times[:, None] * freqs[None, :]
            cos = jnp.cos(theta)[None, :, None, :]
            sin = jnp.sin(theta)[None, :, None, :]
            xr = x.reshape(*x.shape[:-1], half, 2)
            x1, x2 = (xr[..., 0], xr[..., 1])
            r1 = x1 * cos - x2 * sin
            r2 = x1 * sin + x2 * cos
            return jnp.stack([r1, r2], axis=-1).reshape(x.shape)
        Bx, Tx, D = x.shape
        H, Dh = (N_HEAD, HEAD_DIM)
        residual = x
        xn = _layernorm(x, ln1_g, ln1_b)
        times = jnp.arange(Tx, dtype=x.dtype)
        q = _l2norm((xn @ Wq).reshape(Bx, Tx, H, Dh))
        k = _l2norm((xn @ Wk).reshape(Bx, Tx, H, Dh))
        v = (xn @ Wv).reshape(Bx, Tx, H, Dh)
        clock = jax.nn.softplus(xn @ clock_w + clock_b).reshape(Bx, Tx, H, 1)
        q = _rope(q, times)
        k = _rope(k, times)
        gj = -jax.nn.softplus(xn @ gate_w + gate_b).reshape(Bx, Tx, H, Dh)
        gcp = jnp.exp(jnp.clip(jnp.cumsum(gj, axis=1), -60.0, 50.0))
        q = q * gcp
        k = k / (gcp + 1e-08)
        p = (xn @ p_w + p_b).reshape(Bx, Tx, H, Dh)
        p_max = jnp.max(p, axis=1, keepdims=True)
        p_exp = jnp.exp(p - p_max) * clock
        p_cs = jnp.cumsum(p_exp, axis=1)
        q = q / (p_cs + 1e-08)
        k = k * p_exp
        scores = jnp.einsum('bqhd,bkhd->bhqk', q, k) / math.sqrt(Dh)
        mask = jnp.tril(jnp.ones((Tx, Tx), dtype=bool))
        scores = jnp.where(mask[None, None], scores, -jnp.inf)
        attn = jax.nn.softmax(scores, axis=-1)
        out = jnp.einsum('bhqk,bkhd->bqhd', attn, v).reshape(Bx, Tx, D)
        out = out @ out_w + out_b
        x1 = out + residual
        h = _layernorm(x1, ln2_g, ln2_b)
        h = jax.nn.gelu(h @ mlp_w1 + mlp_b1, approximate=False) @ mlp_w2 + mlp_b2
        return x1 + h

    def _L0_ffn_ref(input_features, centroids, ln_g, ln_b, w1, b1, w2, b2):
        import jax, jax.numpy as jnp
        import numpy as np
        B, S, D, F, E = (8, 128, 128, 512, 8)
        EPS = 1e-05
        x = input_features.reshape(-1, D)
        aff = jax.lax.stop_gradient(x @ centroids.T)
        eid = jnp.argmax(aff, axis=-1)
        alpha = jax.nn.sigmoid(jnp.sum(x * centroids[eid], axis=-1, keepdims=True))
        mu = jnp.mean(x, axis=-1, keepdims=True)
        var = jnp.mean((x - mu) ** 2, axis=-1, keepdims=True)
        xn = (x - mu) * jax.lax.rsqrt(var + EPS)
        xln = xn * ln_g[eid] + ln_b[eid]
        onehot = jax.nn.one_hot(eid, E, dtype=x.dtype)
        ffn = jnp.zeros_like(x)
        for e in range(E):
            h = jax.nn.relu(xln @ w1[e] + b1[e])
            ffn = ffn + onehot[:, e:e + 1] * (h @ w2[e] + b2[e])
        out = x + alpha * ffn
        return out.reshape(input_features.shape)

    def _L1_attn_ref(x, W_in, conv_w, conv_b, W_x, W_dt, b_dt, A_log, D, W_out):
        import jax, jax.numpy as jnp
        import numpy as np
        BATCH, L, D_MODEL = (2, 128, 128)
        D_STATE, D_CONV, EXPAND = (16, 4, 2)
        D_INNER = EXPAND * D_MODEL
        DT_RANK = max(1, -(-D_MODEL // 16))

        def _forward(x, W_in, conv_w, conv_b, W_x, W_dt, b_dt, A_log, D, W_out):
            xv = x @ W_in
            xc = jnp.transpose(xv, (0, 2, 1))
            xc = jax.lax.conv_general_dilated(xc, conv_w, window_strides=(1,), padding=[(D_CONV - 1, 0)], dimension_numbers=('NCH', 'OIH', 'NCH'), feature_group_count=D_INNER)
            xv = jnp.transpose(xc, (0, 2, 1)) + conv_b
            xv = jax.nn.silu(xv)
            ssm = xv @ W_x
            dt_raw = ssm[..., :DT_RANK]
            Bp = ssm[..., DT_RANK:DT_RANK + D_STATE]
            Cp = ssm[..., DT_RANK + D_STATE:]
            delta = jax.nn.softplus(dt_raw @ W_dt + b_dt)
            A = -jnp.exp(A_log)
            dA = jnp.exp(delta[..., None] * A)
            dBx = delta[..., None] * Bp[:, :, None, :] * xv[..., None]

            def comb(c1, c2):
                a1, b1 = c1
                a2, b2 = c2
                return (a1 * a2, a2 * b1 + b2)
            _, h = jax.lax.associative_scan(comb, (dA, dBx), axis=1)
            y = jnp.einsum('bldn,bln->bld', h, Cp)
            y = y + xv * D
            return y @ W_out
        return _forward(x, W_in, conv_w, conv_b, W_x, W_dt, b_dt, A_log, D, W_out)

    def _L1_ffn_ref(x, cn_w1, cn_b1, cn_w2, cn_b2, cn_w3, cn_b3, cn_w4, cn_b4, gc_w1, gc_b1, gc_w2, gc_b2, gc_w3, gc_b3, adaptive_range):
        import jax, jax.numpy as jnp
        import numpy as np
        B, S, DIM = (4, 512, 128)
        BASE_COUPLING = 0.1
        NUM_CYCLES = 3

        def _gelu(x):
            return jax.nn.gelu(x, approximate=False)

        def _coupling_net(h, w1, b1, w2, b2, w3, b3, w4, b4):
            h = _gelu(h @ w1 + b1)
            h = _gelu(h @ w2 + b2)
            h = _gelu(h @ w3 + b3)
            return jax.nn.sigmoid(h @ w4 + b4)

        def _global_net(h, w1, b1, w2, b2, w3, b3):
            h = _gelu(h @ w1 + b1)
            h = _gelu(h @ w2 + b2)
            return jax.nn.sigmoid(h @ w3 + b3)

        def _twist(x):
            o_r, o_i, p_r, p_i = jnp.split(x, 4, axis=-1)
            return jnp.concatenate([p_r, -p_i, -o_r, o_i], axis=-1)
        global_context = x.mean(axis=1, keepdims=True)
        gf = _global_net(global_context, gc_w1, gc_b1, gc_w2, gc_b2, gc_w3, gc_b3)
        out = x
        for _ in range(NUM_CYCLES):
            tf = _coupling_net(out, cn_w1, cn_b1, cn_w2, cn_b2, cn_w3, cn_b3, cn_w4, cn_b4)
            combined = 0.7 * gf + 0.3 * tf
            coupling = BASE_COUPLING + adaptive_range * (combined - 0.5) * 2.0
            out = out + coupling * _twist(out)
        return out
    x = L0_attn_x
    x = x + _layernorm(_L0_attn_ref(_layernorm(x, axis=-1), L0_attn_Wq, L0_attn_Wk, L0_attn_Wv, L0_attn_gate_w, L0_attn_gate_b, L0_attn_p_w, L0_attn_p_b, L0_attn_out_w, L0_attn_out_b, L0_attn_clock_w, L0_attn_clock_b, L0_attn_ln1_g, L0_attn_ln1_b, L0_attn_ln2_g, L0_attn_ln2_b, L0_attn_mlp_w1, L0_attn_mlp_b1, L0_attn_mlp_w2, L0_attn_mlp_b2), axis=-1)
    x = x + _layernorm(_L0_ffn_ref(_layernorm(x, axis=-1), L0_ffn_centroids, L0_ffn_ln_g, L0_ffn_ln_b, L0_ffn_w1, L0_ffn_b1, L0_ffn_w2, L0_ffn_b2), axis=-1)
    x = x + _layernorm(_L1_attn_ref(_layernorm(x, axis=-1), L1_attn_W_in, L1_attn_conv_w, L1_attn_conv_b, L1_attn_W_x, L1_attn_W_dt, L1_attn_b_dt, L1_attn_A_log, L1_attn_D, L1_attn_W_out), axis=-1)
    x = x + _layernorm(_L1_ffn_ref(_layernorm(x, axis=-1), L1_ffn_cn_w1, L1_ffn_cn_b1, L1_ffn_cn_w2, L1_ffn_cn_b2, L1_ffn_cn_w3, L1_ffn_cn_b3, L1_ffn_cn_w4, L1_ffn_cn_b4, L1_ffn_gc_w1, L1_ffn_gc_b1, L1_ffn_gc_w2, L1_ffn_gc_b2, L1_ffn_gc_w3, L1_ffn_gc_b3, L1_ffn_adaptive_range), axis=-1)
    return x

_drawn_inputs = setup_inputs


def setup_inputs(seed=0):
    import zlib

    import numpy as np

    out = dict(_drawn_inputs(seed))
    spreads = {'L0_attn_gate_b': (0.0, 2.0),
     'L0_attn_p_b': (0.0, 2.0),
     'L0_attn_out_b': (0.0, 0.1),
     'L0_attn_clock_b': (0.0, 2.0),
     'L0_attn_ln1_g': (1.0, 0.6),
     'L0_attn_ln1_b': (0.0, 0.8),
     'L0_attn_ln2_g': (1.0, 0.6),
     'L0_attn_ln2_b': (0.0, 2.0),
     'L0_attn_mlp_b1': (0.0, 0.704),
     'L0_attn_mlp_b2': (0.0, 0.286),
     'L0_ffn_ln_g': (1.0, 0.6),
     'L0_ffn_ln_b': (0.0, 0.8),
     'L0_ffn_b1': (0.0, 0.8),
     'L0_ffn_b2': (0.0, 0.306),
     'L1_attn_D': (1.0, 0.2),
     'L1_ffn_cn_b1': (0.0, 2.0),
     'L1_ffn_cn_b2': (0.0, 2.0),
     'L1_ffn_cn_b3': (0.0, 2.0),
     'L1_ffn_gc_b1': (0.0, 2.0),
     'L1_ffn_gc_b2': (0.0, 2.0)}
    factors = {'L0_attn_Wq': 200.0,
     'L0_attn_Wk': 200.0,
     'L0_attn_Wv': 8.0,
     'L0_attn_gate_w': 200.0,
     'L0_attn_p_w': 200.0,
     'L0_attn_out_w': 8.0,
     'L0_attn_clock_w': 200.0,
     'L0_ffn_w1': 3.291,
     'L1_attn_W_x': 64.0,
     'L1_attn_W_dt': 171.497,
     'L1_attn_b_dt': 64.0,
     'L1_attn_A_log': 200.0,
     'L1_ffn_cn_w1': 8.0,
     'L1_ffn_cn_w2': 8.0,
     'L1_ffn_cn_w3': 8.0,
     'L1_ffn_cn_w4': 8.0,
     'L1_ffn_gc_w1': 8.0,
     'L1_ffn_gc_w2': 8.0,
     'L1_ffn_gc_w3': 8.0}
    for name, (base, spread) in spreads.items():
        noise = np.random.default_rng([zlib.crc32(name.encode()), seed]).standard_normal(out[name].shape)
        drawn = base * np.exp(spread * noise) if base else spread * noise
        out[name] = jnp.asarray(drawn.astype(out[name].dtype))
    for name, factor in factors.items():
        out[name] = (out[name] * factor).astype(out[name].dtype)
    return out
```

```python
from contextlib import ExitStack, contextmanager

import numpy as np

import concourse.bass as bass
from concourse import mybir

fp32 = mybir.dt.float32
bf16 = mybir.dt.bfloat16
i32 = mybir.dt.int32
ALU = mybir.AluOpType
ACT = mybir.ActivationFunctionType
AX = mybir.AxisListType

P = 128
SEQS, T, D = 32, 256, 128
N = SEQS * T
TILES = N // P
STEP = 2 * T
PAIRS = SEQS // 2
TS = STEP // P
H, DH = 16, 8
HS = 4
F = 512
FC = F // P
E = 8
ETILES = TILES + E
DI, NS, DR, TAPS = 256, 16, 8, 4
DHV = DI // P
CYCLES = 3
EPS = 1e-5
LN2 = float(np.log(2.0))
QK_SHIFT = 20
EXP_LN = "natural_log_exp_and_others"
BIG = 1e30


@contextmanager
def cleared(nc, block, names):
    sems = {n: nc.alloc_semaphore(name=f"{block}_{n}") for n in names.split()}
    yield sems
    nc.clear_and_free_semaphores(list(sems.values()))
    nc.all_engine_barrier()


def semaphores(nc, ctx, block, names):
    return ctx.enter_context(cleared(nc, block, names))


def program(nc, dram, out):
    ctx = ExitStack()
    with ctx:
        def scratch(name, rows, cols):
            return nc.dram_tensor(name, [rows, cols], fp32, kind="Internal").ap()

        d = dict(
            xlb=scratch("xlb_dram", N, D),
            y1=scratch("y1_dram", N, D),
            xl2=scratch("xl2_dram", N, D),
            xn2=scratch("xn2_dram", N, D),
            sorted_in=scratch("sorted_in_dram", ETILES * P, D),
            sorted_out=scratch("sorted_out_dram", ETILES * P, D),
            y2=scratch("y2_dram", N, D),
        )

        def keep(name, shape, dtype=fp32):
            return ctx.enter_context(nc.sbuf_tensor(name, shape, dtype))

        c = dict(
            vec=keep("vec", [P, dram["vec"].shape[1]]),
            rows=keep("rows", [P, 2, P]),
            cent=keep("cent", [P, E]),
            w_c=keep("w_c", [P, dram["w_c"].shape[1]]),
            w_dt=keep("w_dt", [DR, DI]),
            w_conv=keep("w_conv", [P, TAPS, DI]),
            neg_a=keep("neg_a", [P, DHV, NS]),
            consts=keep("consts", [P, dram["consts"].shape[1]]),
            ident_b=keep("ident_b", [P, P], bf16),
            mask_b=keep("mask_b", [P, 2, P], bf16),
            sel=keep("sel", [96, 32, P], bf16),
            b1_split=keep("b1_split", [96, F], bf16),
            b2_split=keep("b2_split", [96, D], bf16),
            aff=keep("aff", [P, TILES, E]),
            alpha=keep("alpha", [P, TILES]),
            slot=keep("slot", [P, TILES], i32),
            tile_col=keep("tile_col", [1, 2, ETILES], i32),
        )
        layer0 = ctx.enter_context(ExitStack())
        for name, shape in (("w_a", [P, dram["w_a"].shape[1]]), ("w_1", [P, E * F]), ("w_2", [P, E * F])):
            c[name] = layer0.enter_context(nc.sbuf_tensor(name, shape, fp32))
        at = 0
        for name, width in CONSTS:
            c[name] = c["consts"][:, at:at + width]
            at += width
        at = 0
        for name, width in VECS:
            c[name] = c["vec"][:, at:at + width]
            at += width
        at = 0
        for name, width in W_A:
            c[name] = c["w_a"][:, at:at + width]
            at += width
        at = 0
        for name, width in W_C:
            c[name] = c["w_c"][:, at:at + width]
            at += width
        banks = [ctx.enter_context(nc.psum_tensor(f"bank{n}", [P, 512], fp32)) for n in range(8)]

        setup(nc, dram, d, c, banks)
        attention(nc, dram, d, c, banks)
        routing(nc, dram, d, c, banks)
        experts(nc, d, c, banks)
        layer0.close()
        scan_layer(nc, d, c, banks, out)


def split3(dve, chain, src, dst, hi, rest, mid, rows):
    chain(dve.tensor_copy(hi, src))
    chain(dve.tensor_tensor(rest, src, hi, ALU.subtract))
    chain(dve.tensor_copy(mid, rest))
    chain(dve.tensor_copy(dst[0:rows], hi))
    chain(dve.tensor_copy(dst[32:32 + rows], mid))
    chain(dve.tensor_tensor(rest, rest, mid, ALU.subtract))
    chain(dve.tensor_copy(dst[64:64 + rows], rest))


def setup(nc, dram, d, c, banks):
    with ExitStack() as ctx:
        s = semaphores(nc, ctx, "setup", "su_small su_cent su_expert su_scan su_zeroed su_zero su_bias_ps su_dve su_pool su_act")
        tmp = lambda name, shape, dtype=fp32: ctx.enter_context(nc.sbuf_tensor(name, shape, dtype))
        e_vec = tmp("e_vec", [P, 2 * E])
        lnb_eye = tmp("lnb_eye", [P, E, E])
        b_1 = tmp("b_1", [E, F])
        b_2 = tmp("b_2", [E, D])
        conv_rows = tmp("conv_rows", [P, TAPS, DI])
        hi = tmp("su_hi", [E, F], bf16)
        mid = tmp("su_mid", [E, F], bf16)
        rest = tmp("su_rest", [E, F])
        zeros = tmp("su_zeros", [P, 1024])
        block = ctx.enter_context(nc.Block())

        @block.sync
        def _(sp):
            sp.dma_start(c["consts"][:, :], dram["consts"]).then_inc(s["su_small"], 16)
            sp.dma_start(c["vec"][:, :], dram["vec"]).then_inc(s["su_small"], 16)
            sp.dma_start(c["rows"][:, :, :], dram["rows"]).then_inc(s["su_small"], 16)
            sp.dma_start(e_vec[:, :], dram["e_vec"]).then_inc(s["su_expert"], 16)
            sp.dma_start(b_1[:, :], dram["b_1"]).then_inc(s["su_expert"], 16)
            sp.dma_start(b_2[:, :], dram["b_2"]).then_inc(s["su_expert"], 16)
            sp.dma_start(c["w_1"][:, :], dram["w_1"]).then_inc(s["su_expert"], 16)
            sp.dma_start(c["neg_a"][:, :, :], dram["a_log"]).then_inc(s["su_scan"], 16)
            sp.dma_start(conv_rows[:, :, :], dram["conv_w"]).then_inc(s["su_scan"], 16)
            sp.dma_start(c["w_c"][:, :], dram["w_c"]).then_inc(s["su_scan"], 16)
            sp.dma_start(c["w_a"][:, :], dram["w_a"]).then_inc(s["su_small"], 16)
            sp.dma_start(c["cent"][:, :], dram["cent"]).then_inc(s["su_cent"], 16)
            sp.dma_start(c["w_2"][:, :], dram["w_2"]).then_inc(s["su_cent"], 16)
            sp.dma_start(c["w_dt"][:, :], dram["w_dt"]).then_inc(s["su_cent"], 16)
            sp.wait_ge(s["su_zero"], 1)
            rows = d["sorted_in"].rearrange("(n p q) d -> n p (q d)", p=P, q=8)
            for n in range(ETILES // 8):
                sp.dma_start(rows[n], zeros[:, :]).then_inc(s["su_zeroed"], 16)
            sp.wait_ge(s["su_small"], 64)
            sp.wait_ge(s["su_cent"], 48)
            sp.wait_ge(s["su_zeroed"], 16 * (ETILES // 8))

        @block.gpsimd
        def _(pool):
            pool.memset(zeros[:, :], 0.0).then_inc(s["su_zero"], 1)
            pool.wait_ge(s["su_scan"], 48)
            for tap in range(TAPS):
                pool.tensor_tensor(c["w_conv"][:, tap, :], conv_rows[:, tap, :], c["w_in"], ALU.mult).then_inc(s["su_pool"], 1)
            pool.wait_ge(s["su_pool"], TAPS)

        @block.scalar
        def _(act):
            act.wait_ge(s["su_dve"], 1)
            act.activation(c["neg_a"][:, :, :], c["neg_a"][:, :, :], ACT.Exp).then_inc(s["su_act"], 1)

        @block.tensor
        def _(pe):
            pe.wait_ge(s["su_dve"], 2)
            for e in range(E):
                last = pe.matmul(banks[0][0:E, :], lnb_eye[:, e, :], c["w_1"][:, e * F:(e + 1) * F],
                                 start=e == 0, stop=e == E - 1)
            last.then_inc(s["su_bias_ps"], 1)

        @block.vector
        def _(dve):
            count = [0]

            def chain(ins):
                count[0] += 1
                ins.then_inc(s["su_dve"], 1)
                dve.wait_ge(s["su_dve"], count[0])

            dve.wait_ge(s["su_scan"], 48)
            chain(dve.tensor_scalar(c["neg_a"][:, :, :], c["neg_a"][:, :, :], 69.0, None, ALU.min))
            dve.wait_ge(s["su_small"], 64)
            dve.wait_ge(s["su_expert"], 64)
            chain(dve.tensor_tensor(lnb_eye[:, :, :], e_vec[:, E:2 * E].unsqueeze(2).to_broadcast([P, E, E]),
                                    c["eye8"].rearrange("p (a b) -> p a b", a=E), ALU.mult))
            dve.wait_ge(s["su_act"], 1)
            chain(dve.tensor_scalar(c["neg_a"][:, :, :], c["neg_a"][:, :, :], -1.0, None, ALU.mult))
            chain(dve.tensor_copy(c["ident_b"][:, :], c["ident"]))
            chain(dve.tensor_copy(c["mask_b"][:, :, :], c["mask"].unsqueeze(1).to_broadcast([P, 2, P])))
            chain(dve.tensor_copy(c["sel"][:, :, :], c["sel_cols"][0:96, :].unsqueeze(2).to_broadcast([96, 32, P])))
            chain(dve.memset(c["b1_split"][:, :], 0.0))
            chain(dve.memset(c["b2_split"][:, :], 0.0))
            dve.wait_ge(s["su_bias_ps"], 1)
            chain(dve.tensor_tensor(b_1[:, :], banks[0][0:E, :], b_1[:, :], ALU.add))
            split3(dve, chain, b_1[:, :], c["b1_split"], hi[:, :], rest[:, :], mid[:, :], E)
            split3(dve, chain, b_2[:, :], c["b2_split"], hi[:, 0:D], rest[:, 0:D], mid[:, 0:D], E)
            for e in range(E):
                chain(dve.tensor_scalar(c["w_1"][:, e * F:(e + 1) * F], c["w_1"][:, e * F:(e + 1) * F],
                                        e_vec[:, e:e + 1], None, ALU.mult))




def attention(nc, dram, d, c, banks):
    with ExitStack() as ctx:
        s = semaphores(nc, ctx, "attn", """
            end_pe end_act end_dve end_pool
            x_loaded0 x_loaded1 xlb_loaded xm_loaded xlb_stored y_stored
            f_st f_mv f_vv f_ln f_rs f_xn f_xl f_xl2 f_xlb f_xt f_xt_sb f_gate f_clock f_pre0 f_pre1 f_abs f_exp f_log
            f_p f_max f_shift f_nb f_pe f_sp f_cum f_clip f_gcp f_lgcp f_px f_pcs f_lpcs
            f_q f_qs f_sq f_ra f_rb f_rq f_ssq f_mq f_lq f_zq f_zq2 f_fq f_qt
            f_k f_ks f_sk f_ka f_kb f_rk f_ssk f_mk f_lk f_zk f_fk f_k1 f_k2 f_km f_v f_vaug
            s_score s_exp s_av s_avs s_tr s_rec s_o
            m_ot m_ot_sb m_ow m_x1 m_x1b m_st m_mv m_ln m_rs m_h m_ht m_ht_sb m_up m_gelu m_dn
            m_x2 m_st2 m_mv2 m_ln2 m_rs2 m_yn m_y1 m_st3 m_mv3 m_vv3 m_ln3 m_rs3 m_xl2 m_xn2a m_xn2
            m_x2t m_x2t_sb m_aff m_aff_sb""")
        sb = lambda name, shape, dtype=fp32: ctx.enter_context(nc.sbuf_tensor(name, shape, dtype))
        x_in = [sb(f"x_in{n}", [P, TS, D]) for n in range(2)]
        stats = sb("f_stats", [P, TS, 6])
        mv = sb("f_mean_var", [P, TS, 2])
        vv = sb("f_vv", [P, 2, TS])
        rs = sb("f_rstd", [P, 2, TS])
        xn = sb("xn", [P, TS, D])
        xl = sb("xl", [P, TS, D])
        xt = sb("xt", [P, STEP])
        pre = sb("pre", [P, 2, STEP])
        mag = sb("mag", [P, 2, STEP])
        cum = sb("cum", [P, STEP])
        lgcp = sb("lgcp", [P, STEP])
        pmax = sb("pmax", [P, 2])
        pneg = sb("pneg", [P, 2])
        pexp = sb("pexp", [P, STEP])
        pcs = sb("pcs", [P, STEP])
        square = sb("square", [P, STEP])
        lnorm = sb("lnorm", [P, STEP])
        rot = sb("rot", [P, STEP])
        rot_b = sb("rot_b", [P, STEP])
        factor = sb("factor", [P, STEP])
        q_t = [sb(f"q_t{n}", [P, STEP]) for n in range(2)]
        k_m = [sb(f"k_m{n}", [P, HS, STEP]) for n in range(2)]
        v_a = [sb(f"v_a{n}", [P, TS, H, 32]) for n in range(2)]
        es = [sb(f"es{n}", [P, 3 * P]) for n in range(8)]
        avs = sb("avs", [P, 512])
        rec = sb("rec", [P, 4, HS])
        o_tok = [sb(f"o_tok{n}", [P, TS, D]) for n in range(2)]
        x_m = sb("x_m", [P, TS, D])
        xlb_m = sb("xlb_m", [P, TS, D])
        o_t = sb("o_t", [P, STEP])
        x1 = sb("x1", [P, TS, D])
        x1b = sb("x1b", [P, TS, D])
        stats_m = sb("m_stats", [P, TS, 6])
        mv_m = sb("m_mean_var", [P, TS, 2])
        ln_m = sb("m_ln", [P, TS])
        rs_m = sb("m_rstd", [P, TS])
        vv_m = sb("m_vv", [P, 2, TS])
        rs3 = sb("m_rstd3", [P, 2, TS])
        h_tok = sb("h_tok", [P, TS, D])
        h_t = sb("h_t", [P, STEP])
        g = sb("g", [P, FC, STEP])
        x2 = sb("x2", [P, TS, D])
        y1 = sb("y1", [P, TS, D])
        xl2 = sb("xl2", [P, TS, D])
        xn2 = sb("xn2", [P, TS, D])
        hold = sb("a_hold", [P, 1])

        FA, FB, M, RING, AV = banks[0], banks[1], banks[2], banks[3:7], banks[7]
        x_loaded = [s["x_loaded0"], s["x_loaded1"]]
        seq = lambda t: t.rearrange("p (b t) -> p b t", b=2)
        tok = lambda t: t.rearrange("p (j d) -> p j d", j=TS)
        of_tile = lambda a: a.unsqueeze(2).to_broadcast([P, TS, D])
        cos = c["cos"].unsqueeze(1).to_broadcast([P, 2, T])
        sin = c["sin"].unsqueeze(1).to_broadcast([P, 2, T])
        rows = lambda ap, at: ap[bass.ds(at, STEP), :].rearrange("(j p) d -> p j d", p=P)
        w_down = c["w_down"].rearrange("p (c d) -> p c d", c=FC)

        def begin(eng, k):
            if isinstance(k, int) and k == 0:
                return
            for sem in (s["end_pe"], s["end_act"], s["end_dve"], s["end_pool"]):
                eng.wait_ge(sem, k)

        def stats_of(dve, src, st, out_mv, s_st, s_mv, r):
            for j in range(TS):
                last = dve.bn_stats(st[:, j, :], src[:, j, :])
            last.then_inc(s_st, 1)
            dve.wait_ge(s_st, r)
            dve.memset(hold[:, :], 0.0)
            for j in range(TS):
                last = dve.bn_aggr(out_mv[:, j, :], st[:, j, :])
            last.then_inc(s_mv, 1)
            dve.wait_ge(s_mv, r)

        def two_variances(dve, v, var, sem):
            dve.tensor_scalar(v[:, 0, :], var, EPS, None, ALU.add)
            dve.tensor_scalar(v[:, 1, :], var, 1.0 + EPS, EPS * EPS, ALU.mult, ALU.add).then_inc(sem, 1)

        x_loaded = [s["x_loaded0"], s["x_loaded1"]]

        def sp_step(sp, k, p, front, tail, load):
            now, rf, rm = (sp.snap(v) for v in (k * 1, k + 1, k - 1))
            here, back_two, ahead = (sp.snap(v) for v in (k * STEP, k * STEP - 2 * STEP, k * STEP + STEP))
            if load:
                sp.wait_ge(s["end_dve"], now)
                sp.wait_ge(s["end_pool"], now)
                sp.dma_start(x_in[1 - p][:, :, :], rows(dram["x"], ahead)).then_inc(x_loaded[1 - p], 16)
            if tail:
                sp.wait_ge(s["end_dve"], now)
                sp.wait_ge(s["end_pool"], now)
                sp.dma_start(xlb_m[:, :, :], rows(d["xlb"], back_two)).then_inc(s["xlb_loaded"], 16)
                sp.dma_start(x_m[:, :, :], rows(dram["x"], back_two)).then_inc(s["xm_loaded"], 16)
            if front:
                sp.wait_ge(s["f_xlb"], rf)
                sp.dma_start(rows(d["xlb"], here), xl[:, :, :]).then_inc(s["xlb_stored"], 16)
            if tail:
                sp.wait_ge(s["m_y1"], rm)
                sp.dma_start(rows(d["y1"], back_two), y1[:, :, :]).then_inc(s["y_stored"], 16)
                sp.wait_ge(s["m_xl2"], rm)
                sp.dma_start(rows(d["xl2"], back_two), xl2[:, :, :]).then_inc(s["y_stored"], 16)
                sp.wait_ge(s["m_xn2"], rm)
                sp.dma_start(rows(d["xn2"], back_two), xn2[:, :, :]).then_inc(s["y_stored"], 16)

        def pe_step(pe, k, half, p, front, scores, tail):
            begin(pe, k)
            rf, u, m = k + 1, k - 1, k - 2
            rm = k - 1

            def project(bank, weight, sem):
                pe.matmul(bank[:, :], weight, xt[:, :], start=True, stop=True).then_inc(sem, 1)

            def transposes(dst, src, sem):
                for j in range(TS):
                    last = pe.transpose(dst[:, j * P:(j + 1) * P], src[:, j, :], c["ident"])
                last.then_inc(sem, 1)

            def quad(n):
                b, v = n // HS, n % HS
                if n:
                    pe.wait_ge(s["s_exp"], u * 8 + n)
                for st in range(HS):
                    q, kk = q_t[1 - p][32 * st:32 * st + 32, b * T:b * T + T], k_m[1 - p][32 * st:32 * st + 32, v, b * T:b * T + T]
                    pe.matmul(RING[st][:, 0:T], kk[:, 0:P], q, start=True, stop=True, tile_position=(32 * st, 0))
                for st in range(HS):
                    q, kk = q_t[1 - p][32 * st:32 * st + 32, b * T:b * T + T], k_m[1 - p][32 * st:32 * st + 32, v, b * T:b * T + T]
                    pe.matmul(RING[st][:, T:T + P], kk[:, P:T], q[:, P:T], start=False, stop=True,
                              tile_position=(32 * st, 0), skip_group_check=True)
                for st in range(HS):
                    diag = RING[st][:, 0:4 * P].rearrange("p (a b) -> p a b", a=2)[:, :, 0:P]
                    pe.matmul(diag, c["ident_b"][:, :], c["mask_b"][:, :, :], start=False, stop=True,
                              skip_group_check=True).then_inc(s["s_score"], 1)

            def weigh(n):
                b, v, i = n // HS, n % HS, n // 2
                pe.wait_ge(s["s_exp"], u * 8 + n + 1)
                if n % 2 == 0 and i:
                    pe.wait_ge(s["s_o"], u * 8 + 2 * i)
                col = (v % 2) * T
                for st in range(HS):
                    e, dst = es[(n % 2) * HS + st], AV[32 * st:32 * st + 32, :]
                    pe.matmul(dst[:, col:col + T], v_a[1 - p][:, 2 * b, HS * st + v, :], e[:, 0:T],
                              start=True, stop=True, tile_position=(0, 32 * st))
                for st in range(HS):
                    e, dst = es[(n % 2) * HS + st], AV[32 * st:32 * st + 32, :]
                    last = pe.matmul(dst[:, col + P:col + T], v_a[1 - p][:, 2 * b + 1, HS * st + v, :], e[:, T:T + P],
                                     start=False, stop=True, tile_position=(0, 32 * st), skip_group_check=True)
                last.then_inc(s["s_av"], 1)

            def back(i):
                pe.wait_ge(s["s_avs"], u * 4 + i + 1)
                for j in range(4):
                    last = pe.transpose(AV[:, j * P:(j + 1) * P], avs[:, j * P:(j + 1) * P], c["ident"])
                last.then_inc(s["s_tr"], 1)

            def up(n):
                if n == 0:
                    pe.wait_ge(s["m_ht_sb"], rm)
                else:
                    pe.wait_ge(s["m_gelu"], 4 * m + n)
                pe.matmul(M[:, :], c["w_up"][:, n * P:(n + 1) * P], h_t[:, :], start=True, stop=True).then_inc(s["m_up"], 1)

            if tail:
                transposes(M, o_tok[p], s["m_ot"])
            if scores:
                quad(0)
            if front:
                pe.wait_ge(s["f_xn"], rf)
                transposes(FA, xn, s["f_xt"])
            if tail:
                pe.wait_ge(s["m_ot_sb"], rm)
                for j in range(TS):
                    last = pe.matmul(M[:, j * P:(j + 1) * P], o_t[:, j * P:(j + 1) * P], c["w_o"], start=True, stop=True)
                last.then_inc(s["m_ow"], 1)
            if front:
                pe.wait_ge(s["f_xt_sb"], rf)
                project(FB, c["w_gate"], s["f_gate"])
                project(FA, c["w_clock"], s["f_clock"])
            if scores:
                quad(1)
                weigh(0)
            if front:
                pe.wait_ge(s["f_pre0"], rf)
                project(FB, c["w_p"], s["f_p"])
            if tail:
                pe.wait_ge(s["m_h"], rm)
                transposes(M, h_tok, s["m_ht"])
            if scores:
                quad(2)
                weigh(1)
            if front:
                pe.wait_ge(s["f_pre1"], rf)
                project(FA, c["w_q"], s["f_q"])
            if tail:
                up(0)
                up(1)
            if front:
                pe.wait_ge(s["f_pe"], rf)
                project(FB, c["w_qs"], s["f_qs"])
            if tail:
                up(2)
                up(3)
            if scores:
                back(0)
                quad(3)
                weigh(2)
            if tail:
                pe.wait_ge(s["m_gelu"], 4 * m + 4)
                for j in range(TS):
                    for n in range(FC):
                        last = pe.matmul(M[:, j * P:(j + 1) * P], g[:, n, j * P:(j + 1) * P], w_down[:, n, :],
                                         start=n == 0, stop=n == FC - 1)
                last.then_inc(s["m_dn"], 1)
            if front:
                pe.wait_ge(s["f_sq"], rf)
                pe.wait_ge(s["f_ra"], rf)
                pe.matmul(FA[:, :], c["ones_blk"], square[:, :], start=True, stop=True).then_inc(s["f_ssq"], 1)
            if scores:
                quad(4)
                weigh(3)
            if front:
                pe.wait_ge(s["f_rb"], rf)
                project(FB, c["w_k"], s["f_k"])
                pe.wait_ge(s["f_mq"], rf)
                project(FA, c["w_ks"], s["f_ks"])
            if scores:
                back(1)
                quad(5)
                weigh(4)
            if front:
                pe.wait_ge(s["f_ka"], rf)
                pe.wait_ge(s["f_sk"], rf)
                pe.matmul(FB[:, :], c["ones_blk"], square[:, :], start=True, stop=True).then_inc(s["f_ssk"], 1)
            if scores:
                quad(6)
                weigh(5)
            if front:
                pe.wait_ge(s["f_kb"], rf)
                for j in range(TS):
                    last = pe.matmul(FA[:, j * P:(j + 1) * P], xt[:, j * P:(j + 1) * P], c["w_v"], start=True, stop=True)
                last.then_inc(s["f_v"], 1)
            if scores:
                back(2)
                quad(7)
                weigh(6)
            if tail:
                pe.wait_ge(s["m_xl2"], rm)
                transposes(M, xl2, s["m_x2t"])
            if scores:
                weigh(7)
            if tail:
                pe.wait_ge(s["m_x2t_sb"], rm)
                for j in range(TS):
                    last = pe.matmul(M[:, j * E:(j + 1) * E], o_t[:, j * P:(j + 1) * P], c["cent"][:, :], start=True, stop=True)
                last.then_inc(s["m_aff"], 1)
            if scores:
                back(3)
            pe.drain().then_inc(s["end_pe"], 1)

        def act_step(act, k, half, p, front, scores, tail):
            act.preload_act_table_set(EXP_LN)
            begin(act, k)
            rf, u, m = k + 1, k - 1, k - 2
            rm = k - 1

            def root(src, ln, dst, wait, s_ln, s_rs, r, bias=0.0):
                act.wait_ge(wait, r)
                act.activation(ln, src, ACT.Ln, bias=bias).then_inc(s_ln, 1)
                act.wait_ge(s_ln, r)
                act.activation(dst, ln, ACT.Exp, scale=-0.5).then_inc(s_rs, 1)

            def exps(n):
                for st in range(HS):
                    act.wait_ge(s["s_score"], u * 32 + HS * n + st + 1)
                    if n >= 2 and st == 0:
                        act.wait_ge(s["s_av"], u * 8 + n - 1)
                    last = act.activation(es[(n % 2) * HS + st][:, :], RING[st][:, 0:3 * P], ACT.Exp, scale=DH ** -0.5)
                last.then_inc(s["s_exp"], 1)

            def av_copy(i):
                act.wait_ge(s["s_av"], u * 8 + 2 * i + 2)
                if i:
                    act.wait_ge(s["s_tr"], u * 4 + i)
                act.activation(avs[:, :], AV[:, :], ACT.Copy).then_inc(s["s_avs"], 1)

            def squared(bank, wait, sem):
                act.wait_ge(wait, rf)
                act.activation(square[:, :], bank[:, :], ACT.Square).then_inc(sem, 1)

            if tail:
                act.wait_ge(s["m_ot"], rm)
                act.activation(o_t[:, :], M[:, :], ACT.Copy).then_inc(s["m_ot_sb"], 1)
            if front:
                root(vv[:, :, :], vv[:, :, :], rs[:, :, :], s["f_vv"], s["f_ln"], s["f_rs"], rf)
            if scores:
                exps(0)
            if front:
                act.wait_ge(s["f_xt"], rf)
                act.activation(xt[:, :], FA[:, :], ACT.Identity, scale=c["ln1_g"], bias=c["ln1_b"]).then_inc(s["f_xt_sb"], 1)
            if tail:
                root(mv_m[:, :, 1], ln_m[:, :], rs_m[:, :], s["m_mv"], s["m_ln"], s["m_rs"], rm, bias=EPS)
            if scores:
                exps(1)
            if front:
                act.wait_ge(s["f_pre1"], rf)
                act.activation(mag[:, :, :], pre[:, :, :], ACT.Abs).then_inc(s["f_abs"], 1)
                act.wait_ge(s["f_abs"], rf)
                act.activation(mag[:, :, :], mag[:, :, :], ACT.Exp, scale=-1.0).then_inc(s["f_exp"], 1)
                act.wait_ge(s["f_exp"], rf)
                act.activation(mag[:, :, :], mag[:, :, :], ACT.Ln, bias=1.0).then_inc(s["f_log"], 1)
            if tail:
                act.wait_ge(s["m_ht"], rm)
                act.activation(h_t[:, :], M[:, :], ACT.Identity, scale=c["ln2_g"], bias=c["ln2_b"]).then_inc(s["m_ht_sb"], 1)
            if front:
                act.wait_ge(s["f_nb"], rf)
                for b in range(2):
                    last = act.activation(pexp[:, b * T:(b + 1) * T], FB[:, b * T:(b + 1) * T], ACT.Exp, bias=pneg[:, b:b + 1])
                last.then_inc(s["f_pe"], 1)
                squared(FA, s["f_q"], s["f_sq"])
            if tail:
                for n in range(FC):
                    act.wait_ge(s["m_up"], 4 * m + n + 1)
                    act.activation(g[:, n, :], M[:, :], ACT.Gelu, bias=c["mlp_b1"][:, n:n + 1]).then_inc(s["m_gelu"], 1)
                act.preload_act_table_set(EXP_LN)
            if scores:
                exps(2)
                av_copy(0)
            if front:
                act.wait_ge(s["f_clip"], rf)
                act.activation(lgcp[:, :], cum[:, :], ACT.Exp, scale=-1.0).then_inc(s["f_gcp"], 1)
                act.wait_ge(s["f_gcp"], rf)
                act.activation(lgcp[:, :], lgcp[:, :], ACT.Ln, bias=1e-8).then_inc(s["f_lgcp"], 1)
                act.wait_ge(s["f_pcs"], rf)
                act.activation(pcs[:, :], pcs[:, :], ACT.Ln, bias=1e-8).then_inc(s["f_lpcs"], 1)
            if scores:
                exps(3)
            if tail:
                root(mv_m[:, :, 1], ln_m[:, :], rs_m[:, :], s["m_mv2"], s["m_ln2"], s["m_rs2"], rm, bias=EPS)
            if front:
                act.wait_ge(s["f_mq"], rf)
                act.activation(lnorm[:, :], lnorm[:, :], ACT.Ln, scale=2.0 ** QK_SHIFT).then_inc(s["f_lq"], 1)
            if scores:
                exps(4)
                av_copy(1)
            if front:
                squared(FB, s["f_k"], s["f_sk"])
                act.wait_ge(s["f_zq2"], rf)
                act.activation(factor[:, :], factor[:, :], ACT.Exp, bias=0.5 * QK_SHIFT * LN2).then_inc(s["f_fq"], 1)
            if tail:
                root(vv_m[:, :, :], vv_m[:, :, :], rs3[:, :, :], s["m_vv3"], s["m_ln3"], s["m_rs3"], rm)
            if scores:
                exps(5)
            if front:
                act.wait_ge(s["f_mk"], rf)
                act.activation(lnorm[:, :], lnorm[:, :], ACT.Ln, scale=2.0 ** QK_SHIFT).then_inc(s["f_lk"], 1)
            if scores:
                exps(6)
                av_copy(2)
            if front:
                act.wait_ge(s["f_zk"], rf)
                act.activation(factor[:, :], factor[:, :], ACT.Exp, bias=0.5 * QK_SHIFT * LN2).then_inc(s["f_fk"], 1)
                act.wait_ge(s["f_v"], rf)
                act.activation(v_a[p][:, :, :, 0:DH], FA.rearrange("p (j h d) -> p j h d", j=TS, h=H), ACT.Copy).then_inc(s["f_vaug"], 1)
            if scores:
                exps(7)
            if tail:
                act.wait_ge(s["m_x2t"], rm)
                act.activation(o_t[:, :], M[:, :], ACT.Copy).then_inc(s["m_x2t_sb"], 1)
            if front:
                act.wait_ge(s["f_k2"], rf)
                for v in range(HS):
                    last = act.activation(k_m[p][:, v, :], rot[:, :], ACT.Copy, scale=c["head_mask"][:, v:v + 1])
                last.then_inc(s["f_km"], 1)
            if scores:
                av_copy(3)
            act.drain().then_inc(s["end_act"], 1)

        def dve_step(dve, k, half, p, front, scores, tail):
            begin(dve, k)
            rf, u, m = k + 1, k - 1, k - 2
            rm = k - 1

            def heads_out(i):
                b, vp = i // 2, i % 2
                tr = AV.rearrange("q (v r s w) -> q v r s w", v=2, r=2, s=HS)
                dve.wait_ge(s["s_tr"], u * 4 + i + 1)
                dve.reciprocal(rec[:, :, :], AV.rearrange("q (n s w) -> q n s w", n=4, s=HS)[:, :, :, DH]).then_inc(s["s_rec"], 1)
                dve.wait_ge(s["s_rec"], u * 4 + i + 1)
                for r in range(2):
                    o = o_tok[1 - p][:, 2 * b + r, :].rearrange("q (s v w) -> q v s w", s=HS, v=HS)[:, 2 * vp:2 * vp + 2, :, :]
                    w = rec.rearrange("q (v r) s -> q v r s", v=2)[:, :, r, :].unsqueeze(3).to_broadcast([P, 2, HS, DH])
                    dve.tensor_tensor(o, tr[:, :, r, :, 0:DH], w, ALU.mult).then_inc(s["s_o"], 1)

            def rotate(bank, bank_sw, s_a, wait_a, s_b, wait_b, s_r):
                dve.wait_ge(wait_a, rf)
                dve.tensor_tensor(seq(rot), seq(bank), cos, ALU.mult).then_inc(s_a, 1)
                dve.wait_ge(wait_b, rf)
                dve.tensor_tensor(seq(rot_b), seq(bank_sw), sin, ALU.mult).then_inc(s_b, 1)
                dve.wait_ge(s_b, rf)
                dve.tensor_tensor(rot[:, :], rot[:, :], rot_b[:, :], ALU.add).then_inc(s_r, 1)

            def centred(dst, src, mean_var, rstd, sem):
                for j in range(TS):
                    last = dve.tensor_scalar(dst[:, j, :], src[:, j, :], mean_var[:, j, 0:1], rstd[:, j:j + 1], ALU.subtract, ALU.mult)
                last.then_inc(sem, 1)

            if front:
                dve.wait_ge(x_loaded[p], 16 * half + 16)
                stats_of(dve, x_in[p], stats, mv, s["f_st"], s["f_mv"], rf)
                two_variances(dve, vv, mv[:, :, 1], s["f_vv"])
                dve.wait_ge(s["f_rs"], rf)
                centred(xn, x_in[p], mv, rs[:, 1, :], s["f_xn"])
            if tail:
                dve.wait_ge(s["xlb_loaded"], 16 * rm)
                dve.wait_ge(s["m_ow"], rm)
                dve.tensor_tensor(x1[:, :, :], tok(M), xlb_m[:, :, :], ALU.add).then_inc(s["m_x1"], 1)
                dve.wait_ge(s["m_x1"], rm)
                stats_of(dve, x1, stats_m, mv_m, s["m_st"], s["m_mv"], rm)
            if tail:
                dve.wait_ge(s["m_rs"], rm)
                centred(h_tok, x1, mv_m, rs_m, s["m_h"])
            if front:
                dve.wait_ge(s["f_gate"], rf)
                dve.tensor_scalar(pre[:, 0, :], FB[:, :], c["gate_b"], None, ALU.add).then_inc(s["f_pre0"], 1)
                dve.wait_ge(s["f_clock"], rf)
                dve.tensor_scalar(pre[:, 1, :], FA[:, :], c["clock_b"], None, ALU.add).then_inc(s["f_pre1"], 1)
                dve.wait_ge(s["f_p"], rf)
                dve.tensor_reduce(pmax[:, :], seq(FB), AX.X, ALU.max).then_inc(s["f_max"], 1)
                dve.wait_ge(s["f_max"], rf)
                dve.tensor_scalar(pmax[:, :], pmax[:, :], c["p_b"], None, ALU.add).then_inc(s["f_shift"], 1)
                dve.wait_ge(s["f_shift"], rf)
                dve.tensor_scalar(pneg[:, :], pmax[:, :], -1.0, c["p_b"], ALU.mult, ALU.add).then_inc(s["f_nb"], 1)
                dve.wait_ge(s["f_log"], rf)
                dve.scalar_tensor_tensor(pre[:, :, :], pre[:, :, :], 0.0, mag[:, :, :], ALU.max, ALU.add).then_inc(s["f_sp"], 1)
                dve.wait_ge(s["f_sp"], rf)
                dve.tensor_tensor_scan(cum[:, :], c["reset"], pre[:, 0, :], 0.0, ALU.mult, ALU.add).then_inc(s["f_cum"], 1)
                dve.wait_ge(s["f_cum"], rf)
                dve.tensor_scalar(cum[:, :], cum[:, :], -50.0, 60.0, ALU.max, ALU.min).then_inc(s["f_clip"], 1)
                dve.wait_ge(s["f_pe"], rf)
                dve.tensor_tensor(pexp[:, :], pexp[:, :], pre[:, 1, :], ALU.mult).then_inc(s["f_px"], 1)
                dve.wait_ge(s["f_px"], rf)
                dve.tensor_tensor_scan(pcs[:, :], c["reset"], pexp[:, :], 0.0, ALU.mult, ALU.add).then_inc(s["f_pcs"], 1)
                rotate(FA, FB, s["f_ra"], s["f_sq"], s["f_rb"], s["f_qs"], s["f_rq"])
            if scores:
                heads_out(0)
            if tail:
                dve.wait_ge(s["m_x1b"], rm)
                dve.wait_ge(s["m_dn"], rm)
                dve.tensor_tensor(x2[:, :, :], tok(M), x1b[:, :, :], ALU.add).then_inc(s["m_x2"], 1)
                dve.wait_ge(s["m_x2"], rm)
                stats_of(dve, x2, stats_m, mv_m, s["m_st2"], s["m_mv2"], rm)
            if front:
                dve.wait_ge(s["f_ssq"], rf)
                dve.tensor_scalar(lnorm[:, :], FA[:, :], 1e-24, None, ALU.max).then_inc(s["f_mq"], 1)
            if tail:
                dve.wait_ge(s["m_rs2"], rm)
                centred(h_tok, x2, mv_m, rs_m, s["m_yn"])
                dve.wait_ge(s["m_yn"], rm)
                dve.wait_ge(s["xm_loaded"], 16 * rm)
                dve.wait_ge(s["y_stored"], 48 * m + 1)
                dve.tensor_tensor(y1[:, :, :], h_tok[:, :, :], x_m[:, :, :], ALU.add).then_inc(s["m_y1"], 1)
                dve.wait_ge(s["m_y1"], rm)
                stats_of(dve, y1, stats_m, mv_m, s["m_st3"], s["m_mv3"], rm)
                two_variances(dve, vv_m, mv_m[:, :, 1], s["m_vv3"])
            if scores:
                heads_out(1)
            if front:
                dve.wait_ge(s["f_lq"], rf)
                dve.scalar_tensor_tensor(factor[:, :], lnorm[:, :], -0.5, cum[:, :], ALU.mult, ALU.subtract).then_inc(s["f_zq"], 1)
                dve.wait_ge(s["f_lpcs"], rf)
                dve.wait_ge(s["f_zq"], rf)
                dve.tensor_tensor(factor[:, :], factor[:, :], pcs[:, :], ALU.subtract).then_inc(s["f_zq2"], 1)
                dve.wait_ge(s["f_fq"], rf)
                dve.tensor_tensor(q_t[p][:, :], rot[:, :], factor[:, :], ALU.mult).then_inc(s["f_qt"], 1)
                dve.wait_ge(s["f_qt"], rf)
                rotate(FB, FA, s["f_ka"], s["f_sk"], s["f_kb"], s["f_ks"], s["f_rk"])
            if tail:
                dve.wait_ge(s["m_rs3"], rm)
                centred(xl2, y1, mv_m, rs3[:, 0, :], s["m_xl2"])
            if front:
                dve.wait_ge(s["f_ssk"], rf)
                dve.tensor_scalar(lnorm[:, :], FB[:, :], 1e-24, None, ALU.max).then_inc(s["f_mk"], 1)
                dve.wait_ge(s["f_lk"], rf)
                dve.wait_ge(s["f_lgcp"], rf)
                dve.scalar_tensor_tensor(factor[:, :], lnorm[:, :], -0.5, lgcp[:, :], ALU.mult, ALU.subtract).then_inc(s["f_zk"], 1)
            if scores:
                heads_out(2)
            if front:
                dve.wait_ge(s["f_fk"], rf)
                dve.tensor_tensor(rot[:, :], rot[:, :], factor[:, :], ALU.mult).then_inc(s["f_k1"], 1)
                dve.wait_ge(s["f_k1"], rf)
                dve.tensor_tensor(rot[:, :], rot[:, :], pexp[:, :], ALU.mult).then_inc(s["f_k2"], 1)
            if tail:
                dve.wait_ge(s["m_aff"], rm)
                dve.tensor_scalar(c["aff"][:, bass.ds(m * TS, TS), :], M[:, 0:TS * E].rearrange("p (j e) -> p j e", j=TS),
                                  1.0, None, ALU.mult).then_inc(s["m_aff_sb"], 1)
            if scores:
                heads_out(3)
            dve.drain().then_inc(s["end_dve"], 1)

        def pool_step(pool, k, half, p, front, scores, tail):
            begin(pool, k)
            rf, m, rm = k + 1, k - 2, k - 1
            if front:
                pool.wait_ge(s["f_rs"], rf)
                pool.wait_ge(s["xlb_stored"], 16 * k)
                pool.tensor_tensor(xl[:, :, :], x_in[p][:, :, :], of_tile(mv[:, :, 0]), ALU.subtract).then_inc(s["f_xl"], 1)
                pool.wait_ge(s["f_xl"], rf)
                pool.tensor_tensor(xl[:, :, :], xl[:, :, :], of_tile(rs[:, 0, :]), ALU.mult).then_inc(s["f_xl2"], 1)
                pool.wait_ge(s["f_xl2"], rf)
                pool.tensor_tensor(xl[:, :, :], xl[:, :, :], c["rows"][:, 0:1, :].to_broadcast([P, TS, D]), ALU.add).then_inc(s["f_xlb"], 1)
            else:
                pool.wait_ge(s["xlb_stored"], 16 * PAIRS)
            if tail:
                pool.wait_ge(s["m_x1"], rm)
                pool.tensor_tensor(x1b[:, :, :], x1[:, :, :], c["rows"][:, 1:2, :].to_broadcast([P, TS, D]), ALU.add).then_inc(s["m_x1b"], 1)
                pool.wait_ge(s["m_rs3"], rm)
                pool.wait_ge(s["y_stored"], 48 * m + 1)
                pool.tensor_tensor(xn2[:, :, :], y1[:, :, :], of_tile(mv_m[:, :, 0]), ALU.subtract).then_inc(s["m_xn2a"], 1)
                pool.wait_ge(s["m_xn2a"], rm)
                pool.tensor_tensor(xn2[:, :, :], xn2[:, :, :], of_tile(rs3[:, 1, :]), ALU.mult).then_inc(s["m_xn2"], 1)
            pool.drain().then_inc(s["end_pool"], 1)

        def steps(eng, step):
            step(eng, 0, 0, 0, True, False, False)
            step(eng, 1, 0, 1, True, True, False)
            with eng.Fori(0, (PAIRS - 2) // 2) as n:
                for p in range(2):
                    step(eng, n * 2 + (2 + p), n + 1, p, True, True, True)
            step(eng, PAIRS, PAIRS // 2, 0, False, True, True)
            step(eng, PAIRS + 1, PAIRS // 2, 1, False, False, True)

        block = ctx.enter_context(nc.Block())

        @block.sync
        def _(sp):
            sp.dma_start(x_in[0][:, :, :], rows(dram["x"], 0)).then_inc(s["x_loaded0"], 16)
            sp_step(sp, 0, 0, True, False, True)
            sp_step(sp, 1, 1, True, False, True)
            with sp.Fori(0, (PAIRS - 2) // 2 - 1) as n:
                for p in range(2):
                    sp_step(sp, n * 2 + (2 + p), p, True, True, True)
            sp_step(sp, PAIRS - 2, 0, True, True, True)
            sp_step(sp, PAIRS - 1, 1, True, True, False)
            sp_step(sp, PAIRS, 0, False, True, False)
            sp_step(sp, PAIRS + 1, 1, False, True, False)
            sp.wait_ge(s["y_stored"], 48 * PAIRS + 1)
            sp.wait_ge(s["xlb_stored"], 16 * PAIRS)

        @block.tensor
        def _(pe):
            steps(pe, pe_step)

        @block.scalar
        def _(act):
            steps(act, act_step)

        @block.vector
        def _(dve):
            dve.sem_inc(s["y_stored"], 1)
            for n in range(2):
                dve.memset(v_a[n][:, :, :, DH:DH + 1], 1.0)
                dve.memset(v_a[n][:, :, :, DH + 1:], 0.0)
            steps(dve, dve_step)

        @block.gpsimd
        def _(pool):
            steps(pool, pool_step)




def routing(nc, dram, d, c, banks):
    with ExitStack() as ctx:
        s = semaphores(nc, ctx, "route", """r_dve r_hot r_rank r_total r_exp r_slot r_passed r_idx
            r_loaded0 r_loaded1 r_sent0 r_sent1""")
        sb = lambda name, shape, dtype=fp32: ctx.enter_context(nc.sbuf_tensor(name, shape, dtype))
        best = sb("best", [P, TILES])
        first = sb("first", [P, TILES])
        hot = sb("hot", [P, TILES, E])
        order = sb("order", [P, E])
        total = sb("total", [P, E, TILES])
        before = sb("before", [P, E, TILES])
        same = sb("same", [P, E, TILES])
        count = sb("count", [P, E])
        count_i = sb("count_i", [P, E], i32)
        end = sb("end", [P, E])
        pos = sb("pos", [P, TILES, E])
        slot_f = sb("slot_f", [P, TILES])
        past = sb("past", [1, ETILES, E - 1])
        of = sb("of", [1, ETILES])
        neg = sb("neg", [P, TILES])
        stage = [sb(f"stage{n}", [P, TS, D]) for n in range(2)]
        idx = [sb(f"idx{n}", [P, TS], i32) for n in range(2)]
        loaded, sent = [s["r_loaded0"], s["r_loaded1"]], [s["r_sent0"], s["r_sent1"]]
        by_tile = lambda a: a.rearrange("p e t -> p t e")
        each = lambda a: a.unsqueeze(2).to_broadcast([P, TILES, E])
        block = ctx.enter_context(nc.Block())

        @block.vector
        def _(dve):
            n = [0]

            def chain(ins):
                n[0] += 1
                ins.then_inc(s["r_dve"], 1)
                dve.wait_ge(s["r_dve"], n[0])

            chain(dve.tensor_reduce(best[:, :], c["aff"][:, :, :], AX.X, ALU.max))
            chain(dve.tensor_scalar(order[:, :], c["tile_no"][:, 0:E], -1.0, float(E), ALU.mult, ALU.add))
            chain(dve.tensor_tensor(hot[:, :, :], c["aff"][:, :, :], each(best[:, :]), ALU.is_ge))
            chain(dve.tensor_tensor(hot[:, :, :], hot[:, :, :], order[:, :].unsqueeze(1).to_broadcast([P, TILES, E]), ALU.mult))
            chain(dve.tensor_reduce(first[:, :], hot[:, :, :], AX.X, ALU.max))
            dve.tensor_tensor(hot[:, :, :], hot[:, :, :], each(first[:, :]), ALU.is_equal).then_inc(s["r_hot"], 1)
            chain(dve.tensor_scalar(neg[:, :], best[:, :], -1.0, 87.0, ALU.mult, ALU.min))
            dve.wait_ge(s["r_exp"], 1)
            chain(dve.tensor_scalar(neg[:, :], neg[:, :], 1.0, None, ALU.add))
            chain(dve.reciprocal(c["alpha"][:, :], neg[:, :]))
            chain(dve.memset(same[:, :, :], 1.0))
            chain(dve.memset(same[:, :, 0:1], 0.0))
            dve.wait_ge(s["r_total"], 1)
            chain(dve.tensor_copy(total[:, :, :], banks[1].rearrange("p (t e) -> p e t", e=E)))
            chain(dve.tensor_tensor_scan(before.rearrange("p e t -> p (e t)"), same.rearrange("p e t -> p (e t)"),
                                         total.rearrange("p e t -> p (e t)"), 0.0, ALU.mult, ALU.add))
            chain(dve.tensor_scalar(count[:, :], before[:, :, TILES - 1], float(P - 1), None, ALU.add))
            chain(dve.tensor_copy(count_i[:, :], count[:, :]))
            chain(dve.tensor_scalar(count_i[:, :], count_i[:, :], 7, None, ALU.logical_shift_right))
            chain(dve.tensor_copy(count[:, :], count_i[:, :]))
            chain(dve.tensor_tensor_scan(end[:, :], c["ones"][:, 0:E], count[:, :], 0.0, ALU.mult, ALU.add))
            chain(dve.tensor_tensor(count[:, :], end[:, :], count[:, :], ALU.subtract))
            chain(dve.tensor_tensor(before[:, :, :], before[:, :, :], total[:, :, :], ALU.subtract))
            chain(dve.tensor_scalar(count[:, :], count[:, :], float(P), None, ALU.mult))
            chain(dve.tensor_tensor(before[:, :, :], before[:, :, :], count[:, :].unsqueeze(2).to_broadcast([P, E, TILES]), ALU.add))
            chain(dve.tensor_tensor(pos[:, :, :], banks[0].rearrange("p (t e) -> p t e", e=E), by_tile(before), ALU.add))
            chain(dve.tensor_tensor(pos[:, :, :], pos[:, :, :], hot[:, :, :], ALU.mult))
            chain(dve.tensor_reduce(slot_f[:, :], pos[:, :, :], AX.X, ALU.add))
            dve.tensor_copy(c["slot"][:, :], slot_f[:, :]).then_inc(s["r_slot"], 1)
            chain(dve.tensor_tensor(past[:, :, :], c["tile_no"][0:1, :].unsqueeze(2).to_broadcast([1, ETILES, E - 1]),
                                    end[0:1, 0:E - 1].unsqueeze(1).to_broadcast([1, ETILES, E - 1]), ALU.is_ge))
            chain(dve.tensor_reduce(of[:, :], past[:, :, :], AX.X, ALU.add))
            dve.tensor_scalar(c["tile_col"][:, 0, :], of[:, :], float(F), None, ALU.mult)
            chain(dve.tensor_copy(c["tile_col"][:, 1, :], of[:, :]))

        @block.scalar
        def _(act):
            act.preload_act_table_set(EXP_LN)
            act.wait_ge(s["r_dve"], 6)
            act.activation(neg[:, :], neg[:, :], ACT.Exp).then_inc(s["r_exp"], 1)

        @block.tensor
        def _(pe):
            pe.wait_ge(s["r_hot"], 1)
            pe.matmul(banks[0][:, :], c["strict"], hot.rearrange("p t e -> p (t e)"), start=True, stop=True)
            pe.matmul(banks[1][:, :], c["ones"], hot.rearrange("p t e -> p (t e)"), start=True, stop=True).then_inc(s["r_total"], 1)

        @block.sync
        def _(sp):
            def load(at, h):
                sp.dma_start(stage[h][:, :, :], d["xn2"][bass.ds(at, STEP), :].rearrange("(j p) d -> p j d", p=P)).then_inc(loaded[h], 16)

            for h in range(2):
                load(h * STEP, h)
            with sp.Fori(0, PAIRS // 2 - 1) as n:
                for h in range(2):
                    at, free = sp.snap(n * (2 * STEP) + (2 + h) * STEP), sp.snap(n * (16 * TS) + 16 * TS)
                    sp.wait_ge(sent[h], free)
                    load(at, h)

        @block.gpsimd
        def _(pool):
            pool.wait_ge(s["r_slot"], 1)
            with pool.Fori(0, PAIRS // 2) as n:
                for h in range(2):
                    pool.wait_ge(loaded[h], 16 * n + 16)
                    pool.sem_inc(s["r_passed"], 1)
                    pool.tensor_copy(idx[h][:, :], c["slot"][:, bass.ds(n * (2 * TS) + h * TS, TS)]).then_inc(s["r_idx"], 1)
                    pool.wait_ge(s["r_idx"], 2 * n + (h + 1))
                    pool.sem_inc(s["r_passed"], 1)
                    for j in range(TS):
                        pool.indirect_dma_start(out=d["sorted_in"], out_offset=bass.IndirectOffsetOnAxis(ap=idx[h][:, j:j + 1], axis=0),
                                                in_=stage[h][:, j, :], in_offset=None).then_inc(sent[h], 16)
            for h in range(2):
                pool.wait_ge(sent[h], 16 * TS * (PAIRS // 2))




def experts(nc, d, c, banks):
    SLOTS = 4
    PASSES = ETILES // SLOTS
    with ExitStack() as ctx:
        s = semaphores(nc, ctx, "expert", """loaded0 loaded1 loaded2 loaded3 stored0 stored1 stored2 stored3
            x_t xt_sb weights hidden relu_sb result result_sb passed w_passed""")
        sb = lambda name, shape, dtype=fp32: [ctx.enter_context(nc.sbuf_tensor(f"{name}{h}", shape, dtype)) for h in range(SLOTS)]
        xs, xt, hid, ys = sb("xs", [P, D]), sb("xst", [P, P]), sb("hid", [P, F]), sb("ys", [P, D])
        w1 = sb("w1_tile", [P, F])
        loaded, stored = [s["loaded0"], s["loaded1"], s["loaded2"], s["loaded3"]], [s["stored0"], s["stored1"], s["stored2"], s["stored3"]]
        XB, HB, YB = banks[0:2], banks[2:4], banks[4:6]
        block = ctx.enter_context(nc.Block())

        @block.sync
        def _(sp):
            def load(at, j):
                sp.dma_start(xs[j][:, :], d["sorted_in"][bass.ds(at, P), :]).then_inc(loaded[j], 16)

            def store(at, j):
                sp.dma_start(d["sorted_out"][bass.ds(at, P), :], ys[j][:, :]).then_inc(stored[j], 16)

            for j in range(SLOTS):
                load(j * P, j)
            with sp.Fori(0, PASSES - 1) as n:
                for j in range(SLOTS):
                    done, ahead, here = (sp.snap(v) for v in (n * SLOTS + (j + 1), n * (SLOTS * P) + (SLOTS + j) * P, n * (SLOTS * P) + j * P))
                    sp.wait_ge(s["x_t"], done)
                    load(ahead, j)
                    sp.wait_ge(s["result_sb"], done)
                    store(here, j)
            for j in range(SLOTS):
                t = ETILES - SLOTS + j
                sp.wait_ge(s["result_sb"], t + 1)
                store(t * P, j)
            for j in range(SLOTS):
                sp.wait_ge(stored[j], 16 * PASSES)

        @block.tensor
        def _(pe):
            def expert_of(t):
                col = pe.value_load(c["tile_col"][0:1, 0, bass.ds(t, 1)], min_val=0, max_val=(E - 1) * F)
                ex = pe.value_load(c["tile_col"][0:1, 1, bass.ds(t, 1)], min_val=0, max_val=E - 1)
                return col, c["sel"][:, bass.ds(ex, 1), :].rearrange("k a p -> k (a p)")

            def turned(n, j, first):
                t = n * SLOTS + j
                pe.wait_ge(loaded[j % SLOTS], 16 * n + 16 * (1 + j // SLOTS))
                if not (first and j < 2):
                    pe.wait_ge(s["xt_sb"], t - 1)
                pe.transpose(XB[j % 2][:, 0:P], xs[j % SLOTS][:, :], c["ident"]).then_inc(s["x_t"], 1)

            def up(n, j, first, col, row):
                t, bank = n * SLOTS + j, HB[j % 2]
                if not (first and j < 2):
                    pe.wait_ge(s["relu_sb"], t - 1)
                pe.sem_inc(s["passed"], 1)
                for f in range(FC):
                    pe.matmul(bank[:, f * P:(f + 1) * P], c["b1_split"][:, f * P:(f + 1) * P], row, start=f == 0, stop=False, skip_group_check=True)
                pe.wait_ge(s["xt_sb"], t + 1)
                pe.wait_ge(s["weights"], t + 1)
                for f in range(FC):
                    last = pe.matmul(bank[:, f * P:(f + 1) * P], w1[j][:, f * P:(f + 1) * P], xt[j][:, :],
                                     start=False, stop=True, skip_group_check=True)
                last.then_inc(s["hidden"], 1)

            def down(n, j, first, col, row):
                t, bank = n * SLOTS + j, YB[j % 2]
                if not (first and j < 2):
                    pe.wait_ge(s["result_sb"], t - 1)
                pe.sem_inc(s["passed"], 1)
                pe.matmul(bank[:, 0:D], row, c["b2_split"][:, :], start=True, stop=False)
                pe.wait_ge(s["relu_sb"], t + 1)
                for f in range(FC):
                    last = pe.matmul(bank[:, 0:D], hid[j][:, f * P:(f + 1) * P], c["w_2"][:, bass.ds(col + f * P, P)],
                                     start=False, stop=f == FC - 1)
                last.then_inc(s["result"], 1)

            def one_pass(n, before, first, last):
                behind = None
                if not first:
                    behind = (before, SLOTS - 1, expert_of(before * SLOTS + (SLOTS - 1)))
                for j in range(SLOTS):
                    weights = expert_of(n * SLOTS + j)
                    if not (last and j + 2 >= SLOTS):
                        turned(n, j + 2, first)
                    up(n, j, first, *weights)
                    if behind:
                        down(behind[0], behind[1], first and behind[1] < 2, *behind[2])
                    behind = (n, j, weights)
                if last:
                    down(behind[0], behind[1], False, *behind[2])

            turned(0, 0, True)
            turned(0, 1, True)
            one_pass(0, None, True, False)
            with pe.Fori(0, PASSES - 2) as n:
                one_pass(n + 1, n, False, False)
            one_pass(PASSES - 1, PASSES - 2, False, True)

        @block.gpsimd
        def _(pool):
            def copy(n, j, first):
                t = n * SLOTS + j
                col = pool.value_load(c["tile_col"][0:1, 0, bass.ds(t, 1)], min_val=0, max_val=(E - 1) * F)
                if not first:
                    pool.wait_ge(s["hidden"], t - (SLOTS - 1))
                    pool.sem_inc(s["w_passed"], 1)
                pool.tensor_copy(w1[j][:, :], c["w_1"][:, bass.ds(col, F)]).then_inc(s["weights"], 1)

            for j in range(SLOTS):
                copy(0, j, True)
            with pool.Fori(0, PASSES - 1) as n:
                for j in range(SLOTS):
                    copy(n + 1, j, False)

        @block.scalar
        def _(act):
            def relu(n, j, first):
                t = n * SLOTS + j
                if not first:
                    act.wait_ge(s["result"], t - (SLOTS - 1))
                act.wait_ge(s["hidden"], t + 1)
                act.activation(hid[j][:, :], HB[j % 2][:, :], ACT.Relu).then_inc(s["relu_sb"], 1)

            for j in range(SLOTS):
                relu(0, j, True)
            with act.Fori(0, PASSES - 1) as n:
                for j in range(SLOTS):
                    relu(n + 1, j, False)

        @block.vector
        def _(dve):
            def features(n, j, first):
                t = n * SLOTS + j
                if not (first and j < SLOTS):
                    dve.wait_ge(s["hidden"], t - (SLOTS - 1))
                dve.wait_ge(s["x_t"], t + 1)
                dve.tensor_copy(xt[j % SLOTS][:, :], XB[j % 2][:, 0:P]).then_inc(s["xt_sb"], 1)

            def result(n, j, first):
                t = n * SLOTS + j
                if not first:
                    dve.wait_ge(stored[j], 16 * n)
                dve.wait_ge(s["result"], t + 1)
                dve.tensor_copy(ys[j][:, :], YB[j % 2][:, 0:D]).then_inc(s["result_sb"], 1)

            def one_pass(n, first, last):
                for j in range(SLOTS):
                    if not (last and j + 2 >= SLOTS):
                        features(n, j + 2, first)
                    result(n, j, first)

            features(0, 0, True)
            features(0, 1, True)
            one_pass(0, True, False)
            with dve.Fori(0, PASSES - 2) as n:
                one_pass(n + 1, False, False)
            one_pass(PASSES - 1, False, True)


def scan_layer(nc, d, c, banks, out):
    with ExitStack() as ctx:
        s = semaphores(nc, ctx, "scan", """
            end_pe end_act end_dve end_pool
            g_loaded0 g_loaded1 g_gathered0 g_gathered1 g_passed g_idx
            g_al g_o g_st g_mv g_ln g_rs g_on g_y2 g_y2_stored g_st2 g_mv2 g_ln2 g_rs2 g_xn
            g_t g_xt g_conv g_silu g_ssm g_ssm_sb g_dtr g_split g_dt g_pre g_abs g_exp g_log g_delta g_u
            n_b n_c n_c_sb w_passed n_da n_dbx n_h n_hc n_y n_yt
            w_y2_loaded w_proj w_st w_mv w_ln w_rs w_on w_y3 w_st2 w_mv2 w_ln2 w_rs2 w_xl w_t w_ot w_mean
            w_gc w_gc_sb w_base w_net w_net_sb w_twist w_cp w_turn w_o
            o_t o_st o_mv o_ln o_rs o_on o_sum o_stored""")
        sb = lambda name, shape, dtype=fp32: ctx.enter_context(nc.sbuf_tensor(name, shape, dtype))
        two = lambda name, shape, dtype=fp32: [sb(f"{name}{n}", shape, dtype) for n in range(2)]
        y1 = two("g_y1", [P, TS, D])
        xl2 = two("g_xl2", [P, TS, D])
        ffn = two("g_ffn", [P, TS, D])
        idx = two("g_idx", [P, TS], i32)
        al = sb("g_al", [P, TS])
        o = sb("g_o", [P, TS, D])
        y2 = sb("g_y2", [P, TS, D])
        xn = sb("g_xn", [P, TS, D])
        stats_g = sb("g_stats", [P, TS, 6])
        mv_g = sb("g_mean_var", [P, TS, 2])
        ln_g = sb("g_ln", [P, TS])
        rs_g = sb("g_rstd", [P, TS])
        xpad = sb("xpad", [P, 2, T + TAPS - 1])
        ssm = sb("ssm", [2 * NS + DR, STEP])
        dtr = sb("dtr", [DR, STEP])
        hi = sb("bc_hi", [2 * NS, STEP], bf16)
        mid = sb("bc_mid", [2 * NS, STEP], bf16)
        rest = sb("bc_rest", [2 * NS, STEP])
        pre = sb("g_pre", [P, DHV, STEP])
        mag = sb("g_mag", [P, DHV, STEP])
        xv = two("xv", [P, DHV, STEP])
        bcs = two("bcs", [96, STEP], bf16)
        delta = two("delta", [P, DHV, STEP])
        u_in = two("u_in", [P, DHV, STEP])
        RING = 8
        decay = [sb(f"decay{n}", [P, DHV, 2, T]) for n in range(RING)]
        dbx = two("dbx", [P, DHV, STEP])
        h = [sb(f"h{n}", [P, DHV, STEP]) for n in range(3)]
        crep = two("crep", [P, STEP])
        hc = two("hc", [P, DHV, STEP])
        yt = two("yt", [P, DHV, STEP])
        y2r = sb("w_y2", [P, TS, D])
        on = sb("w_on", [P, TS, D])
        xl4 = sb("w_xl", [P, TS, D])
        stats_w = sb("w_stats", [P, TS, 6])
        mv_w = sb("w_mean_var", [P, TS, 2])
        ln_w = sb("w_ln", [P, TS])
        rs_w = sb("w_rstd", [P, TS])
        total = sb("w_total", [P, 2])
        gc1 = sb("gc1", [64, 2])
        gc2 = sb("gc2", [32, 2])
        gc3 = sb("gc3", [P, 2])
        base = sb("w_base", [P, 2])
        net1 = sb("net1", [P, STEP])
        net2 = sb("net2", [64, STEP])
        net3 = sb("net3", [32, STEP])
        th = sb("w_th", [P, STEP])
        cp = sb("w_cp", [P, STEP])
        half_cn = sb("half_cn", [P, 1])
        half_gc = sb("half_gc", [P, 1])
        ar3 = sb("ar3", [P, 1])
        ar7 = sb("ar7", [P, 1])
        y3 = two("y3", [P, TS, D])
        o_t = two("o_t", [P, STEP])
        stats_o = sb("o_stats", [P, TS, 6])
        mv_o = sb("o_mean_var", [P, TS, 2])
        ln_o = sb("o_ln", [P, TS])
        rs_o = sb("o_rstd", [P, TS])
        fin = sb("fin", [P, TS, D])
        res = sb("res", [P, TS, D])
        hold = sb("c_hold", [P, 1])

        BB, TW, CB, YB, GA, GB, W = banks[0], banks[1], banks[2], banks[3:5], banks[5], banks[6], banks[7]
        loaded, gathered = [s["g_loaded0"], s["g_loaded1"]], [s["g_gathered0"], s["g_gathered1"]]
        tok = lambda t: t.rearrange("p (j d) -> p j d", j=TS)
        rows = lambda ap, at: ap[bass.ds(at, STEP), :].rearrange("(j p) d -> p j d", p=P)
        w_x = c["w_x"].rearrange("p (f m) -> p f m", f=DHV)
        w_out = c["w_out"].rearrange("p (f m) -> p f m", f=DHV)
        NET, GCN = 4 * CYCLES, 3

        def begin(eng, k):
            if isinstance(k, int) and k == 0:
                return
            for sem in (s["end_pe"], s["end_act"], s["end_dve"], s["end_pool"]):
                eng.wait_ge(sem, k)

        def sp_step(sp, k, p, front, states, wave, finish, load):
            now, rf, ro = (sp.snap(v) for v in (k * 1, k + 1, k - 2 if finish else k * 1))
            here, back_two, back_three, ahead = (sp.snap(v) for v in (
                k * STEP, k * STEP - 2 * STEP if wave else k * STEP, k * STEP - 3 * STEP if finish else k * STEP, k * STEP + STEP))
            if load:
                sp.wait_ge(s["end_dve"], now)
                sp.dma_start(y1[1 - p][:, :, :], rows(d["y1"], ahead)).then_inc(loaded[1 - p], 16)
                sp.dma_start(xl2[1 - p][:, :, :], rows(d["xl2"], ahead)).then_inc(loaded[1 - p], 16)
            if wave:
                sp.wait_ge(s["end_dve"], now)
                if not front:
                    sp.wait_ge(s["g_y2_stored"], 16 * PAIRS)
                sp.dma_start(y2r[:, :, :], rows(d["y2"], back_two)).then_inc(s["w_y2_loaded"], 16)
            if front:
                sp.wait_ge(s["g_y2"], rf)
                sp.dma_start(rows(d["y2"], here), y2[:, :, :]).then_inc(s["g_y2_stored"], 16)
            if finish:
                sp.wait_ge(s["o_sum"], ro)
                sp.dma_start(rows(out, back_three), res[:, :, :]).then_inc(s["o_stored"], 16)

        def pe_step(pe, k, half, p, front, states, wave, finish):
            begin(pe, k)
            rf, u, m, rm, ro = k + 1, k - 1, k - 2, k - 1, k - 2

            def transposes(dst, src, sem):
                for j in range(TS):
                    last = pe.transpose(dst[:, j * P:(j + 1) * P], src[:, j, :], c["ident"])
                last.then_inc(sem, 1)

            def bc(n):
                if not states or n >= NS:
                    return
                if n:
                    pe.wait_ge(s["n_dbx"], u * NS + n)
                pe.matmul(BB[:, :], c["sel"][:, n, :], bcs[1 - p][:, :], start=True, stop=True).then_inc(s["n_b"], 1)
                if n:
                    pe.wait_ge(s["n_c_sb"], u * NS + n)
                pe.matmul(CB[:, :], c["sel"][:, NS + n, :], bcs[1 - p][:, :], start=True, stop=True).then_inc(s["n_c"], 1)

            def y_sum(n):
                if not states or n < 0:
                    return
                pe.wait_ge(s["n_hc"], u * NS + n + 1)
                for hf in range(DHV):
                    last = pe.matmul(YB[hf][:, :], c["ident"], hc[n % 2][:, hf, :], start=n == 0, stop=n == NS - 1)
                last.then_inc(s["n_y"], 1)

            def slot(n):
                bc(n + 1)
                y_sum(n - 2)

            def conv(hf):
                dst = (GB, GA)[hf]
                for tap in range(TAPS):
                    last = pe.matmul(dst.rearrange("p (b t) -> p b t", b=2), c["w_conv"][:, tap, hf * P:(hf + 1) * P],
                                     xpad[:, :, tap:tap + T], start=tap == 0, stop=tap == TAPS - 1)
                last.then_inc(s["g_conv"], 1)

            def context(i):
                if i == 0:
                    pe.wait_ge(s["w_mean"], rm)
                    pe.matmul(W[0:64, 0:2], c["gc_w1"], total[:, :], start=True, stop=True).then_inc(s["w_gc"], 1)
                else:
                    pe.wait_ge(s["w_gc_sb"], m * GCN + i)
                    if i == 1:
                        pe.sem_inc(s["w_passed"], 1)
                        pe.matmul(W[0:32, 0:2], c["gc_w2"][0:64, :], gc1[:, :], start=True, stop=True).then_inc(s["w_gc"], 1)
                    else:
                        pe.matmul(W[:, 0:2], c["gc_w3"][0:32, :], gc2[:, :], start=True, stop=True).then_inc(s["w_gc"], 1)

            def net(i, layer):
                if not wave:
                    return
                if layer == 0:
                    if i == 0:
                        pe.wait_ge(s["w_gc_sb"], m * GCN + GCN)
                        if finish:
                            pe.wait_ge(s["o_on"], ro)
                    else:
                        pe.wait_ge(s["w_o"], m * CYCLES + i)
                    pe.matmul(W[:, :], c["cn_w1"], o_t[p][:, :], start=True, stop=True).then_inc(s["w_net"], 1)
                    pe.matmul(TW[:, :], c["twist"], o_t[p][:, :], start=True, stop=True).then_inc(s["w_twist"], 1)
                    return
                pe.wait_ge(s["w_net_sb"], m * NET + i * 4 + layer)
                if layer == 1:
                    pe.matmul(W[0:64, :], c["cn_w2"], net1[:, :], start=True, stop=True).then_inc(s["w_net"], 1)
                elif layer == 2:
                    pe.sem_inc(s["w_passed"], 1)
                    pe.matmul(W[0:32, :], c["cn_w3"][0:64, :], net2[:, :], start=True, stop=True).then_inc(s["w_net"], 1)
                else:
                    pe.matmul(W[:, :], c["cn_w4"][0:32, :], net3[:, :], start=True, stop=True).then_inc(s["w_net"], 1)

            bc(0)
            if wave:
                for j in range(TS):
                    for hf in range(DHV):
                        last = pe.matmul(W[:, j * P:(j + 1) * P], yt[p][:, hf, j * P:(j + 1) * P], w_out[:, hf, :],
                                         start=hf == 0, stop=hf == DHV - 1)
                last.then_inc(s["w_proj"], 1)
            if finish:
                for j in range(TS):
                    last = pe.transpose(TW[:, j * P:(j + 1) * P], o_t[1 - p][:, j * P:(j + 1) * P], c["ident"])
                last.then_inc(s["o_t"], 1)
            slot(0)
            slot(1)
            if front:
                pe.wait_ge(s["g_xn"], rf)
                transposes(GA, xn, s["g_t"])
            if wave:
                pe.wait_ge(s["w_xl"], rm)
                transposes(W, xl4, s["w_t"])
            slot(2)
            slot(3)
            if front:
                pe.wait_ge(s["g_xt"], rf)
                conv(0)
            slot(4)
            if front:
                conv(1)
            if wave:
                context(0)
            slot(5)
            slot(6)
            slot(7)
            if front:
                pe.wait_ge(s["g_silu"], 2 * k + 2)
                for hf in range(DHV):
                    last = pe.matmul(GB[0:2 * NS + DR, :], w_x[:, hf, :], xv[p][:, hf, :], start=hf == 0, stop=hf == DHV - 1)
                last.then_inc(s["g_ssm"], 1)
            if wave:
                context(1)
            slot(8)
            if wave:
                context(2)
            net(0, 0)
            slot(9)
            net(0, 1)
            if front:
                pe.wait_ge(s["g_dtr"], rf)
                for hf in range(DHV):
                    last = pe.matmul((GA, GB)[hf][:, :], c["w_dt"][:, hf * P:(hf + 1) * P], dtr[:, :], start=True, stop=True)
                last.then_inc(s["g_dt"], 1)
            net(0, 2)
            slot(10)
            net(0, 3)
            slot(11)
            net(1, 0)
            net(1, 1)
            slot(12)
            net(1, 2)
            net(1, 3)
            slot(13)
            net(2, 0)
            net(2, 1)
            slot(14)
            net(2, 2)
            net(2, 3)
            slot(15)
            y_sum(14)
            y_sum(15)
            pe.drain().then_inc(s["end_pe"], 1)

        def act_step(act, k, half, p, front, states, wave, finish):
            act.preload_act_table_set(EXP_LN)
            begin(act, k)
            rf, u, m, rm, ro = k + 1, k - 1, k - 2, k - 1, k - 2

            def root(var, ln, dst, wait, s_ln, s_rs, r):
                act.wait_ge(wait, r)
                act.activation(ln[:, :], var, ACT.Ln, bias=EPS).then_inc(s_ln, 1)
                act.wait_ge(s_ln, r)
                act.activation(dst[:, :], ln[:, :], ACT.Exp, scale=-0.5).then_inc(s_rs, 1)

            def decays(n):
                if not states:
                    return
                if n >= RING:
                    act.wait_ge(s["n_h"], u * NS + n - RING + 1)
                for hf in range(DHV):
                    src = delta[1 - p][:, hf, :].rearrange("p (b t) -> p b t", b=2)
                    last = act.activation(decay[n % RING][:, hf, :, 1:], src[:, :, 1:], ACT.Exp, scale=c["neg_a"][:, hf, n:n + 1])
                last.then_inc(s["n_da"], 1)

            def copy_c(n):
                if not states:
                    return
                if n >= 2:
                    act.wait_ge(s["n_hc"], u * NS + n - 1)
                act.wait_ge(s["n_c"], u * NS + n + 1)
                act.activation(crep[n % 2][:, :], CB[:, :], ACT.Copy).then_inc(s["n_c_sb"], 1)

            def context(i):
                act.wait_ge(s["w_gc"], m * GCN + i + 1)
                if i == 0:
                    act.activation(gc1[:, :], W[0:64, 0:2], ACT.Gelu, bias=c["gc_b1"][0:64, :], scale=1.0 / T).then_inc(s["w_gc_sb"], 1)
                elif i == 1:
                    act.activation(gc2[:, :], W[0:32, 0:2], ACT.Gelu, bias=c["gc_b2"][0:32, :]).then_inc(s["w_gc_sb"], 1)
                else:
                    act.activation(gc3[:, :], W[:, 0:2], ACT.Tanh, bias=half_gc[:, :], scale=0.5).then_inc(s["w_gc_sb"], 1)

            def net(i, layer):
                if not wave:
                    return
                act.wait_ge(s["w_net"], m * NET + i * 4 + layer + 1)
                if layer == 0:
                    ins = act.activation(net1[:, :], W[:, :], ACT.Gelu, bias=c["cn_b1"])
                elif layer == 1:
                    ins = act.activation(net2[:, :], W[0:64, :], ACT.Gelu, bias=c["cn_b2"][0:64, :])
                elif layer == 2:
                    ins = act.activation(net3[:, :], W[0:32, :], ACT.Gelu, bias=c["cn_b3"][0:32, :])
                else:
                    ins = act.activation(th[:, :], W[:, :], ACT.Tanh, bias=half_cn[:, :], scale=0.5)
                ins.then_inc(s["w_net_sb"], 1)

            decays(0)
            copy_c(0)
            if front:
                root(mv_g[:, :, 1], ln_g, rs_g, s["g_mv"], s["g_ln"], s["g_rs"], rf)
            if wave:
                root(mv_w[:, :, 1], ln_w, rs_w, s["w_mv"], s["w_ln"], s["w_rs"], rm)
            decays(1)
            if finish:
                root(mv_o[:, :, 1], ln_o, rs_o, s["o_mv"], s["o_ln"], s["o_rs"], ro)
            copy_c(1)
            decays(2)
            if front:
                root(mv_g[:, :, 1], ln_g, rs_g, s["g_mv2"], s["g_ln2"], s["g_rs2"], rf)
            if wave:
                root(mv_w[:, :, 1], ln_w, rs_w, s["w_mv2"], s["w_ln2"], s["w_rs2"], rm)
            decays(3)
            copy_c(2)
            decays(4)
            if front:
                act.wait_ge(s["g_t"], rf)
                act.activation(xpad[:, :, TAPS - 1:], GA.rearrange("p (b t) -> p b t", b=2), ACT.Copy).then_inc(s["g_xt"], 1)
            copy_c(3)
            if wave:
                act.wait_ge(s["w_t"], rm)
                act.activation(o_t[p][:, :], W[:, :], ACT.Copy).then_inc(s["w_ot"], 1)
            for n in range(5, NS):
                decays(n)
                if n % 2 == 0:
                    copy_c(4 + (n - 6) // 2)
            if front:
                for hf in range(DHV):
                    act.wait_ge(s["g_conv"], 2 * k + hf + 1)
                    act.activation(xv[p][:, hf, :], (GB, GA)[hf][:, :], ACT.Silu, bias=c["conv_b"][:, hf:hf + 1]).then_inc(s["g_silu"], 1)
            if wave:
                context(0)
            if front:
                act.wait_ge(s["g_ssm"], rf)
                act.activation(ssm[:, :], GB[0:2 * NS + DR, :], ACT.Copy).then_inc(s["g_ssm_sb"], 1)
            if wave:
                context(1)
                context(2)
            copy_c(9)
            net(0, 0)
            net(0, 1)
            copy_c(10)
            net(0, 2)
            net(0, 3)
            copy_c(11)
            net(1, 0)
            net(1, 1)
            copy_c(12)
            net(1, 2)
            net(1, 3)
            copy_c(13)
            net(2, 0)
            net(2, 1)
            copy_c(14)
            net(2, 2)
            net(2, 3)
            copy_c(15)
            if front:
                act.preload_act_table_set(EXP_LN)
                act.wait_ge(s["g_pre"], rf)
                act.activation(mag[:, :, :], pre[:, :, :], ACT.Abs).then_inc(s["g_abs"], 1)
                act.wait_ge(s["g_abs"], rf)
                act.activation(mag[:, :, :], mag[:, :, :], ACT.Exp, scale=-1.0).then_inc(s["g_exp"], 1)
                act.wait_ge(s["g_exp"], rf)
                act.activation(mag[:, :, :], mag[:, :, :], ACT.Ln, bias=1.0).then_inc(s["g_log"], 1)
            act.drain().then_inc(s["end_act"], 1)

        def dve_step(dve, k, half, p, front, states, wave, finish):
            if front:
                dve.wait_ge(s["end_dve"], k)
                dve.tensor_scalar(al[:, :], c["alpha"][:, bass.ds(k * TS, TS)], 1.0, None, ALU.mult).then_inc(s["g_al"], 1)
            begin(dve, k)
            rf, u, m, rm, ro = k + 1, k - 1, k - 2, k - 1, k - 2

            def stats_of(src, st, out_mv, s_st, s_mv, r):
                for j in range(TS):
                    last = dve.bn_stats(st[:, j, :], src[:, j, :])
                last.then_inc(s_st, 1)
                dve.wait_ge(s_st, r)
                dve.memset(hold[:, :], 0.0)
                for j in range(TS):
                    last = dve.bn_aggr(out_mv[:, j, :], st[:, j, :])
                last.then_inc(s_mv, 1)

            def centred(dst, src, mean_var, rstd, wait, sem, r):
                dve.wait_ge(wait, r)
                for j in range(TS):
                    last = dve.tensor_scalar(dst[:, j, :], src[:, j, :], mean_var[:, j, 0:1], rstd[:, j:j + 1], ALU.subtract, ALU.mult)
                last.then_inc(sem, 1)

            def drive(n):
                if not states or n >= NS:
                    return
                dve.wait_ge(s["n_b"], u * NS + n + 1)
                if n >= 2:
                    dve.wait_ge(s["n_h"], u * NS + n - 1)
                dve.tensor_tensor(dbx[n % 2][:, :, :], u_in[1 - p][:, :, :], BB[:, :].unsqueeze(1).to_broadcast([P, DHV, STEP]),
                                  ALU.mult).then_inc(s["n_dbx"], 1)

            def scan(n):
                if not states:
                    return
                dve.wait_ge(s["n_da"], u * NS + n + 1)
                dve.wait_ge(s["n_dbx"], u * NS + n + 1)
                if n >= 3:
                    dve.wait_ge(s["n_hc"], u * NS + n - 2)
                dve.tensor_tensor_scan(h[n % 3].rearrange("p f t -> p (f t)"), decay[n % RING].rearrange("p f b t -> p (f b t)"),
                                       dbx[n % 2].rearrange("p f t -> p (f t)"), 0.0, ALU.mult, ALU.add).then_inc(s["n_h"], 1)

            def slot(n):
                drive(n + 1)
                scan(n)

            def turn(i):
                if not wave:
                    return
                dve.wait_ge(s["w_net_sb"], m * NET + i * 4 + 4)
                if i == 0:
                    dve.wait_ge(s["w_base"], rm)
                for b in range(2):
                    last = dve.tensor_scalar(cp[:, b * T:(b + 1) * T], th[:, b * T:(b + 1) * T], ar3[:, :], base[:, b:b + 1], ALU.mult, ALU.add)
                last.then_inc(s["w_cp"], 1)
                dve.wait_ge(s["w_cp"], m * CYCLES + i + 1)
                dve.wait_ge(s["w_twist"], m * CYCLES + i + 1)
                dve.tensor_tensor(cp[:, :], cp[:, :], TW[:, :], ALU.mult).then_inc(s["w_turn"], 1)
                dve.wait_ge(s["w_turn"], m * CYCLES + i + 1)
                dve.tensor_tensor(o_t[p][:, :], o_t[p][:, :], cp[:, :], ALU.add).then_inc(s["w_o"], 1)

            drive(0)
            if front:
                dve.wait_ge(s["g_al"], rf)
                dve.wait_ge(loaded[p], 32 * half + 32)
                dve.wait_ge(gathered[p], 16 * TS * half + 16 * TS)
                for j in range(TS):
                    last = dve.scalar_tensor_tensor(o[:, j, :], ffn[p][:, j, :], al[:, j:j + 1], xl2[p][:, j, :], ALU.mult, ALU.add)
                last.then_inc(s["g_o"], 1)
                dve.wait_ge(s["g_o"], rf)
                stats_of(o, stats_g, mv_g, s["g_st"], s["g_mv"], rf)
            slot(0)
            if wave:
                dve.wait_ge(s["w_proj"], rm)
                stats_of(tok(W), stats_w, mv_w, s["w_st"], s["w_mv"], rm)
            if front:
                centred(o, o, mv_g, rs_g, s["g_rs"], s["g_on"], rf)
                dve.wait_ge(s["g_on"], rf)
                dve.wait_ge(s["g_y2_stored"], 16 * k)
                dve.tensor_tensor(y2[:, :, :], o[:, :, :], y1[p][:, :, :], ALU.add).then_inc(s["g_y2"], 1)
                dve.wait_ge(s["g_y2"], rf)
                stats_of(y2, stats_g, mv_g, s["g_st2"], s["g_mv2"], rf)
            if wave:
                centred(on, tok(W), mv_w, rs_w, s["w_rs"], s["w_on"], rm)
                dve.wait_ge(s["w_on"], rm)
                dve.wait_ge(s["w_y2_loaded"], 16 * rm)
                dve.tensor_tensor(y3[p][:, :, :], on[:, :, :], y2r[:, :, :], ALU.add).then_inc(s["w_y3"], 1)
                dve.wait_ge(s["w_y3"], rm)
                stats_of(y3[p], stats_w, mv_w, s["w_st2"], s["w_mv2"], rm)
            if finish:
                dve.wait_ge(s["o_t"], ro)
                stats_of(tok(TW), stats_o, mv_o, s["o_st"], s["o_mv"], ro)
            slot(1)
            if front:
                centred(xn, y2, mv_g, rs_g, s["g_rs2"], s["g_xn"], rf)
            if wave:
                centred(xl4, y3[p], mv_w, rs_w, s["w_rs2"], s["w_xl"], rm)
            slot(2)
            if finish:
                centred(fin, tok(TW), mv_o, rs_o, s["o_rs"], s["o_on"], ro)
                dve.wait_ge(s["o_on"], ro)
                dve.wait_ge(s["o_stored"], 16 * (k - 3) + 1)
                dve.tensor_tensor(res[:, :, :], fin[:, :, :], y3[1 - p][:, :, :], ALU.add).then_inc(s["o_sum"], 1)
            slot(3)
            if wave:
                dve.wait_ge(s["w_ot"], rm)
                dve.tensor_reduce(total[:, :], o_t[p].rearrange("p (b t) -> p b t", b=2), AX.X, ALU.add).then_inc(s["w_mean"], 1)
            slot(4)
            slot(5)
            slot(6)
            slot(7)
            if front:
                dve.wait_ge(s["g_ssm_sb"], rf)
                dve.tensor_copy(dtr[:, :], ssm[2 * NS:2 * NS + DR, :]).then_inc(s["g_dtr"], 1)
                n = [0]

                def chain(ins):
                    n[0] += 1
                    ins.then_inc(s["g_split"], 1)
                    dve.wait_ge(s["g_split"], 7 * k + n[0])

                split3(dve, chain, ssm[0:2 * NS, :], bcs[p], hi[:, :], rest[:, :], mid[:, :], 2 * NS)
            slot(8)
            if wave:
                dve.wait_ge(s["w_gc_sb"], m * GCN + GCN)
                dve.tensor_scalar(base[:, :], gc3[:, :], ar7[:, :], 0.1, ALU.mult, ALU.add).then_inc(s["w_base"], 1)
            slot(9)
            if front:
                dve.wait_ge(s["g_dt"], rf)
                for hf in range(DHV):
                    last = dve.tensor_scalar(pre[:, hf, :], (GA, GB)[hf][:, :], c["b_dt"][:, hf:hf + 1], None, ALU.add)
                last.then_inc(s["g_pre"], 1)
            slot(10)
            turn(0)
            slot(11)
            slot(12)
            turn(1)
            slot(13)
            slot(14)
            turn(2)
            slot(15)
            if front:
                dve.wait_ge(s["g_log"], rf)
                dve.scalar_tensor_tensor(delta[p][:, :, :], pre[:, :, :], 0.0, mag[:, :, :], ALU.max, ALU.add).then_inc(s["g_delta"], 1)
                dve.wait_ge(s["g_delta"], rf)
                dve.tensor_tensor(u_in[p][:, :, :], delta[p][:, :, :], xv[p][:, :, :], ALU.mult).then_inc(s["g_u"], 1)
            if states:
                dve.wait_ge(s["n_y"], u * NS + NS)
                for hf in range(DHV):
                    last = dve.scalar_tensor_tensor(yt[1 - p][:, hf, :], xv[1 - p][:, hf, :], c["skip"][:, hf:hf + 1], YB[hf][:, :], ALU.mult, ALU.add)
                last.then_inc(s["n_yt"], 1)
            dve.drain().then_inc(s["end_dve"], 1)

        def gather(pool, pair, p):
            pool.tensor_copy(idx[p][:, :], c["slot"][:, bass.ds(pair * TS, TS)]).then_inc(s["g_idx"], 1)
            pool.wait_ge(s["g_idx"], pair + 1)
            pool.sem_inc(s["g_passed"], 1)
            for j in range(TS):
                pool.indirect_dma_start(out=ffn[p][:, j, :], out_offset=None, in_=d["sorted_out"],
                                        in_offset=bass.IndirectOffsetOnAxis(ap=idx[p][:, j:j + 1], axis=0)).then_inc(gathered[p], 16)

        def pool_step(pool, k, half, p, front, states, wave, finish, load):
            begin(pool, k)
            u = k - 1
            if load:
                pool.sem_inc(s["g_passed"], 1)
                gather(pool, k + 1, 1 - p)
            if states:
                for n in range(NS):
                    pool.wait_ge(s["n_h"], u * NS + n + 1)
                    pool.wait_ge(s["n_c_sb"], u * NS + n + 1)
                    if n >= 2:
                        pool.wait_ge(s["n_y"], u * NS + n - 1)
                    pool.tensor_tensor(hc[n % 2][:, :, :], h[n % 3][:, :, :], crep[n % 2][:, :].unsqueeze(1).to_broadcast([P, DHV, STEP]),
                                       ALU.mult).then_inc(s["n_hc"], 1)
            pool.drain().then_inc(s["end_pool"], 1)

        def steps(eng, step):
            step(eng, 0, 0, 0, True, False, False, False)
            step(eng, 1, 0, 1, True, True, False, False)
            step(eng, 2, 1, 0, True, True, True, False)
            with eng.Fori(0, (PAIRS - 4) // 2) as n:
                step(eng, n * 2 + 3, n + 1, 1, True, True, True, True)
                step(eng, n * 2 + 4, n + 2, 0, True, True, True, True)
            step(eng, PAIRS - 1, PAIRS // 2 - 1, 1, True, True, True, True)
            step(eng, PAIRS, PAIRS // 2, 0, False, True, True, True)
            step(eng, PAIRS + 1, PAIRS // 2, 1, False, False, True, True)
            step(eng, PAIRS + 2, PAIRS // 2 + 1, 0, False, False, False, True)

        block = ctx.enter_context(nc.Block())

        @block.sync
        def _(sp):
            sp.dma_start(y1[0][:, :, :], rows(d["y1"], 0)).then_inc(loaded[0], 16)
            sp.dma_start(xl2[0][:, :, :], rows(d["xl2"], 0)).then_inc(loaded[0], 16)
            steps(sp, lambda eng, k, half, p, *stages: sp_step(eng, k, p, *stages, load=not isinstance(k, int) or k < PAIRS - 1))
            sp.wait_ge(s["o_stored"], 16 * PAIRS + 1)
            sp.wait_ge(s["g_y2_stored"], 16 * PAIRS)

        @block.tensor
        def _(pe):
            steps(pe, pe_step)

        @block.scalar
        def _(act):
            steps(act, act_step)

        @block.vector
        def _(dve):
            dve.sem_inc(s["o_stored"], 1)
            dve.memset(xpad[:, :, 0:TAPS - 1], 0.0)
            for n in range(2):
                dve.memset(bcs[n][:, :], 0.0)
            for n in range(RING):
                dve.memset(decay[n][:, :, :, 0:1], 0.0)
            dve.tensor_scalar(half_cn[:, :], c["cn_b4"], 0.5, None, ALU.mult)
            dve.tensor_scalar(half_gc[:, :], c["gc_b3"], 0.5, None, ALU.mult)
            dve.tensor_scalar(ar3[:, :], c["arange"], 0.3, None, ALU.mult)
            dve.tensor_scalar(ar7[:, :], c["arange"], 0.7, None, ALU.mult)
            steps(dve, dve_step)

        @block.gpsimd
        def _(pool):
            gather(pool, 0, 0)
            steps(pool, lambda eng, k, half, p, *stages: pool_step(eng, k, half, p, *stages, load=not isinstance(k, int) or k < PAIRS - 1))


CONSTS = [("ident", P), ("mask", P), ("ones_blk", P), ("strict", P), ("ones", P), ("twist", P), ("cos", T), ("sin", T),
          ("head_mask", HS), ("sel_cols", 32), ("reset", STEP), ("eye8", E * E), ("tile_no", ETILES)]
VECS = [("gate_b", 1), ("clock_b", 1), ("p_b", 1), ("ln1_g", 1), ("ln1_b", 1), ("ln2_g", 1), ("ln2_b", 1), ("mlp_b1", FC),
        ("conv_b", DHV), ("b_dt", DHV), ("skip", DHV), ("cn_b1", 1), ("cn_b2", 1), ("cn_b3", 1), ("cn_b4", 1),
        ("gc_b1", 1), ("gc_b2", 1), ("gc_b3", 1), ("arange", 1)]
W_A = [("w_gate", D), ("w_clock", D), ("w_p", D), ("w_q", D), ("w_qs", D), ("w_k", D), ("w_ks", D), ("w_v", D), ("w_o", D),
       ("w_up", F), ("w_down", F)]
W_C = [("w_in", DI), ("w_x", DHV * (DR + 2 * NS)), ("w_out", DHV * D), ("cn_w1", 128), ("cn_w2", 64), ("cn_w3", 32), ("cn_w4", P),
       ("gc_w1", 64), ("gc_w2", 32), ("gc_w3", P)]


def constants():
    f = np.float32
    row, col = np.arange(P)[:, None], np.arange(P)[None, :]
    half = DH // 2
    freqs = np.exp(-np.arange(half, dtype=f) * f(np.log(10000.0) / half)).astype(f)
    theta = np.arange(T, dtype=f)[None, :] * freqs[:, None]
    angle = theta[(np.arange(P) % DH) // 2]
    sign = np.where(np.arange(P) % 2 == 0, -1.0, 1.0)[:, None]
    quarter = P // 4
    twist = np.zeros((P, P), f)
    for to, of, by in ((0, 2, 1), (1, 3, -1), (2, 0, -1), (3, 1, 1)):
        twist[of * quarter + np.arange(quarter), to * quarter + np.arange(quarter)] = by
    parts = dict(
        ident=row == col, mask=np.where(row > col, -BIG, 0.0), ones_blk=row // DH == col // DH, strict=row < col,
        ones=np.ones((P, P)), twist=twist, cos=np.cos(angle), sin=np.sin(angle) * sign,
        head_mask=(np.arange(P)[:, None] // DH) % HS == np.arange(HS)[None, :],
        sel_cols=row % 32 == np.arange(32)[None, :],
        reset=np.broadcast_to(np.arange(STEP)[None, :] % T != 0, (P, STEP)),
        eye8=np.broadcast_to(np.eye(E).reshape(1, E * E), (P, E * E)),
        tile_no=np.broadcast_to(np.arange(ETILES)[None, :], (P, ETILES)))
    return np.concatenate([np.asarray(parts[n], f) for n, _ in CONSTS], axis=1)


def laid_out(i):
    def column(v, rows=P):
        v = np.asarray(v).reshape(-1)
        if v.size < rows:
            v = np.concatenate([v, np.zeros(rows - v.size, v.dtype)])
        return v.reshape(-1, rows).T

    def down(w):
        w = np.asarray(w)
        return np.concatenate([w, np.zeros((P - w.shape[0], w.shape[1]), w.dtype)]) if w.shape[0] < P else w

    a = lambda n: np.asarray(i["L0_attn_" + n])
    e = lambda n: np.asarray(i["L0_ffn_" + n])
    m = lambda n: np.asarray(i["L1_attn_" + n])
    n_ = lambda n: np.asarray(i["L1_ffn_" + n])
    swap = np.arange(D) ^ 1
    heads = lambda w: np.repeat(w, DH, axis=-1)
    all_rows = lambda w: np.repeat(w, P, axis=1)
    wx = m("W_x")
    bcd = np.concatenate([wx[:, DR:], wx[:, :DR]], axis=1)
    w_a = dict(w_gate=a("gate_w"), w_clock=heads(a("clock_w")), w_p=a("p_w"), w_q=a("Wq"), w_qs=a("Wq")[:, swap],
               w_k=a("Wk"), w_ks=a("Wk")[:, swap], w_v=a("Wv"), w_o=a("out_w"), w_up=a("mlp_w1"),
               w_down=a("mlp_w2").reshape(FC, P, D).transpose(1, 0, 2).reshape(P, -1))
    w_c = dict(w_in=m("W_in"), w_x=bcd.reshape(DHV, P, -1).transpose(1, 0, 2).reshape(P, -1),
               w_out=m("W_out").reshape(DHV, P, D).transpose(1, 0, 2).reshape(P, -1),
               cn_w1=n_("cn_w1"), cn_w2=n_("cn_w2"), cn_w3=n_("cn_w3"), cn_w4=all_rows(n_("cn_w4")),
               gc_w1=n_("gc_w1"), gc_w2=n_("gc_w2"), gc_w3=all_rows(n_("gc_w3")))
    vec = dict(gate_b=a("gate_b"), clock_b=heads(a("clock_b")), p_b=a("p_b"), ln1_g=a("ln1_g"), ln1_b=a("ln1_b"),
               ln2_g=a("ln2_g"), ln2_b=a("ln2_b"), mlp_b1=a("mlp_b1"), conv_b=m("conv_b"), b_dt=m("b_dt"), skip=m("D"),
               cn_b1=n_("cn_b1"), cn_b2=n_("cn_b2"), cn_b3=n_("cn_b3"), cn_b4=np.repeat(n_("cn_b4"), P),
               gc_b1=n_("gc_b1"), gc_b2=n_("gc_b2"), gc_b3=np.repeat(n_("gc_b3"), P), arange=np.repeat(n_("adaptive_range"), P))
    return dict(
        x=a("x").reshape(N, D),
        consts=constants(),
        w_a=np.concatenate([w_a[n] for n, _ in W_A], axis=1),
        w_c=np.concatenate([down(w_c[n]) for n, _ in W_C], axis=1),
        vec=np.concatenate([column(vec[n]) for n, _ in VECS], axis=1),
        rows=np.repeat(np.stack([a("out_b"), a("mlp_b2")])[None], P, axis=0),
        cent=e("centroids").T,
        e_vec=np.concatenate([e("ln_g").T, e("ln_b").T], axis=1),
        w_1=e("w1").transpose(1, 0, 2).reshape(D, E * F),
        w_2=e("w2").reshape(E, FC, P, D).transpose(2, 0, 1, 3).reshape(P, E * F),
        b_1=e("b1"), b_2=e("b2"),
        a_log=m("A_log").reshape(DHV, P, NS).transpose(1, 0, 2),
        conv_w=np.repeat(m("conv_w")[:, 0, :].T[None], P, axis=0),
        w_dt=m("W_dt"),
    )


def kernel(**inputs):
    import concourse.bacc as _bacc
    from concourse import mybir as _mybir
    from concourse.bass_utils import run_bass_kernel_spmd as _run

    nc = _bacc.Bacc("TRN2", target_bir_lowering=False, num_devices=1)
    arrays, dram = {}, {}
    for name, a in laid_out(inputs).items():
        a = np.ascontiguousarray(a)
        arrays[f"in_{name}_dram"] = a
        dram[name] = nc.dram_tensor(f"in_{name}_dram", a.shape, _mybir.dt.from_np(a.dtype), kind="ExternalInput").ap()
    out = nc.dram_tensor("out_dram", (N, D), fp32, kind="ExternalOutput").ap()
    program(nc, dram, out)
    r = _run(nc, [arrays], core_ids=[0])
    return r.results[0]["out_dram"].reshape(SEQS, T, D)
```

```python
from contextlib import ExitStack, contextmanager

import numpy as np

import concourse.bass as bass
from concourse import mybir

fp32 = mybir.dt.float32
bf16 = mybir.dt.bfloat16
i32 = mybir.dt.int32
ALU = mybir.AluOpType
ACT = mybir.ActivationFunctionType
AX = mybir.AxisListType

P = 128
SEQS, T, D = 32, 256, 128
N = SEQS * T
TILES = N // P
STEP = 2 * T
PAIRS = SEQS // 2
TS = STEP // P
H, DH = 16, 8
HS = 4
F = 512
FC = F // P
E = 8
ETILES = TILES + E
DI, NS, DR, TAPS = 256, 16, 8, 4
DHV = DI // P
CYCLES = 3
EPS = 1e-5
LN2 = float(np.log(2.0))
QK_SHIFT = 20
EXP_LN = "natural_log_exp_and_others"
BIG = 1e30


@contextmanager
def cleared(nc, block, names):
    sems = {n: nc.alloc_semaphore(name=f"{block}_{n}") for n in names.split()}
    yield sems
    nc.clear_and_free_semaphores(list(sems.values()))
    nc.all_engine_barrier()


def semaphores(nc, ctx, block, names):
    return ctx.enter_context(cleared(nc, block, names))


def program(nc, dram, out):
    ctx = ExitStack()
    with ctx:
        def scratch(name, rows, cols):
            return nc.dram_tensor(name, [rows, cols], fp32, kind="Internal").ap()

        d = dict(
            xlb=scratch("xlb_dram", N, D),
            y1=scratch("y1_dram", N, D),
            xl2=scratch("xl2_dram", N, D),
            xn2=scratch("xn2_dram", N, D),
            sorted_in=scratch("sorted_in_dram", ETILES * P, D),
            sorted_out=scratch("sorted_out_dram", ETILES * P, D),
            y2=scratch("y2_dram", N, D),
            y3=scratch("y3_dram", N, D),
        )

        def keep(name, shape, dtype=fp32):
            return ctx.enter_context(nc.sbuf_tensor(name, shape, dtype))

        c = dict(
            vec=keep("vec", [P, dram["vec"].shape[1]]),
            rows=keep("rows", [P, 2, P]),
            cent=keep("cent", [P, E]),
            w_c=keep("w_c", [P, dram["w_c"].shape[1]]),
            w_dt=keep("w_dt", [DR, DI]),
            w_conv=keep("w_conv", [P, TAPS, DI]),
            neg_a=keep("neg_a", [P, DHV, NS]),
            consts=keep("consts", [P, dram["consts"].shape[1]]),
            ident_b=keep("ident_b", [P, P], bf16),
            mask_b=keep("mask_b", [P, 2, P], bf16),
            skip_diag=keep("skip_diag", [P, DHV, P]),
            sel=keep("sel", [P, 32, P], bf16),
            b1_split=keep("b1_split", [P, F], bf16),
            b2_split=keep("b2_split", [P, D], bf16),
            aff=keep("aff", [P, TILES, E]),
            alpha=keep("alpha", [P, TILES]),
            slot=keep("slot", [P, TILES], i32),
            tile_col=keep("tile_col", [1, 2, ETILES], i32),
        )
        layer0 = ctx.enter_context(ExitStack())
        for name, shape in (("w_a", [P, dram["w_a"].shape[1]]), ("w_1", [P, E * F]), ("w_2", [P, E * F])):
            c[name] = layer0.enter_context(nc.sbuf_tensor(name, shape, fp32))
        at = 0
        for name, width in CONSTS:
            c[name] = c["consts"][:, at:at + width]
            at += width
        at = 0
        for name, width in VECS:
            c[name] = c["vec"][:, at:at + width]
            at += width
        at = 0
        for name, width in W_A:
            c[name] = c["w_a"][:, at:at + width]
            at += width
        at = 0
        for name, width in W_C:
            c[name] = c["w_c"][:, at:at + width]
            at += width
        banks = [ctx.enter_context(nc.psum_tensor(f"bank{n}", [P, 512], fp32)) for n in range(8)]

        setup(nc, dram, d, c, banks)
        attention(nc, dram, d, c, banks)
        routing(nc, dram, d, c, banks)
        experts(nc, d, c, banks)
        layer0.close()
        scan_layer(nc, d, c, banks)
        rotation(nc, d, c, banks, out)


def split3(dve, chain, src, dst, hi, rest, mid, rows):
    chain(dve.tensor_copy(hi, src))
    chain(dve.tensor_tensor(rest, src, hi, ALU.subtract))
    chain(dve.tensor_copy(mid, rest))
    chain(dve.tensor_copy(dst[0:rows], hi))
    chain(dve.tensor_copy(dst[64:64 + rows], mid))
    chain(dve.tensor_tensor(rest, rest, mid, ALU.subtract))
    chain(dve.tensor_copy(dst[96:96 + rows], rest))


def setup(nc, dram, d, c, banks):
    with ExitStack() as ctx:
        s = semaphores(nc, ctx, "setup", "su_small su_cent su_expert su_scan su_zeroed su_zero su_bias_ps su_dve su_pool su_act")
        tmp = lambda name, shape, dtype=fp32: ctx.enter_context(nc.sbuf_tensor(name, shape, dtype))
        e_vec = tmp("e_vec", [P, 2 * E])
        lnb_eye = tmp("lnb_eye", [P, E, E])
        b_1 = tmp("b_1", [E, F])
        b_2 = tmp("b_2", [E, D])
        conv_rows = tmp("conv_rows", [P, TAPS, DI])
        hi = tmp("su_hi", [E, F], bf16)
        mid = tmp("su_mid", [E, F], bf16)
        rest = tmp("su_rest", [E, F])
        zeros = tmp("su_zeros", [P, 1024])
        block = ctx.enter_context(nc.Block())

        @block.sync
        def _(sp):
            sp.dma_start(c["consts"][:, :], dram["consts"]).then_inc(s["su_small"], 16)
            sp.dma_start(c["vec"][:, :], dram["vec"]).then_inc(s["su_small"], 16)
            sp.dma_start(c["rows"][:, :, :], dram["rows"]).then_inc(s["su_small"], 16)
            sp.dma_start(e_vec[:, :], dram["e_vec"]).then_inc(s["su_expert"], 16)
            sp.dma_start(b_1[:, :], dram["b_1"]).then_inc(s["su_expert"], 16)
            sp.dma_start(b_2[:, :], dram["b_2"]).then_inc(s["su_expert"], 16)
            sp.dma_start(c["w_1"][:, :], dram["w_1"]).then_inc(s["su_expert"], 16)
            sp.dma_start(c["neg_a"][:, :, :], dram["a_log"]).then_inc(s["su_scan"], 16)
            sp.dma_start(conv_rows[:, :, :], dram["conv_w"]).then_inc(s["su_scan"], 16)
            sp.dma_start(c["w_c"][:, :], dram["w_c"]).then_inc(s["su_scan"], 16)
            sp.dma_start(c["w_a"][:, :], dram["w_a"]).then_inc(s["su_small"], 16)
            sp.dma_start(c["cent"][:, :], dram["cent"]).then_inc(s["su_cent"], 16)
            sp.dma_start(c["w_2"][:, :], dram["w_2"]).then_inc(s["su_cent"], 16)
            sp.dma_start(c["w_dt"][:, :], dram["w_dt"]).then_inc(s["su_cent"], 16)
            sp.wait_ge(s["su_zero"], 1)
            rows = d["sorted_in"].rearrange("(n p q) d -> n p (q d)", p=P, q=8)
            for n in range(ETILES // 8):
                sp.dma_start(rows[n], zeros[:, :]).then_inc(s["su_zeroed"], 16)
            sp.wait_ge(s["su_small"], 64)
            sp.wait_ge(s["su_cent"], 48)
            sp.wait_ge(s["su_zeroed"], 16 * (ETILES // 8))

        @block.gpsimd
        def _(pool):
            pool.memset(zeros[:, :], 0.0).then_inc(s["su_zero"], 1)
            pool.wait_ge(s["su_scan"], 48)
            for tap in range(TAPS):
                pool.tensor_tensor(c["w_conv"][:, tap, :], conv_rows[:, tap, :], c["w_in"], ALU.mult).then_inc(s["su_pool"], 1)
            pool.wait_ge(s["su_pool"], TAPS)

        @block.scalar
        def _(act):
            act.wait_ge(s["su_dve"], 1)
            act.activation(c["neg_a"][:, :, :], c["neg_a"][:, :, :], ACT.Exp).then_inc(s["su_act"], 1)

        @block.tensor
        def _(pe):
            pe.wait_ge(s["su_dve"], 2)
            for e in range(E):
                last = pe.matmul(banks[0][0:E, :], lnb_eye[:, e, :], c["w_1"][:, e * F:(e + 1) * F],
                                 start=e == 0, stop=e == E - 1)
            last.then_inc(s["su_bias_ps"], 1)

        @block.vector
        def _(dve):
            count = [0]

            def chain(ins):
                count[0] += 1
                ins.then_inc(s["su_dve"], 1)
                dve.wait_ge(s["su_dve"], count[0])

            dve.wait_ge(s["su_scan"], 48)
            chain(dve.tensor_scalar(c["neg_a"][:, :, :], c["neg_a"][:, :, :], 69.0, None, ALU.min))
            dve.wait_ge(s["su_small"], 64)
            dve.wait_ge(s["su_expert"], 64)
            chain(dve.tensor_tensor(lnb_eye[:, :, :], e_vec[:, E:2 * E].unsqueeze(2).to_broadcast([P, E, E]),
                                    c["eye8"].rearrange("p (a b) -> p a b", a=E), ALU.mult))
            dve.wait_ge(s["su_act"], 1)
            chain(dve.tensor_scalar(c["neg_a"][:, :, :], c["neg_a"][:, :, :], -1.0, None, ALU.mult))
            chain(dve.tensor_copy(c["ident_b"][:, :], c["ident"]))
            chain(dve.tensor_copy(c["mask_b"][:, :, :], c["mask"].unsqueeze(1).to_broadcast([P, 2, P])))
            chain(dve.tensor_copy(c["sel"][:, :, :], c["sel_cols"].unsqueeze(2).to_broadcast([P, 32, P])))
            for hf in range(DHV):
                chain(dve.tensor_scalar(c["skip_diag"][:, hf, :], c["ident"], c["skip"][:, hf:hf + 1], None, ALU.mult))
            chain(dve.memset(c["b1_split"][:, :], 0.0))
            chain(dve.memset(c["b2_split"][:, :], 0.0))
            dve.wait_ge(s["su_bias_ps"], 1)
            chain(dve.tensor_tensor(b_1[:, :], banks[0][0:E, :], b_1[:, :], ALU.add))
            split3(dve, chain, b_1[:, :], c["b1_split"], hi[:, :], rest[:, :], mid[:, :], E)
            split3(dve, chain, b_2[:, :], c["b2_split"], hi[:, 0:D], rest[:, 0:D], mid[:, 0:D], E)
            for e in range(E):
                chain(dve.tensor_scalar(c["w_1"][:, e * F:(e + 1) * F], c["w_1"][:, e * F:(e + 1) * F],
                                        e_vec[:, e:e + 1], None, ALU.mult))




def attention(nc, dram, d, c, banks):
    with ExitStack() as ctx:
        s = semaphores(nc, ctx, "attn", """
            end_pe end_act end_dve end_pool
            x_loaded0 x_loaded1 xlb_loaded xm_loaded xlb_stored y_stored
            f_st f_mv f_vv f_ln f_rs f_xn f_xl f_xl2 f_xlb f_xt f_xt_sb f_gate f_clock f_pre0 f_pre1 f_abs f_exp f_log f_u1 f_log1 f_back f_lost f_soft f_sp1
            f_p f_max f_shift f_nb f_pe f_sp f_cum f_clip f_gcp f_lgcp f_px f_pcs f_lpcs
            f_q f_qs f_sq f_ra f_rb f_rq f_ssq f_mq f_lq f_zq f_zq2 f_fq f_qt
            f_k f_ks f_sk f_ka f_kb f_rk f_ssk f_mk f_lk f_zk f_fk f_k1 f_k2 f_km f_v f_vaug
            s_score s_exp s_av s_avs s_tr s_rec s_o
            m_ot m_ot_sb m_ow m_x1 m_x1b m_st m_mv m_ln m_rs m_h m_ht m_ht_sb m_up m_gelu m_dn
            m_x2 m_st2 m_mv2 m_ln2 m_rs2 m_yn m_y1 m_st3 m_mv3 m_vv3 m_ln3 m_rs3 m_xl2 m_xn2a m_xn2
            m_x2t m_x2t_sb m_aff m_aff_sb""")
        sb = lambda name, shape, dtype=fp32: ctx.enter_context(nc.sbuf_tensor(name, shape, dtype))
        x_in = [sb(f"x_in{n}", [P, TS, D]) for n in range(2)]
        stats = sb("f_stats", [P, TS, 6])
        mv = sb("f_mean_var", [P, TS, 2])
        vv = sb("f_vv", [P, 2, TS])
        rs = sb("f_rstd", [P, 2, TS])
        xn = sb("xn", [P, TS, D])
        xl = sb("xl", [P, TS, D])
        xt = sb("xt", [P, STEP])
        pre = sb("pre", [P, 2, STEP])
        mag = sb("mag", [P, 2, STEP])
        log = sb("log", [P, 2, STEP])
        one_up = sb("one_up", [P, STEP])
        cum = sb("cum", [P, STEP])
        lgcp = sb("lgcp", [P, STEP])
        pmax = sb("pmax", [P, 2])
        pneg = sb("pneg", [P, 2])
        pexp = sb("pexp", [P, STEP])
        pcs = sb("pcs", [P, STEP])
        square = sb("square", [P, STEP])
        lnorm = sb("lnorm", [P, STEP])
        rot = sb("rot", [P, STEP])
        rot_b = sb("rot_b", [P, STEP])
        factor = sb("factor", [P, STEP])
        q_t = [sb(f"q_t{n}", [P, STEP]) for n in range(2)]
        k_m = [sb(f"k_m{n}", [P, HS, STEP]) for n in range(2)]
        v_a = [sb(f"v_a{n}", [P, TS, H, 32]) for n in range(2)]
        es = [sb(f"es{n}", [P, 3 * P]) for n in range(8)]
        avs = sb("avs", [P, 512])
        rec = sb("rec", [P, 4, HS])
        o_tok = [sb(f"o_tok{n}", [P, TS, D]) for n in range(2)]
        x_m = sb("x_m", [P, TS, D])
        xlb_m = sb("xlb_m", [P, TS, D])
        o_t = sb("o_t", [P, STEP])
        x1 = sb("x1", [P, TS, D])
        x1b = sb("x1b", [P, TS, D])
        stats_m = sb("m_stats", [P, TS, 6])
        mv_m = sb("m_mean_var", [P, TS, 2])
        ln_m = sb("m_ln", [P, TS])
        rs_m = sb("m_rstd", [P, TS])
        vv_m = sb("m_vv", [P, 2, TS])
        rs3 = sb("m_rstd3", [P, 2, TS])
        h_tok = sb("h_tok", [P, TS, D])
        h_t = sb("h_t", [P, STEP])
        g = sb("g", [P, FC, STEP])
        x2 = sb("x2", [P, TS, D])
        y1 = sb("y1", [P, TS, D])
        xl2 = sb("xl2", [P, TS, D])
        xn2 = sb("xn2", [P, TS, D])
        hold = sb("a_hold", [P, 1])

        FA, FB, M, RING, AV = banks[0], banks[1], banks[2], banks[3:7], banks[7]
        x_loaded = [s["x_loaded0"], s["x_loaded1"]]
        seq = lambda t: t.rearrange("p (b t) -> p b t", b=2)
        tok = lambda t: t.rearrange("p (j d) -> p j d", j=TS)
        of_tile = lambda a: a.unsqueeze(2).to_broadcast([P, TS, D])
        cos = c["cos"].unsqueeze(1).to_broadcast([P, 2, T])
        sin = c["sin"].unsqueeze(1).to_broadcast([P, 2, T])
        rows = lambda ap, at: ap[bass.ds(at, STEP), :].rearrange("(j p) d -> p j d", p=P)
        w_down = c["w_down"].rearrange("p (c d) -> p c d", c=FC)

        def begin(eng, k):
            if isinstance(k, int) and k == 0:
                return
            for sem in (s["end_pe"], s["end_act"], s["end_dve"], s["end_pool"]):
                eng.wait_ge(sem, k)

        def stats_of(dve, src, st, out_mv, s_st, s_mv, r):
            for j in range(TS):
                last = dve.bn_stats(st[:, j, :], src[:, j, :])
            last.then_inc(s_st, 1)
            dve.wait_ge(s_st, r)
            dve.memset(hold[:, :], 0.0)
            for j in range(TS):
                last = dve.bn_aggr(out_mv[:, j, :], st[:, j, :])
            last.then_inc(s_mv, 1)
            dve.wait_ge(s_mv, r)

        def two_variances(dve, v, var, sem):
            dve.tensor_scalar(v[:, 0, :], var, EPS, None, ALU.add)
            dve.tensor_scalar(v[:, 1, :], var, 1.0 + EPS, EPS * EPS, ALU.mult, ALU.add).then_inc(sem, 1)

        x_loaded = [s["x_loaded0"], s["x_loaded1"]]

        def sp_step(sp, k, p, front, tail, load):
            now, rf, rm = (sp.snap(v) for v in (k * 1, k + 1, k - 1))
            here, back_two, ahead = (sp.snap(v) for v in (k * STEP, k * STEP - 2 * STEP, k * STEP + STEP))
            if load:
                sp.wait_ge(s["end_dve"], now)
                sp.wait_ge(s["end_pool"], now)
                sp.dma_start(x_in[1 - p][:, :, :], rows(dram["x"], ahead)).then_inc(x_loaded[1 - p], 16)
            if tail:
                sp.wait_ge(s["end_dve"], now)
                sp.wait_ge(s["end_pool"], now)
                sp.dma_start(xlb_m[:, :, :], rows(d["xlb"], back_two)).then_inc(s["xlb_loaded"], 16)
                sp.dma_start(x_m[:, :, :], rows(dram["x"], back_two)).then_inc(s["xm_loaded"], 16)
            if front:
                sp.wait_ge(s["f_xlb"], rf)
                sp.dma_start(rows(d["xlb"], here), xl[:, :, :]).then_inc(s["xlb_stored"], 16)
            if tail:
                sp.wait_ge(s["m_y1"], rm)
                sp.dma_start(rows(d["y1"], back_two), y1[:, :, :]).then_inc(s["y_stored"], 16)
                sp.wait_ge(s["m_xl2"], rm)
                sp.dma_start(rows(d["xl2"], back_two), xl2[:, :, :]).then_inc(s["y_stored"], 16)
                sp.wait_ge(s["m_xn2"], rm)
                sp.dma_start(rows(d["xn2"], back_two), xn2[:, :, :]).then_inc(s["y_stored"], 16)

        def pe_step(pe, k, half, p, front, scores, tail):
            begin(pe, k)
            rf, u, m = k + 1, k - 1, k - 2
            rm = k - 1

            def project(bank, weight, sem):
                pe.matmul(bank[:, :], weight, xt[:, :], start=True, stop=True).then_inc(sem, 1)

            def transposes(dst, src, sem):
                for j in range(TS):
                    last = pe.transpose(dst[:, j * P:(j + 1) * P], src[:, j, :], c["ident"])
                last.then_inc(sem, 1)

            def quad(n):
                b, v = n // HS, n % HS
                if n:
                    pe.wait_ge(s["s_exp"], u * 8 + n)
                for st in range(HS):
                    q, kk = q_t[1 - p][32 * st:32 * st + 32, b * T:b * T + T], k_m[1 - p][32 * st:32 * st + 32, v, b * T:b * T + T]
                    pe.matmul(RING[st][:, 0:T], kk[:, 0:P], q, start=True, stop=True, tile_position=(32 * st, 0))
                for st in range(HS):
                    q, kk = q_t[1 - p][32 * st:32 * st + 32, b * T:b * T + T], k_m[1 - p][32 * st:32 * st + 32, v, b * T:b * T + T]
                    pe.matmul(RING[st][:, T:T + P], kk[:, P:T], q[:, P:T], start=False, stop=True,
                              tile_position=(32 * st, 0), skip_group_check=True)
                for st in range(HS):
                    diag = RING[st][:, 0:4 * P].rearrange("p (a b) -> p a b", a=2)[:, :, 0:P]
                    pe.matmul(diag, c["ident_b"][:, :], c["mask_b"][:, :, :], start=False, stop=True,
                              skip_group_check=True).then_inc(s["s_score"], 1)

            def weigh(n):
                b, v, i = n // HS, n % HS, n // 2
                pe.wait_ge(s["s_exp"], u * 8 + n + 1)
                if n % 2 == 0 and i:
                    pe.wait_ge(s["s_o"], u * 8 + 2 * i)
                col = (v % 2) * T
                for st in range(HS):
                    e, dst = es[(n % 2) * HS + st], AV[32 * st:32 * st + 32, :]
                    pe.matmul(dst[:, col:col + T], v_a[1 - p][:, 2 * b, HS * st + v, :], e[:, 0:T],
                              start=True, stop=True, tile_position=(0, 32 * st))
                for st in range(HS):
                    e, dst = es[(n % 2) * HS + st], AV[32 * st:32 * st + 32, :]
                    last = pe.matmul(dst[:, col + P:col + T], v_a[1 - p][:, 2 * b + 1, HS * st + v, :], e[:, T:T + P],
                                     start=False, stop=True, tile_position=(0, 32 * st), skip_group_check=True)
                last.then_inc(s["s_av"], 1)

            def back(i):
                pe.wait_ge(s["s_avs"], u * 4 + i + 1)
                for j in range(4):
                    last = pe.transpose(AV[:, j * P:(j + 1) * P], avs[:, j * P:(j + 1) * P], c["ident"])
                last.then_inc(s["s_tr"], 1)

            def up(n):
                if n == 0:
                    pe.wait_ge(s["m_ht_sb"], rm)
                else:
                    pe.wait_ge(s["m_gelu"], 4 * m + n)
                pe.matmul(M[:, :], c["w_up"][:, n * P:(n + 1) * P], h_t[:, :], start=True, stop=True).then_inc(s["m_up"], 1)

            if tail:
                transposes(M, o_tok[p], s["m_ot"])
            if scores:
                quad(0)
            if front:
                pe.wait_ge(s["f_xn"], rf)
                transposes(FA, xn, s["f_xt"])
            if tail:
                pe.wait_ge(s["m_ot_sb"], rm)
                for j in range(TS):
                    last = pe.matmul(M[:, j * P:(j + 1) * P], o_t[:, j * P:(j + 1) * P], c["w_o"], start=True, stop=True)
                last.then_inc(s["m_ow"], 1)
            if front:
                pe.wait_ge(s["f_xt_sb"], rf)
                project(FB, c["w_gate"], s["f_gate"])
                project(FA, c["w_clock"], s["f_clock"])
            if scores:
                quad(1)
                weigh(0)
            if front:
                pe.wait_ge(s["f_pre0"], rf)
                project(FB, c["w_p"], s["f_p"])
            if tail:
                pe.wait_ge(s["m_h"], rm)
                transposes(M, h_tok, s["m_ht"])
            if front:
                pe.wait_ge(s["f_pre1"], rf)
                project(FA, c["w_q"], s["f_q"])
            if scores:
                quad(2)
            if tail:
                up(0)
            if scores:
                weigh(1)
            if tail:
                up(1)
            if front:
                pe.wait_ge(s["f_pe"], rf)
                project(FB, c["w_qs"], s["f_qs"])
            if tail:
                up(2)
            if front:
                pe.wait_ge(s["f_sq"], rf)
                pe.wait_ge(s["f_ra"], rf)
                pe.matmul(FA[:, :], c["ones_blk"], square[:, :], start=True, stop=True).then_inc(s["f_ssq"], 1)
            if tail:
                up(3)
                pe.wait_ge(s["m_gelu"], 4 * m + 4)
                for j in range(TS):
                    for n in range(FC):
                        last = pe.matmul(M[:, j * P:(j + 1) * P], g[:, n, j * P:(j + 1) * P], w_down[:, n, :],
                                         start=n == 0, stop=n == FC - 1)
                last.then_inc(s["m_dn"], 1)
            if scores:
                back(0)
                quad(3)
                weigh(2)
            if scores:
                quad(4)
                weigh(3)
            if front:
                pe.wait_ge(s["f_rb"], rf)
                project(FB, c["w_k"], s["f_k"])
                pe.wait_ge(s["f_mq"], rf)
                project(FA, c["w_ks"], s["f_ks"])
            if scores:
                back(1)
                quad(5)
                weigh(4)
            if front:
                pe.wait_ge(s["f_ka"], rf)
                pe.wait_ge(s["f_sk"], rf)
                pe.matmul(FB[:, :], c["ones_blk"], square[:, :], start=True, stop=True).then_inc(s["f_ssk"], 1)
            if scores:
                quad(6)
                weigh(5)
            if front:
                pe.wait_ge(s["f_kb"], rf)
                for j in range(TS):
                    last = pe.matmul(FA[:, j * P:(j + 1) * P], xt[:, j * P:(j + 1) * P], c["w_v"], start=True, stop=True)
                last.then_inc(s["f_v"], 1)
            if scores:
                back(2)
                quad(7)
                weigh(6)
            if tail:
                pe.wait_ge(s["m_xl2"], rm)
                transposes(M, xl2, s["m_x2t"])
            if scores:
                weigh(7)
            if tail:
                pe.wait_ge(s["m_x2t_sb"], rm)
                for j in range(TS):
                    last = pe.matmul(M[:, j * E:(j + 1) * E], o_t[:, j * P:(j + 1) * P], c["cent"][:, :], start=True, stop=True)
                last.then_inc(s["m_aff"], 1)
            if scores:
                back(3)
            pe.drain().then_inc(s["end_pe"], 1)

        def act_step(act, k, half, p, front, scores, tail):
            act.preload_act_table_set(EXP_LN)
            begin(act, k)
            rf, u, m = k + 1, k - 1, k - 2
            rm = k - 1

            def root(src, ln, dst, wait, s_ln, s_rs, r, bias=0.0):
                act.wait_ge(wait, r)
                act.activation(ln, src, ACT.Ln, bias=bias).then_inc(s_ln, 1)
                act.wait_ge(s_ln, r)
                act.activation(dst, ln, ACT.Exp, scale=-0.5).then_inc(s_rs, 1)

            def exps(n):
                for st in range(HS):
                    act.wait_ge(s["s_score"], u * 32 + HS * n + st + 1)
                    if n >= 2 and st == 0:
                        act.wait_ge(s["s_av"], u * 8 + n - 1)
                    last = act.activation(es[(n % 2) * HS + st][:, :], RING[st][:, 0:3 * P], ACT.Exp, scale=DH ** -0.5)
                last.then_inc(s["s_exp"], 1)

            def av_copy(i):
                act.wait_ge(s["s_av"], u * 8 + 2 * i + 2)
                if i:
                    act.wait_ge(s["s_tr"], u * 4 + i)
                act.activation(avs[:, :], AV[:, :], ACT.Copy).then_inc(s["s_avs"], 1)

            def squared(bank, wait, sem):
                act.wait_ge(wait, rf)
                act.activation(square[:, :], bank[:, :], ACT.Square).then_inc(sem, 1)

            if tail:
                act.wait_ge(s["m_ot"], rm)
                act.activation(o_t[:, :], M[:, :], ACT.Copy).then_inc(s["m_ot_sb"], 1)
            if front:
                root(vv[:, :, :], vv[:, :, :], rs[:, :, :], s["f_vv"], s["f_ln"], s["f_rs"], rf)
            if scores:
                exps(0)
            if front:
                act.wait_ge(s["f_xt"], rf)
                act.activation(xt[:, :], FA[:, :], ACT.Identity, scale=c["ln1_g"], bias=c["ln1_b"]).then_inc(s["f_xt_sb"], 1)
            if tail:
                root(mv_m[:, :, 1], ln_m[:, :], rs_m[:, :], s["m_mv"], s["m_ln"], s["m_rs"], rm, bias=EPS)
            if scores:
                exps(1)
            if front:
                act.wait_ge(s["f_pre1"], rf)
                act.activation(mag[:, :, :], pre[:, :, :], ACT.Abs).then_inc(s["f_abs"], 1)
                act.wait_ge(s["f_abs"], rf)
                act.activation(mag[:, :, :], mag[:, :, :], ACT.Exp, scale=-1.0).then_inc(s["f_exp"], 1)
                act.wait_ge(s["f_exp"], rf)
                act.activation(log[:, 0, :], mag[:, 0, :], ACT.Ln, bias=1.0).then_inc(s["f_log"], 1)
            if tail:
                act.wait_ge(s["m_ht"], rm)
                act.activation(h_t[:, :], M[:, :], ACT.Identity, scale=c["ln2_g"], bias=c["ln2_b"]).then_inc(s["m_ht_sb"], 1)
            if front:
                act.wait_ge(s["f_nb"], rf)
                for b in range(2):
                    last = act.activation(pexp[:, b * T:(b + 1) * T], FB[:, b * T:(b + 1) * T], ACT.Exp, bias=pneg[:, b:b + 1])
                last.then_inc(s["f_pe"], 1)
                squared(FA, s["f_q"], s["f_sq"])
            if tail:
                for n in range(FC):
                    act.wait_ge(s["m_up"], 4 * m + n + 1)
                    act.activation(g[:, n, :], M[:, :], ACT.Gelu, bias=c["mlp_b1"][:, n:n + 1]).then_inc(s["m_gelu"], 1)
                act.preload_act_table_set(EXP_LN)
            if scores:
                exps(2)
                av_copy(0)
            if front:
                act.activation(one_up[:, :], mag[:, 1, :], ACT.Identity, bias=1.0).then_inc(s["f_u1"], 1)
                act.wait_ge(s["f_u1"], rf)
                act.activation(log[:, 1, :], one_up[:, :], ACT.Ln).then_inc(s["f_log1"], 1)
                act.wait_ge(s["f_log1"], rf)
                act.activation(one_up[:, :], one_up[:, :], ACT.Identity, bias=-1.0).then_inc(s["f_back"], 1)
                act.wait_ge(s["f_clip"], rf)
                act.activation(lgcp[:, :], cum[:, :], ACT.Exp, scale=-1.0).then_inc(s["f_gcp"], 1)
                act.wait_ge(s["f_gcp"], rf)
                act.activation(lgcp[:, :], lgcp[:, :], ACT.Ln, bias=1e-8).then_inc(s["f_lgcp"], 1)
            if scores:
                exps(3)
            if tail:
                root(mv_m[:, :, 1], ln_m[:, :], rs_m[:, :], s["m_mv2"], s["m_ln2"], s["m_rs2"], rm, bias=EPS)
            if front:
                act.wait_ge(s["f_pcs"], rf)
                act.activation(pcs[:, :], pcs[:, :], ACT.Ln, bias=1e-8).then_inc(s["f_lpcs"], 1)
                act.wait_ge(s["f_mq"], rf)
                act.activation(lnorm[:, :], lnorm[:, :], ACT.Ln, scale=2.0 ** QK_SHIFT).then_inc(s["f_lq"], 1)
            if scores:
                exps(4)
                av_copy(1)
            if front:
                squared(FB, s["f_k"], s["f_sk"])
                act.wait_ge(s["f_zq2"], rf)
                act.activation(factor[:, :], factor[:, :], ACT.Exp, bias=0.5 * QK_SHIFT * LN2).then_inc(s["f_fq"], 1)
            if tail:
                root(vv_m[:, :, :], vv_m[:, :, :], rs3[:, :, :], s["m_vv3"], s["m_ln3"], s["m_rs3"], rm)
            if scores:
                exps(5)
            if front:
                act.wait_ge(s["f_mk"], rf)
                act.activation(lnorm[:, :], lnorm[:, :], ACT.Ln, scale=2.0 ** QK_SHIFT).then_inc(s["f_lk"], 1)
            if scores:
                exps(6)
                av_copy(2)
            if front:
                act.wait_ge(s["f_zk"], rf)
                act.activation(factor[:, :], factor[:, :], ACT.Exp, bias=0.5 * QK_SHIFT * LN2).then_inc(s["f_fk"], 1)
                act.wait_ge(s["f_v"], rf)
                act.activation(v_a[p][:, :, :, 0:DH], FA.rearrange("p (j h d) -> p j h d", j=TS, h=H), ACT.Copy).then_inc(s["f_vaug"], 1)
            if scores:
                exps(7)
            if tail:
                act.wait_ge(s["m_x2t"], rm)
                act.activation(o_t[:, :], M[:, :], ACT.Copy).then_inc(s["m_x2t_sb"], 1)
            if scores:
                av_copy(3)
            if front:
                act.wait_ge(s["f_k2"], rf)
                for v in range(HS):
                    last = act.activation(k_m[p][:, v, :], rot[:, :], ACT.Copy, scale=c["head_mask"][:, v:v + 1])
                last.then_inc(s["f_km"], 1)
            act.drain().then_inc(s["end_act"], 1)

        def dve_step(dve, k, half, p, front, scores, tail):
            begin(dve, k)
            rf, u, m = k + 1, k - 1, k - 2
            rm = k - 1

            def heads_out(i):
                b, vp = i // 2, i % 2
                tr = AV.rearrange("q (v r s w) -> q v r s w", v=2, r=2, s=HS)
                dve.wait_ge(s["s_tr"], u * 4 + i + 1)
                dve.reciprocal(rec[:, :, :], AV.rearrange("q (n s w) -> q n s w", n=4, s=HS)[:, :, :, DH]).then_inc(s["s_rec"], 1)
                dve.wait_ge(s["s_rec"], u * 4 + i + 1)
                for r in range(2):
                    o = o_tok[1 - p][:, 2 * b + r, :].rearrange("q (s v w) -> q v s w", s=HS, v=HS)[:, 2 * vp:2 * vp + 2, :, :]
                    w = rec.rearrange("q (v r) s -> q v r s", v=2)[:, :, r, :].unsqueeze(3).to_broadcast([P, 2, HS, DH])
                    dve.tensor_tensor(o, tr[:, :, r, :, 0:DH], w, ALU.mult).then_inc(s["s_o"], 1)

            def rotate(bank, bank_sw, s_a, wait_a, s_b, wait_b, s_r):
                dve.wait_ge(wait_a, rf)
                dve.tensor_tensor(seq(rot), seq(bank), cos, ALU.mult).then_inc(s_a, 1)
                dve.wait_ge(wait_b, rf)
                dve.tensor_tensor(seq(rot_b), seq(bank_sw), sin, ALU.mult).then_inc(s_b, 1)
                dve.wait_ge(s_b, rf)
                dve.tensor_tensor(rot[:, :], rot[:, :], rot_b[:, :], ALU.add).then_inc(s_r, 1)

            def centred(dst, src, mean_var, rstd, sem):
                for j in range(TS):
                    last = dve.tensor_scalar(dst[:, j, :], src[:, j, :], mean_var[:, j, 0:1], rstd[:, j:j + 1], ALU.subtract, ALU.mult)
                last.then_inc(sem, 1)

            if front:
                dve.wait_ge(x_loaded[p], 16 * half + 16)
                stats_of(dve, x_in[p], stats, mv, s["f_st"], s["f_mv"], rf)
                two_variances(dve, vv, mv[:, :, 1], s["f_vv"])
                dve.wait_ge(s["f_rs"], rf)
                centred(xn, x_in[p], mv, rs[:, 1, :], s["f_xn"])
            if tail:
                dve.wait_ge(s["xlb_loaded"], 16 * rm)
                dve.wait_ge(s["m_ow"], rm)
                dve.tensor_tensor(x1[:, :, :], tok(M), xlb_m[:, :, :], ALU.add).then_inc(s["m_x1"], 1)
                dve.wait_ge(s["m_x1"], rm)
                stats_of(dve, x1, stats_m, mv_m, s["m_st"], s["m_mv"], rm)
            if tail:
                dve.wait_ge(s["m_rs"], rm)
                centred(h_tok, x1, mv_m, rs_m, s["m_h"])
            if front:
                dve.wait_ge(s["f_gate"], rf)
                dve.tensor_scalar(pre[:, 0, :], FB[:, :], c["gate_b"], None, ALU.add).then_inc(s["f_pre0"], 1)
                dve.wait_ge(s["f_clock"], rf)
                dve.tensor_scalar(pre[:, 1, :], FA[:, :], c["clock_b"], None, ALU.add).then_inc(s["f_pre1"], 1)
                dve.wait_ge(s["f_p"], rf)
                dve.tensor_reduce(pmax[:, :], seq(FB), AX.X, ALU.max).then_inc(s["f_max"], 1)
                dve.wait_ge(s["f_max"], rf)
                dve.tensor_scalar(pmax[:, :], pmax[:, :], c["p_b"], None, ALU.add).then_inc(s["f_shift"], 1)
                dve.wait_ge(s["f_shift"], rf)
                dve.tensor_scalar(pneg[:, :], pmax[:, :], -1.0, c["p_b"], ALU.mult, ALU.add).then_inc(s["f_nb"], 1)
                dve.wait_ge(s["f_log"], rf)
                dve.scalar_tensor_tensor(pre[:, 0, :], pre[:, 0, :], 0.0, log[:, 0, :], ALU.max, ALU.add).then_inc(s["f_sp"], 1)
                dve.wait_ge(s["f_sp"], rf)
                dve.tensor_tensor_scan(cum[:, :], c["reset"], pre[:, 0, :], 0.0, ALU.mult, ALU.add).then_inc(s["f_cum"], 1)
                dve.wait_ge(s["f_cum"], rf)
                dve.tensor_scalar(cum[:, :], cum[:, :], -50.0, 60.0, ALU.max, ALU.min).then_inc(s["f_clip"], 1)
                rotate(FA, FB, s["f_ra"], s["f_sq"], s["f_rb"], s["f_qs"], s["f_rq"])
            if scores:
                heads_out(0)
            if tail:
                dve.wait_ge(s["m_x1b"], rm)
                dve.wait_ge(s["m_dn"], rm)
                dve.tensor_tensor(x2[:, :, :], tok(M), x1b[:, :, :], ALU.add).then_inc(s["m_x2"], 1)
                dve.wait_ge(s["m_x2"], rm)
                stats_of(dve, x2, stats_m, mv_m, s["m_st2"], s["m_mv2"], rm)
            if front:
                dve.wait_ge(s["f_soft"], rf)
                dve.scalar_tensor_tensor(pre[:, 1, :], pre[:, 1, :], 0.0, log[:, 1, :], ALU.max, ALU.add).then_inc(s["f_sp1"], 1)
                dve.wait_ge(s["f_sp1"], rf)
                dve.wait_ge(s["f_pe"], rf)
                dve.tensor_tensor(pexp[:, :], pexp[:, :], pre[:, 1, :], ALU.mult).then_inc(s["f_px"], 1)
                dve.wait_ge(s["f_px"], rf)
                dve.tensor_tensor_scan(pcs[:, :], c["reset"], pexp[:, :], 0.0, ALU.mult, ALU.add).then_inc(s["f_pcs"], 1)
                dve.wait_ge(s["f_ssq"], rf)
                dve.tensor_scalar(lnorm[:, :], FA[:, :], 1e-24, None, ALU.max).then_inc(s["f_mq"], 1)
            if tail:
                dve.wait_ge(s["m_rs2"], rm)
                centred(h_tok, x2, mv_m, rs_m, s["m_yn"])
                dve.wait_ge(s["m_yn"], rm)
                dve.wait_ge(s["xm_loaded"], 16 * rm)
                dve.wait_ge(s["y_stored"], 48 * m + 1)
                dve.tensor_tensor(y1[:, :, :], h_tok[:, :, :], x_m[:, :, :], ALU.add).then_inc(s["m_y1"], 1)
                dve.wait_ge(s["m_y1"], rm)
                stats_of(dve, y1, stats_m, mv_m, s["m_st3"], s["m_mv3"], rm)
                two_variances(dve, vv_m, mv_m[:, :, 1], s["m_vv3"])
            if scores:
                heads_out(1)
            if front:
                dve.wait_ge(s["f_lq"], rf)
                dve.scalar_tensor_tensor(factor[:, :], lnorm[:, :], -0.5, cum[:, :], ALU.mult, ALU.subtract).then_inc(s["f_zq"], 1)
                dve.wait_ge(s["f_lpcs"], rf)
                dve.wait_ge(s["f_zq"], rf)
                dve.tensor_tensor(factor[:, :], factor[:, :], pcs[:, :], ALU.subtract).then_inc(s["f_zq2"], 1)
                dve.wait_ge(s["f_fq"], rf)
                dve.tensor_tensor(q_t[p][:, :], rot[:, :], factor[:, :], ALU.mult).then_inc(s["f_qt"], 1)
                dve.wait_ge(s["f_qt"], rf)
                rotate(FB, FA, s["f_ka"], s["f_sk"], s["f_kb"], s["f_ks"], s["f_rk"])
            if tail:
                dve.wait_ge(s["m_rs3"], rm)
                centred(xl2, y1, mv_m, rs3[:, 0, :], s["m_xl2"])
            if front:
                dve.wait_ge(s["f_ssk"], rf)
                dve.tensor_scalar(lnorm[:, :], FB[:, :], 1e-24, None, ALU.max).then_inc(s["f_mk"], 1)
                dve.wait_ge(s["f_lk"], rf)
                dve.wait_ge(s["f_lgcp"], rf)
                dve.scalar_tensor_tensor(factor[:, :], lnorm[:, :], -0.5, lgcp[:, :], ALU.mult, ALU.subtract).then_inc(s["f_zk"], 1)
            if scores:
                heads_out(2)
            if front:
                dve.wait_ge(s["f_fk"], rf)
                dve.tensor_tensor(rot[:, :], rot[:, :], factor[:, :], ALU.mult).then_inc(s["f_k1"], 1)
                dve.wait_ge(s["f_k1"], rf)
                dve.tensor_tensor(rot[:, :], rot[:, :], pexp[:, :], ALU.mult).then_inc(s["f_k2"], 1)
            if tail:
                dve.wait_ge(s["m_aff"], rm)
                dve.tensor_scalar(c["aff"][:, bass.ds(m * TS, TS), :], M[:, 0:TS * E].rearrange("p (j e) -> p j e", j=TS),
                                  1.0, None, ALU.mult).then_inc(s["m_aff_sb"], 1)
            if scores:
                heads_out(3)
            dve.drain().then_inc(s["end_dve"], 1)

        def pool_step(pool, k, half, p, front, scores, tail):
            begin(pool, k)
            rf, m, rm = k + 1, k - 2, k - 1
            if front:
                pool.wait_ge(s["f_rs"], rf)
                pool.wait_ge(s["xlb_stored"], 16 * k)
                pool.tensor_tensor(xl[:, :, :], x_in[p][:, :, :], of_tile(mv[:, :, 0]), ALU.subtract).then_inc(s["f_xl"], 1)
                pool.wait_ge(s["f_xl"], rf)
                pool.tensor_tensor(xl[:, :, :], xl[:, :, :], of_tile(rs[:, 0, :]), ALU.mult).then_inc(s["f_xl2"], 1)
                pool.wait_ge(s["f_xl2"], rf)
                pool.tensor_tensor(xl[:, :, :], xl[:, :, :], c["rows"][:, 0:1, :].to_broadcast([P, TS, D]), ALU.add).then_inc(s["f_xlb"], 1)
            else:
                pool.wait_ge(s["xlb_stored"], 16 * PAIRS)
            if tail:
                pool.wait_ge(s["m_x1"], rm)
                pool.tensor_tensor(x1b[:, :, :], x1[:, :, :], c["rows"][:, 1:2, :].to_broadcast([P, TS, D]), ALU.add).then_inc(s["m_x1b"], 1)
            if front:
                pool.wait_ge(s["f_back"], rf)
                pool.tensor_tensor(mag[:, 1, :], mag[:, 1, :], one_up[:, :], ALU.subtract).then_inc(s["f_lost"], 1)
                pool.wait_ge(s["f_lost"], rf)
                pool.tensor_tensor(log[:, 1, :], log[:, 1, :], mag[:, 1, :], ALU.add).then_inc(s["f_soft"], 1)
            if tail:
                pool.wait_ge(s["m_rs3"], rm)
                pool.wait_ge(s["y_stored"], 48 * m + 1)
                pool.tensor_tensor(xn2[:, :, :], y1[:, :, :], of_tile(mv_m[:, :, 0]), ALU.subtract).then_inc(s["m_xn2a"], 1)
                pool.wait_ge(s["m_xn2a"], rm)
                pool.tensor_tensor(xn2[:, :, :], xn2[:, :, :], of_tile(rs3[:, 1, :]), ALU.mult).then_inc(s["m_xn2"], 1)
            pool.drain().then_inc(s["end_pool"], 1)

        def steps(eng, step):
            step(eng, 0, 0, 0, True, False, False)
            step(eng, 1, 0, 1, True, True, False)
            with eng.Fori(0, (PAIRS - 2) // 2) as n:
                for p in range(2):
                    step(eng, n * 2 + (2 + p), n + 1, p, True, True, True)
            step(eng, PAIRS, PAIRS // 2, 0, False, True, True)
            step(eng, PAIRS + 1, PAIRS // 2, 1, False, False, True)

        block = ctx.enter_context(nc.Block())

        @block.sync
        def _(sp):
            sp.dma_start(x_in[0][:, :, :], rows(dram["x"], 0)).then_inc(s["x_loaded0"], 16)
            sp_step(sp, 0, 0, True, False, True)
            sp_step(sp, 1, 1, True, False, True)
            with sp.Fori(0, (PAIRS - 2) // 2 - 1) as n:
                for p in range(2):
                    sp_step(sp, n * 2 + (2 + p), p, True, True, True)
            sp_step(sp, PAIRS - 2, 0, True, True, True)
            sp_step(sp, PAIRS - 1, 1, True, True, False)
            sp_step(sp, PAIRS, 0, False, True, False)
            sp_step(sp, PAIRS + 1, 1, False, True, False)
            sp.wait_ge(s["y_stored"], 48 * PAIRS + 1)
            sp.wait_ge(s["xlb_stored"], 16 * PAIRS)

        @block.tensor
        def _(pe):
            steps(pe, pe_step)

        @block.scalar
        def _(act):
            steps(act, act_step)

        @block.vector
        def _(dve):
            dve.sem_inc(s["y_stored"], 1)
            for n in range(2):
                dve.memset(v_a[n][:, :, :, DH:DH + 1], 1.0)
                dve.memset(v_a[n][:, :, :, DH + 1:], 0.0)
            steps(dve, dve_step)

        @block.gpsimd
        def _(pool):
            steps(pool, pool_step)




def routing(nc, dram, d, c, banks):
    with ExitStack() as ctx:
        s = semaphores(nc, ctx, "route", """r_dve r_hot r_rank r_total r_exp r_slot r_passed r_idx
            r_loaded0 r_loaded1 r_sent0 r_sent1""")
        sb = lambda name, shape, dtype=fp32: ctx.enter_context(nc.sbuf_tensor(name, shape, dtype))
        best = sb("best", [P, TILES])
        first = sb("first", [P, TILES])
        hot = sb("hot", [P, TILES, E])
        order = sb("order", [P, E])
        total = sb("total", [P, E, TILES])
        before = sb("before", [P, E, TILES])
        same = sb("same", [P, E, TILES])
        count = sb("count", [P, E])
        count_i = sb("count_i", [P, E], i32)
        end = sb("end", [P, E])
        pos = sb("pos", [P, TILES, E])
        slot_f = sb("slot_f", [P, TILES])
        past = sb("past", [1, ETILES, E - 1])
        of = sb("of", [1, ETILES])
        neg = sb("neg", [P, TILES])
        stage = [sb(f"stage{n}", [P, TS, D]) for n in range(2)]
        idx = [sb(f"idx{n}", [P, TS], i32) for n in range(2)]
        loaded, sent = [s["r_loaded0"], s["r_loaded1"]], [s["r_sent0"], s["r_sent1"]]
        by_tile = lambda a: a.rearrange("p e t -> p t e")
        each = lambda a: a.unsqueeze(2).to_broadcast([P, TILES, E])
        block = ctx.enter_context(nc.Block())

        @block.vector
        def _(dve):
            n = [0]

            def chain(ins):
                n[0] += 1
                ins.then_inc(s["r_dve"], 1)
                dve.wait_ge(s["r_dve"], n[0])

            chain(dve.tensor_reduce(best[:, :], c["aff"][:, :, :], AX.X, ALU.max))
            chain(dve.tensor_scalar(order[:, :], c["tile_no"][:, 0:E], -1.0, float(E), ALU.mult, ALU.add))
            chain(dve.tensor_tensor(hot[:, :, :], c["aff"][:, :, :], each(best[:, :]), ALU.is_ge))
            chain(dve.tensor_tensor(hot[:, :, :], hot[:, :, :], order[:, :].unsqueeze(1).to_broadcast([P, TILES, E]), ALU.mult))
            chain(dve.tensor_reduce(first[:, :], hot[:, :, :], AX.X, ALU.max))
            dve.tensor_tensor(hot[:, :, :], hot[:, :, :], each(first[:, :]), ALU.is_equal).then_inc(s["r_hot"], 1)
            chain(dve.tensor_scalar(neg[:, :], best[:, :], -1.0, 87.0, ALU.mult, ALU.min))
            dve.wait_ge(s["r_exp"], 1)
            chain(dve.tensor_scalar(neg[:, :], neg[:, :], 1.0, None, ALU.add))
            chain(dve.reciprocal(c["alpha"][:, :], neg[:, :]))
            chain(dve.memset(same[:, :, :], 1.0))
            chain(dve.memset(same[:, :, 0:1], 0.0))
            dve.wait_ge(s["r_total"], 1)
            chain(dve.tensor_copy(total[:, :, :], banks[1].rearrange("p (t e) -> p e t", e=E)))
            chain(dve.tensor_tensor_scan(before.rearrange("p e t -> p (e t)"), same.rearrange("p e t -> p (e t)"),
                                         total.rearrange("p e t -> p (e t)"), 0.0, ALU.mult, ALU.add))
            chain(dve.tensor_scalar(count[:, :], before[:, :, TILES - 1], float(P - 1), None, ALU.add))
            chain(dve.tensor_copy(count_i[:, :], count[:, :]))
            chain(dve.tensor_scalar(count_i[:, :], count_i[:, :], 7, None, ALU.logical_shift_right))
            chain(dve.tensor_copy(count[:, :], count_i[:, :]))
            chain(dve.tensor_tensor_scan(end[:, :], c["ones"][:, 0:E], count[:, :], 0.0, ALU.mult, ALU.add))
            chain(dve.tensor_tensor(count[:, :], end[:, :], count[:, :], ALU.subtract))
            chain(dve.tensor_tensor(before[:, :, :], before[:, :, :], total[:, :, :], ALU.subtract))
            chain(dve.tensor_scalar(count[:, :], count[:, :], float(P), None, ALU.mult))
            chain(dve.tensor_tensor(before[:, :, :], before[:, :, :], count[:, :].unsqueeze(2).to_broadcast([P, E, TILES]), ALU.add))
            chain(dve.tensor_tensor(pos[:, :, :], banks[0].rearrange("p (t e) -> p t e", e=E), by_tile(before), ALU.add))
            chain(dve.tensor_tensor(pos[:, :, :], pos[:, :, :], hot[:, :, :], ALU.mult))
            chain(dve.tensor_reduce(slot_f[:, :], pos[:, :, :], AX.X, ALU.add))
            dve.tensor_copy(c["slot"][:, :], slot_f[:, :]).then_inc(s["r_slot"], 1)
            chain(dve.tensor_tensor(past[:, :, :], c["tile_no"][0:1, :].unsqueeze(2).to_broadcast([1, ETILES, E - 1]),
                                    end[0:1, 0:E - 1].unsqueeze(1).to_broadcast([1, ETILES, E - 1]), ALU.is_ge))
            chain(dve.tensor_reduce(of[:, :], past[:, :, :], AX.X, ALU.add))
            dve.tensor_scalar(c["tile_col"][:, 0, :], of[:, :], float(F), None, ALU.mult)
            chain(dve.tensor_copy(c["tile_col"][:, 1, :], of[:, :]))

        @block.scalar
        def _(act):
            act.preload_act_table_set(EXP_LN)
            act.wait_ge(s["r_dve"], 6)
            act.activation(neg[:, :], neg[:, :], ACT.Exp).then_inc(s["r_exp"], 1)

        @block.tensor
        def _(pe):
            pe.wait_ge(s["r_hot"], 1)
            pe.matmul(banks[0][:, :], c["strict"], hot.rearrange("p t e -> p (t e)"), start=True, stop=True)
            pe.matmul(banks[1][:, :], c["ones"], hot.rearrange("p t e -> p (t e)"), start=True, stop=True).then_inc(s["r_total"], 1)

        @block.sync
        def _(sp):
            def load(at, h):
                sp.dma_start(stage[h][:, :, :], d["xn2"][bass.ds(at, STEP), :].rearrange("(j p) d -> p j d", p=P)).then_inc(loaded[h], 16)

            for h in range(2):
                load(h * STEP, h)
            with sp.Fori(0, PAIRS // 2 - 1) as n:
                for h in range(2):
                    at, free = sp.snap(n * (2 * STEP) + (2 + h) * STEP), sp.snap(n * (16 * TS) + 16 * TS)
                    sp.wait_ge(sent[h], free)
                    load(at, h)

        @block.gpsimd
        def _(pool):
            pool.wait_ge(s["r_slot"], 1)
            with pool.Fori(0, PAIRS // 2) as n:
                for h in range(2):
                    pool.wait_ge(loaded[h], 16 * n + 16)
                    pool.sem_inc(s["r_passed"], 1)
                    pool.tensor_copy(idx[h][:, :], c["slot"][:, bass.ds(n * (2 * TS) + h * TS, TS)]).then_inc(s["r_idx"], 1)
                    pool.wait_ge(s["r_idx"], 2 * n + (h + 1))
                    pool.sem_inc(s["r_passed"], 1)
                    for j in range(TS):
                        pool.indirect_dma_start(out=d["sorted_in"], out_offset=bass.IndirectOffsetOnAxis(ap=idx[h][:, j:j + 1], axis=0),
                                                in_=stage[h][:, j, :], in_offset=None).then_inc(sent[h], 16)
            for h in range(2):
                pool.wait_ge(sent[h], 16 * TS * (PAIRS // 2))




def experts(nc, d, c, banks):
    SLOTS = 4
    PASSES = ETILES // SLOTS
    with ExitStack() as ctx:
        s = semaphores(nc, ctx, "expert", """loaded0 loaded1 loaded2 loaded3 stored0 stored1 stored2 stored3
            x_t xt_sb weights hidden relu_sb result result_sb passed w_passed""")
        sb = lambda name, shape, dtype=fp32: [ctx.enter_context(nc.sbuf_tensor(f"{name}{h}", shape, dtype)) for h in range(SLOTS)]
        xs, xt, hid, ys = sb("xs", [P, D]), sb("xst", [P, P]), sb("hid", [P, F]), sb("ys", [P, D])
        w1 = sb("w1_tile", [P, F])
        loaded, stored = [s["loaded0"], s["loaded1"], s["loaded2"], s["loaded3"]], [s["stored0"], s["stored1"], s["stored2"], s["stored3"]]
        XB, HB, YB = banks[0:2], banks[2:4], banks[4:6]
        block = ctx.enter_context(nc.Block())

        @block.sync
        def _(sp):
            def load(at, j):
                sp.dma_start(xs[j][:, :], d["sorted_in"][bass.ds(at, P), :]).then_inc(loaded[j], 16)

            def store(at, j):
                sp.dma_start(d["sorted_out"][bass.ds(at, P), :], ys[j][:, :]).then_inc(stored[j], 16)

            for j in range(SLOTS):
                load(j * P, j)
            with sp.Fori(0, PASSES - 1) as n:
                for j in range(SLOTS):
                    done, ahead, here = (sp.snap(v) for v in (n * SLOTS + (j + 1), n * (SLOTS * P) + (SLOTS + j) * P, n * (SLOTS * P) + j * P))
                    sp.wait_ge(s["x_t"], done)
                    load(ahead, j)
                    sp.wait_ge(s["result_sb"], done)
                    store(here, j)
            for j in range(SLOTS):
                t = ETILES - SLOTS + j
                sp.wait_ge(s["result_sb"], t + 1)
                store(t * P, j)
            for j in range(SLOTS):
                sp.wait_ge(stored[j], 16 * PASSES)

        @block.tensor
        def _(pe):
            def expert_of(t):
                col = pe.value_load(c["tile_col"][0:1, 0, bass.ds(t, 1)], min_val=0, max_val=(E - 1) * F)
                ex = pe.value_load(c["tile_col"][0:1, 1, bass.ds(t, 1)], min_val=0, max_val=E - 1)
                return col, c["sel"][:, bass.ds(ex, 1), :].rearrange("k a p -> k (a p)")

            def turned(n, j, first):
                t = n * SLOTS + j
                pe.wait_ge(loaded[j % SLOTS], 16 * n + 16 * (1 + j // SLOTS))
                if not (first and j < 2):
                    pe.wait_ge(s["xt_sb"], t - 1)
                pe.transpose(XB[j % 2][:, 0:P], xs[j % SLOTS][:, :], c["ident"]).then_inc(s["x_t"], 1)

            def up(n, j, first, col, row):
                t, bank = n * SLOTS + j, HB[j % 2]
                if not (first and j < 2):
                    pe.wait_ge(s["relu_sb"], t - 1)
                pe.sem_inc(s["passed"], 1)
                for f in range(FC):
                    pe.matmul(bank[:, f * P:(f + 1) * P], c["b1_split"][:, f * P:(f + 1) * P], row, start=f == 0, stop=False, skip_group_check=True)
                pe.wait_ge(s["xt_sb"], t + 1)
                pe.wait_ge(s["weights"], t + 1)
                for f in range(FC):
                    last = pe.matmul(bank[:, f * P:(f + 1) * P], w1[j][:, f * P:(f + 1) * P], xt[j][:, :],
                                     start=False, stop=True, skip_group_check=True)
                last.then_inc(s["hidden"], 1)

            def down(n, j, first, col, row):
                t, bank = n * SLOTS + j, YB[j % 2]
                if not (first and j < 2):
                    pe.wait_ge(s["result_sb"], t - 1)
                pe.sem_inc(s["passed"], 1)
                pe.matmul(bank[:, 0:D], row, c["b2_split"][:, :], start=True, stop=False)
                pe.wait_ge(s["relu_sb"], t + 1)
                for f in range(FC):
                    last = pe.matmul(bank[:, 0:D], hid[j][:, f * P:(f + 1) * P], c["w_2"][:, bass.ds(col + f * P, P)],
                                     start=False, stop=f == FC - 1)
                last.then_inc(s["result"], 1)

            def one_pass(n, before, first, last):
                behind = None
                if not first:
                    behind = (before, SLOTS - 1, expert_of(before * SLOTS + (SLOTS - 1)))
                for j in range(SLOTS):
                    weights = expert_of(n * SLOTS + j)
                    if not (last and j + 2 >= SLOTS):
                        turned(n, j + 2, first)
                    up(n, j, first, *weights)
                    if behind:
                        down(behind[0], behind[1], first and behind[1] < 2, *behind[2])
                    behind = (n, j, weights)
                if last:
                    down(behind[0], behind[1], False, *behind[2])

            turned(0, 0, True)
            turned(0, 1, True)
            one_pass(0, None, True, False)
            with pe.Fori(0, PASSES - 2) as n:
                one_pass(n + 1, n, False, False)
            one_pass(PASSES - 1, PASSES - 2, False, True)

        @block.gpsimd
        def _(pool):
            def copy(n, j, first):
                t = n * SLOTS + j
                col = pool.value_load(c["tile_col"][0:1, 0, bass.ds(t, 1)], min_val=0, max_val=(E - 1) * F)
                if not first:
                    pool.wait_ge(s["hidden"], t - (SLOTS - 1))
                    pool.sem_inc(s["w_passed"], 1)
                pool.tensor_copy(w1[j][:, :], c["w_1"][:, bass.ds(col, F)]).then_inc(s["weights"], 1)

            for j in range(SLOTS):
                copy(0, j, True)
            with pool.Fori(0, PASSES - 1) as n:
                for j in range(SLOTS):
                    copy(n + 1, j, False)

        @block.scalar
        def _(act):
            def relu(n, j, first):
                t = n * SLOTS + j
                if not first:
                    act.wait_ge(s["result"], t - (SLOTS - 1))
                act.wait_ge(s["hidden"], t + 1)
                act.activation(hid[j][:, :], HB[j % 2][:, :], ACT.Relu).then_inc(s["relu_sb"], 1)

            for j in range(SLOTS):
                relu(0, j, True)
            with act.Fori(0, PASSES - 1) as n:
                for j in range(SLOTS):
                    relu(n + 1, j, False)

        @block.vector
        def _(dve):
            def features(n, j, first):
                t = n * SLOTS + j
                if not (first and j < SLOTS):
                    dve.wait_ge(s["hidden"], t - (SLOTS - 1))
                dve.wait_ge(s["x_t"], t + 1)
                dve.tensor_copy(xt[j % SLOTS][:, :], XB[j % 2][:, 0:P]).then_inc(s["xt_sb"], 1)

            def result(n, j, first):
                t = n * SLOTS + j
                if not first:
                    dve.wait_ge(stored[j], 16 * n)
                dve.wait_ge(s["result"], t + 1)
                dve.tensor_copy(ys[j][:, :], YB[j % 2][:, 0:D]).then_inc(s["result_sb"], 1)

            def one_pass(n, first, last):
                for j in range(SLOTS):
                    if not (last and j + 2 >= SLOTS):
                        features(n, j + 2, first)
                    result(n, j, first)

            features(0, 0, True)
            features(0, 1, True)
            one_pass(0, True, False)
            with dve.Fori(0, PASSES - 2) as n:
                one_pass(n + 1, False, False)
            one_pass(PASSES - 1, False, True)


def scan_layer(nc, d, c, banks):
    with ExitStack() as ctx:
        s = semaphores(nc, ctx, "scan", """
            end_dve
            g_loaded0 g_loaded1 g_gathered0 g_gathered1 g_passed g_idx
            g_al g_o g_st g_mv g_ln g_rs g_on g_y2 g_y2_stored g_st2 g_mv2 g_ln2 g_rs2 g_xn g_t g_xt
            f_conv f_silu f_ssm f_dtr f_split f_dt f_pre f_abs f_exp f_u1 f_log f_back f_lost f_soft f_delta f_u
            n_b n_c n_c_sb n_da n_dbx n_h n_hc n_y n_yt
            w_y2_loaded w_proj w_st w_mv w_ln w_rs w_on w_y3 w_stored""")
        sb = lambda name, shape, dtype=fp32: ctx.enter_context(nc.sbuf_tensor(name, shape, dtype))
        two = lambda name, shape, dtype=fp32: [sb(f"{name}{n}", shape, dtype) for n in range(2)]
        y1 = two("g_y1", [P, TS, D])
        xl2 = two("g_xl2", [P, TS, D])
        ffn = two("g_ffn", [P, TS, D])
        idx = two("g_idx", [P, TS], i32)
        al = sb("g_al", [P, TS])
        o = sb("g_o", [P, TS, D])
        y2 = sb("g_y2", [P, TS, D])
        xn = sb("g_xn", [P, TS, D])
        stats_g = sb("g_stats", [P, TS, 6])
        mv_g = sb("g_mean_var", [P, TS, 2])
        ln_g = sb("g_ln", [P, TS])
        rs_g = sb("g_rstd", [P, TS])
        xpad = two("xpad", [P, 2, T + TAPS - 1])
        dtr = sb("dtr", [DR, STEP])
        rest = sb("bc_rest", [P, STEP])
        pre = sb("f_pre", [P, DHV, STEP])
        mag = sb("f_mag", [P, DHV, STEP])
        one_up = sb("f_one_up", [P, DHV, STEP])
        log = sb("f_log", [P, DHV, STEP])
        xv = two("xv", [P, DHV, STEP])
        bcs = two("bcs", [P, STEP], bf16)
        delta = two("delta", [P, DHV, STEP])
        u_in = two("u_in", [P, DHV, STEP])
        RING = 8
        decay = [sb(f"decay{n}", [P, DHV, 2, T]) for n in range(RING)]
        dbx = two("dbx", [P, DHV, STEP])
        h = [sb(f"h{n}", [P, DHV, STEP]) for n in range(4)]
        crep = [sb(f"crep{n}", [P, STEP]) for n in range(4)]
        hc = two("hc", [P, DHV, STEP])
        yt = sb("yt", [P, DHV, STEP])
        y2r = sb("w_y2", [P, TS, D])
        on = sb("w_on", [P, TS, D])
        y3 = sb("w_y3", [P, TS, D])
        stats_w = sb("w_stats", [P, TS, 6])
        mv_w = sb("w_mean_var", [P, TS, 2])
        ln_w = sb("w_ln", [P, TS])
        rs_w = sb("w_rstd", [P, TS])
        hold = sb("c_hold", [P, 1])

        BB, CB, YB, GA, GB, W = banks[0:2], banks[2], banks[3:5], banks[5], banks[6], banks[7]
        loaded, gathered = [s["g_loaded0"], s["g_loaded1"]], [s["g_gathered0"], s["g_gathered1"]]
        tok = lambda t: t.rearrange("p (j d) -> p j d", j=TS)
        seq = lambda t: t.rearrange("p (b t) -> p b t", b=2)
        rows = lambda ap, at: ap[bass.ds(at, STEP), :].rearrange("(j p) d -> p j d", p=P)
        w_x = c["w_x"].rearrange("p (f m) -> p f m", f=DHV)
        w_out = c["w_out"].rearrange("p (f m) -> p f m", f=DHV)

        def sp_step(sp, k, half, p, gather, front, states, output, load):
            now, rg, rm = (sp.snap(v) for v in (k * 1, k + 1, k - 2 if output else k * 1))
            here, back, ahead = (sp.snap(v) for v in (k * STEP, k * STEP - 3 * STEP if output else k * STEP, k * STEP + STEP))
            if load:
                if not (isinstance(k, int) and k == 0):
                    sp.wait_ge(s["end_dve"], now)
                sp.dma_start(y1[1 - p][:, :, :], rows(d["y1"], ahead)).then_inc(loaded[1 - p], 16)
                sp.dma_start(xl2[1 - p][:, :, :], rows(d["xl2"], ahead)).then_inc(loaded[1 - p], 16)
            if output:
                sp.wait_ge(s["end_dve"], now)
                if not gather:
                    sp.wait_ge(s["g_y2_stored"], 16 * PAIRS)
                sp.dma_start(y2r[:, :, :], rows(d["y2"], back)).then_inc(s["w_y2_loaded"], 16)
            if gather:
                sp.wait_ge(s["g_y2"], rg)
                sp.dma_start(rows(d["y2"], here), y2[:, :, :]).then_inc(s["g_y2_stored"], 16)
            if output:
                sp.wait_ge(s["w_y3"], rm)
                sp.dma_start(rows(d["y3"], back), y3[:, :, :]).then_inc(s["w_stored"], 16)

        def of_step(n, front, states, output):
            return output if n < 0 else front if n >= NS else states

        def since(eng, sem, count):
            if not isinstance(count, int) or count > 0:
                eng.wait_ge(sem, count)

        def pe_step(pe, k, half, p, gather, front, states, output):
            rg, u, rm = k + 1, k - 2, k - 2
            first = u * NS

            def b_row(n):
                if not of_step(n, front, states, output):
                    return
                if n == NS:
                    pe.wait_ge(s["f_split"], 4 * k)
                since(pe, s["n_dbx"], first + n - 1)
                pe.matmul(BB[n % 2][:, :], c["sel"][:, n % NS, :], bcs[p if n < NS else 1 - p][:, :], start=True, stop=True).then_inc(s["n_b"], 1)

            def c_row(n):
                if not of_step(n, front, states, output):
                    return
                since(pe, s["n_c_sb"], first + n)
                pe.matmul(CB[:, :], c["sel"][:, NS + n % NS, :], bcs[p if n < NS else 1 - p][:, :], start=True, stop=True).then_inc(s["n_c"], 1)

            def y_sum(n):
                if not of_step(n, front, states, output):
                    return
                pe.wait_ge(s["n_hc"], first + n + 1)
                for hf in range(DHV):
                    last = pe.matmul(YB[hf][:, :], c["ident"], hc[n % 2][:, hf, :], start=False, stop=n == -1)
                last.then_inc(s["n_y"], 1)

            def conv(hf, taps):
                if not front:
                    return
                for tap in taps:
                    last = pe.matmul(seq((GA, GB)[hf]), c["w_conv"][:, tap, hf * P:(hf + 1) * P],
                                     xpad[1 - p][:, :, tap:tap + T], start=tap == 0, stop=tap == TAPS - 1)
                if tap == TAPS - 1:
                    last.then_inc(s["f_conv"], 1)

            if front:
                pe.wait_ge(s["g_xt"], k)
            conv(0, (0, 1))
            for n in range(NS):
                if n == 2 and states:
                    since(pe, s["n_yt"], u)
                    for hf in range(DHV):
                        pe.matmul(YB[hf][:, :], c["skip_diag"][:, hf, :], xv[p][:, hf, :], start=True, stop=False)
                y_sum(n - 2)
                b_row(n + 2)
                if n == 0:
                    conv(0, (2, 3))
                elif n == 1:
                    conv(1, (0, 1))
                elif n == 2:
                    conv(1, (2, 3))
                elif n == 4 and front:
                    pe.wait_ge(s["f_silu"], 2 * (k - 1) + 2)
                    for hf in range(DHV):
                        last = pe.matmul(GA[:, :], w_x[:, hf, :], xv[1 - p][:, hf, :], start=hf == 0, stop=hf == DHV - 1)
                    last.then_inc(s["f_ssm"], 1)
                elif n == 6 and front:
                    pe.wait_ge(s["f_split"], 4 * (k - 1) + 2)
                    pe.wait_ge(s["f_dtr"], k)
                    for hf in range(DHV):
                        last = pe.matmul((GA, GB)[hf][:, :], c["w_dt"][:, hf * P:(hf + 1) * P], dtr[:, :], start=True, stop=True)
                    last.then_inc(s["f_dt"], 1)
                elif n == 8 and output:
                    pe.wait_ge(s["n_yt"], rm)
                    pe.wait_ge(s["w_on"], rm)
                    for j in range(TS):
                        for hf in range(DHV):
                            last = pe.matmul(W[:, j * P:(j + 1) * P], yt[:, hf, j * P:(j + 1) * P], w_out[:, hf, :],
                                             start=hf == 0, stop=hf == DHV - 1)
                    last.then_inc(s["w_proj"], 1)
                elif n == 11 and gather:
                    pe.wait_ge(s["g_xn"], rg)
                    if front:
                        pe.wait_ge(s["f_pre"], k)
                    for j in range(TS):
                        last = pe.transpose(GA[:, j * P:(j + 1) * P], xn[:, j, :], c["ident"])
                    last.then_inc(s["g_t"], 1)
                c_row(n + 2)

        def act_step(act, k, half, p, gather, front, states, output):
            rg, rf, u, rm = k + 1, k, k - 2, k - 2
            first = u * NS

            def root(var, ln, dst, wait, s_ln, s_rs, r):
                act.wait_ge(wait, r)
                act.activation(ln[:, :], var, ACT.Ln, bias=EPS).then_inc(s_ln, 1)
                act.wait_ge(s_ln, r)
                act.activation(dst[:, :], ln[:, :], ACT.Exp, scale=-0.5).then_inc(s_rs, 1)

            def decays(n):
                if not of_step(n, front, states, output):
                    return
                if n == NS:
                    act.wait_ge(s["f_delta"], rf)
                since(act, s["n_h"], first + n - RING + 1)
                for hf in range(DHV):
                    last = act.activation(decay[n % RING][:, hf, :, 1:], seq(delta[p if n < NS else 1 - p][:, hf, :])[:, :, 1:], ACT.Exp,
                                          scale=c["neg_a"][:, hf, n % NS:n % NS + 1])
                last.then_inc(s["n_da"], 1)

            def copy_c(n):
                if not of_step(n, front, states, output):
                    return
                since(act, s["n_hc"], first + n - 3)
                act.wait_ge(s["n_c"], first + n + 1)
                act.activation(crep[n % 4][:, :], CB[:, :], ACT.Copy).then_inc(s["n_c_sb"], 1)

            for n in range(NS):
                copy_c(n + 1)
                decays(n + 4)
                if n == 1 and output:
                    act.wait_ge(s["n_y"], rm * NS)
                    for hf in range(DHV):
                        last = act.activation(yt[:, hf, :], YB[hf][:, :], ACT.Copy)
                    last.then_inc(s["n_yt"], 1)
                elif n == 2 and front:
                    for hf in range(DHV):
                        act.wait_ge(s["f_conv"], 2 * (k - 1) + hf + 1)
                        act.activation(xv[1 - p][:, hf, :], (GA, GB)[hf][:, :], ACT.Silu, bias=c["conv_b"][:, hf:hf + 1]).then_inc(s["f_silu"], 1)
                    act.preload_act_table_set(EXP_LN)
                elif n == 3 and gather:
                    root(mv_g[:, :, 1], ln_g, rs_g, s["g_mv"], s["g_ln"], s["g_rs"], rg)
                elif n == 4 and front:
                    act.wait_ge(s["f_ssm"], rf)
                    act.activation(dtr[:, :], GA[32:32 + DR, :], ACT.Copy).then_inc(s["f_dtr"], 1)
                elif n == 6 and front:
                    act.wait_ge(s["f_dt"], rf)
                    for hf in range(DHV):
                        last = act.activation(pre[:, hf, :], (GA, GB)[hf][:, :], ACT.Identity, bias=c["b_dt"][:, hf:hf + 1])
                    last.then_inc(s["f_pre"], 1)
                    act.wait_ge(s["f_pre"], rf)
                    act.activation(mag[:, :, :], pre[:, :, :], ACT.Abs).then_inc(s["f_abs"], 1)
                elif n == 7 and front:
                    act.wait_ge(s["f_abs"], rf)
                    act.activation(mag[:, :, :], mag[:, :, :], ACT.Exp, scale=-1.0).then_inc(s["f_exp"], 1)
                    act.wait_ge(s["f_exp"], rf)
                    act.activation(one_up[:, :, :], mag[:, :, :], ACT.Identity, bias=1.0).then_inc(s["f_u1"], 1)
                elif n == 8 and front:
                    act.wait_ge(s["f_u1"], rf)
                    act.activation(log[:, :, :], one_up[:, :, :], ACT.Ln).then_inc(s["f_log"], 1)
                    act.wait_ge(s["f_log"], rf)
                    act.activation(one_up[:, :, :], one_up[:, :, :], ACT.Identity, bias=-1.0).then_inc(s["f_back"], 1)
                elif n == 9 and gather:
                    root(mv_g[:, :, 1], ln_g, rs_g, s["g_mv2"], s["g_ln2"], s["g_rs2"], rg)
                elif n == 10 and output:
                    root(mv_w[:, :, 1], ln_w, rs_w, s["w_mv"], s["w_ln"], s["w_rs"], rm)
                elif n == 13 and gather:
                    act.wait_ge(s["g_t"], rg)
                    act.activation(xpad[p][:, :, TAPS - 1:], seq(GA), ACT.Copy).then_inc(s["g_xt"], 1)

        def dve_step(dve, k, half, p, gather, front, states, output):
            if gather:
                if not (isinstance(k, int) and k == 0):
                    dve.wait_ge(s["end_dve"], k)
                dve.tensor_scalar(al[:, :], c["alpha"][:, bass.ds(k * TS, TS)], 1.0, None, ALU.mult).then_inc(s["g_al"], 1)
            rg, rf, u, rm = k + 1, k, k - 2, k - 2
            first = u * NS

            def stats_of(src, st, out_mv, s_st, s_mv, r):
                for j in range(TS):
                    last = dve.bn_stats(st[:, j, :], src[:, j, :])
                last.then_inc(s_st, 1)
                dve.wait_ge(s_st, r)
                dve.memset(hold[:, :], 0.0)
                for j in range(TS):
                    last = dve.bn_aggr(out_mv[:, j, :], st[:, j, :])
                last.then_inc(s_mv, 1)

            def centred(dst, src, mean_var, rstd, wait, sem, r):
                dve.wait_ge(wait, r)
                for j in range(TS):
                    last = dve.tensor_scalar(dst[:, j, :], src[:, j, :], mean_var[:, j, 0:1], rstd[:, j:j + 1], ALU.subtract, ALU.mult)
                last.then_inc(sem, 1)

            def drive(n):
                if not of_step(n, front, states, output):
                    return
                if n == NS:
                    dve.wait_ge(s["f_u"], rf)
                dve.wait_ge(s["n_b"], first + n + 1)
                since(dve, s["n_h"], first + n - 1)
                dve.tensor_tensor(dbx[n % 2][:, :, :], u_in[p if n < NS else 1 - p][:, :, :], BB[n % 2][:, :].unsqueeze(1).to_broadcast([P, DHV, STEP]),
                                  ALU.mult).then_inc(s["n_dbx"], 1)

            def scan(n):
                if not of_step(n, front, states, output):
                    return
                dve.wait_ge(s["n_da"], first + n + 1)
                dve.wait_ge(s["n_dbx"], first + n + 1)
                since(dve, s["n_hc"], first + n - 3)
                dve.tensor_tensor_scan(h[n % 4].rearrange("p f t -> p (f t)"), decay[n % RING].rearrange("p f b t -> p (f b t)"),
                                       dbx[n % 2].rearrange("p f t -> p (f t)"), 0.0, ALU.mult, ALU.add).then_inc(s["n_h"], 1)

            def slot(n):
                drive(n + 1)
                scan(n)

            for n in range(NS):
                slot(n)
                if n == 1 and gather:
                    dve.wait_ge(s["g_al"], rg)
                    dve.wait_ge(loaded[p], 32 * half + 32)
                    dve.wait_ge(gathered[p], 16 * TS * half + 16 * TS)
                    for j in range(TS):
                        last = dve.scalar_tensor_tensor(o[:, j, :], ffn[p][:, j, :], al[:, j:j + 1], xl2[p][:, j, :], ALU.mult, ALU.add)
                    last.then_inc(s["g_o"], 1)
                elif n == 2 and gather:
                    dve.wait_ge(s["g_o"], rg)
                    stats_of(o, stats_g, mv_g, s["g_st"], s["g_mv"], rg)
                elif n == 5 and gather:
                    centred(o, o, mv_g, rs_g, s["g_rs"], s["g_on"], rg)
                    dve.wait_ge(s["g_on"], rg)
                    dve.wait_ge(s["g_y2_stored"], 16 * k)
                    dve.tensor_tensor(y2[:, :, :], o[:, :, :], y1[p][:, :, :], ALU.add).then_inc(s["g_y2"], 1)
                elif n == 6 and gather:
                    dve.wait_ge(s["g_y2"], rg)
                    stats_of(y2, stats_g, mv_g, s["g_st2"], s["g_mv2"], rg)
                elif n == 9 and output:
                    dve.wait_ge(s["w_proj"], rm)
                    stats_of(tok(W), stats_w, mv_w, s["w_st"], s["w_mv"], rm)
                elif n == 4 and front:
                    count = [0]

                    def chain(ins):
                        count[0] += 1
                        ins.then_inc(s["f_split"], 1)
                        dve.wait_ge(s["f_split"], 4 * (k - 1) + count[0])

                    b = bcs[1 - p]
                    dve.wait_ge(s["f_dtr"], rf)
                    chain(dve.tensor_copy(b[:, :], GA[:, :]))
                    chain(dve.tensor_tensor(rest[:, :], GA[:, :], b[:, :], ALU.subtract))
                    chain(dve.tensor_copy(b[64:, :], rest[64:, :]))
                    dve.tensor_tensor(b[96:, :], rest[96:, :], b[96:, :], ALU.subtract).then_inc(s["f_split"], 1)
                elif n == 11 and output:
                    centred(on, tok(W), mv_w, rs_w, s["w_rs"], s["w_on"], rm)
                    dve.wait_ge(s["w_on"], rm + 1)
                    dve.wait_ge(s["w_y2_loaded"], 16 * rm)
                    dve.wait_ge(s["w_stored"], 16 * (k - 3) + 1)
                    dve.tensor_tensor(y3[:, :, :], on[:, :, :], y2r[:, :, :], ALU.add).then_inc(s["w_y3"], 1)
                elif n == 10 and gather:
                    if front:
                        dve.wait_ge(s["g_t"], k)
                    centred(xn, y2, mv_g, rs_g, s["g_rs2"], s["g_xn"], rg)
                elif n == 12 and front:
                    dve.wait_ge(s["f_soft"], rf)
                    dve.scalar_tensor_tensor(delta[1 - p][:, :, :], pre[:, :, :], 0.0, log[:, :, :], ALU.max, ALU.add).then_inc(s["f_delta"], 1)
                elif n == 13 and front:
                    dve.wait_ge(s["f_delta"], rf)
                    dve.tensor_tensor(u_in[1 - p][:, :, :], delta[1 - p][:, :, :], xv[1 - p][:, :, :], ALU.mult).then_inc(s["f_u"], 1)
            dve.drain().then_inc(s["end_dve"], 1)

        def fetch(pool, pair, p):
            pool.tensor_copy(idx[p][:, :], c["slot"][:, bass.ds(pair * TS, TS)]).then_inc(s["g_idx"], 1)
            pool.wait_ge(s["g_idx"], pair + 1)
            pool.sem_inc(s["g_passed"], 1)
            for j in range(TS):
                pool.indirect_dma_start(out=ffn[p][:, j, :], out_offset=None, in_=d["sorted_out"],
                                        in_offset=bass.IndirectOffsetOnAxis(ap=idx[p][:, j:j + 1], axis=0)).then_inc(gathered[p], 16)

        def pool_step(pool, k, half, p, gather, front, states, output, load):
            u, rf = k - 2, k

            def product(n):
                if not states:
                    return
                pool.wait_ge(s["n_h"], u * NS + n + 1)
                pool.wait_ge(s["n_c_sb"], u * NS + n + 1)
                since(pool, s["n_y"], u * NS + n - 1)
                pool.tensor_tensor(hc[n % 2][:, :, :], h[n % 4][:, :, :], crep[n % 4][:, :].unsqueeze(1).to_broadcast([P, DHV, STEP]),
                                   ALU.mult).then_inc(s["n_hc"], 1)

            for n in range(NS):
                product(n)
                if n == 1 and load:
                    if not (isinstance(k, int) and k == 0):
                        pool.wait_ge(s["end_dve"], k)
                    pool.sem_inc(s["g_passed"], 1)
                    fetch(pool, k + 1, 1 - p)
                elif n == 8 and front:
                    pool.wait_ge(s["f_back"], rf)
                    pool.tensor_tensor(mag[:, :, :], mag[:, :, :], one_up[:, :, :], ALU.subtract).then_inc(s["f_lost"], 1)
                elif n == 9 and front:
                    pool.wait_ge(s["f_lost"], rf)
                    pool.tensor_tensor(log[:, :, :], log[:, :, :], mag[:, :, :], ALU.add).then_inc(s["f_soft"], 1)

        def steps(eng, step):
            step(eng, 0, 0, 0, True, False, False, False)
            step(eng, 1, 0, 1, True, True, False, False)
            step(eng, 2, 1, 0, True, True, True, False)
            with eng.Fori(0, (PAIRS - 4) // 2) as n:
                step(eng, n * 2 + 3, n + 1, 1, True, True, True, True)
                step(eng, n * 2 + 4, n + 2, 0, True, True, True, True)
            step(eng, PAIRS - 1, PAIRS // 2 - 1, 1, True, True, True, True)
            step(eng, PAIRS, PAIRS // 2, 0, False, True, True, True)
            step(eng, PAIRS + 1, PAIRS // 2, 1, False, False, True, True)
            step(eng, PAIRS + 2, PAIRS // 2 + 1, 0, False, False, False, True)

        more = lambda k: not isinstance(k, int) or k < PAIRS - 1
        block = ctx.enter_context(nc.Block())

        @block.sync
        def _(sp):
            sp.dma_start(y1[0][:, :, :], rows(d["y1"], 0)).then_inc(loaded[0], 16)
            sp.dma_start(xl2[0][:, :, :], rows(d["xl2"], 0)).then_inc(loaded[0], 16)
            steps(sp, lambda eng, k, *a: sp_step(eng, k, *a, load=more(k)))
            sp.wait_ge(s["w_stored"], 16 * PAIRS + 1)

        @block.tensor
        def _(pe):
            steps(pe, pe_step)

        @block.scalar
        def _(act):
            act.preload_act_table_set(EXP_LN)
            steps(act, act_step)

        @block.vector
        def _(dve):
            dve.sem_inc(s["w_stored"], 1)
            dve.sem_inc(s["w_on"], 1)
            for n in range(2):
                dve.memset(xpad[n][:, :, 0:TAPS - 1], 0.0)
            for n in range(RING):
                dve.memset(decay[n][:, :, :, 0:1], 0.0)
            steps(dve, dve_step)

        @block.gpsimd
        def _(pool):
            fetch(pool, 0, 0)
            steps(pool, lambda eng, k, *a: pool_step(eng, k, *a, load=more(k)))


def rotation(nc, d, c, banks, out):
    LANES = 2
    GROUPS = PAIRS // LANES
    GT = LANES * TS
    GS = LANES * STEP
    NET, GCN = 4, 3
    with ExitStack() as ctx:
        s = semaphores(nc, ctx, "rot", """
            end_pe end_act end_dve passed
            a_loaded a_st a_mv b_xl b_t b_o b_mean b_gc b_gc_sb b_base
            c_net c_net_sb c_rot c_cp c_turn c_o d_t d_st d_mv ln rs e_loaded e_on e_sum e_stored""")
        sb = lambda name, shape, dtype=fp32: ctx.enter_context(nc.sbuf_tensor(name, shape, dtype))
        two = lambda name, shape, dtype=fp32: [sb(f"{name}{n}", shape, dtype) for n in range(2)]
        y3 = two("r_y3", [P, GT, D])
        xl = sb("r_xl", [P, GT, D])
        o_t = two("r_o_t", [P, LANES, STEP])
        o_f = two("r_o_f", [P, LANES, STEP])
        stats = sb("r_stats", [P, 2 * GT, 6])
        mv = two("r_mean_var", [P, 2 * GT, 2])
        ln = sb("r_ln", [P, 2 * GT])
        rs = two("r_rstd", [P, 2 * GT])
        total = sb("r_total", [P, 2 * LANES])
        gc1 = sb("gc1", [64, 2 * LANES])
        gc2 = sb("gc2", [32, 2 * LANES])
        gc3 = sb("gc3", [P, 2 * LANES])
        base = two("r_base", [P, 2 * LANES])
        net1 = [sb(f"net1_{n}", [P, STEP]) for n in range(LANES)]
        net2 = [sb(f"net2_{n}", [P, T]) for n in range(LANES)]
        net3 = [sb(f"net3_{n}", [64, T]) for n in range(LANES)]
        th = [sb(f"r_th{n}", [P, STEP]) for n in range(LANES)]
        cp = [sb(f"r_cp{n}", [P, STEP]) for n in range(LANES)]
        y3_e = sb("r_y3_e", [P, GT, D])
        fin = sb("r_fin", [P, GT, D])
        res = sb("r_res", [P, GT, D])
        half_cn = sb("half_cn", [P, 1])
        half_gc = sb("half_gc", [P, 1])
        ar3 = sb("ar3", [P, 1])
        ar7 = sb("ar7", [P, 1])
        hold = sb("r_hold", [P, 1])
        W, TW, HB, DB = banks[0:2], banks[2:4], banks[4:6], banks[6:8]
        tok = lambda t: t.rearrange("p (j d) -> p j d", j=TS)
        rows = lambda ap, at: ap[bass.ds(at, GS), :].rearrange("(j p) d -> p j d", p=P)

        def begin(eng, k):
            if isinstance(k, int) and k == 0:
                return
            for sem in (s["end_pe"], s["end_act"], s["end_dve"]):
                eng.wait_ge(sem, k)

        def sp_step(sp, k, p, norm, turn_in, cycles, turn_back, finish):
            now, re = (sp.snap(v) for v in (k * 1, k - 3 if finish else k * 1))
            here, back = (sp.snap(v) for v in (k * GS, k * GS - 4 * GS if finish else k * GS))
            if not (isinstance(k, int) and k == 0):
                sp.wait_ge(s["end_dve"], now)
            if norm:
                sp.dma_start(y3[p][:, :, :], rows(d["y3"], here)).then_inc(s["a_loaded"], 16)
            if finish:
                sp.dma_start(y3_e[:, :, :], rows(d["y3"], back)).then_inc(s["e_loaded"], 16)
                sp.wait_ge(s["e_sum"], re)
                sp.dma_start(rows(out, back), res[:, :, :]).then_inc(s["e_stored"], 16)

        def pe_step(pe, k, p, norm, turn_in, cycles, turn_back, finish):
            begin(pe, k)
            f, m = k - 1, k - 2

            def at(i, layer, lane):
                return ((m * CYCLES + i) * NET + layer) * LANES + lane

            def net(i, layer):
                if not cycles:
                    return
                for lane in range(LANES):
                    if layer == 0:
                        if i:
                            pe.wait_ge(s["c_o"], (m * CYCLES + i - 1) * LANES + lane + 1)
                        pe.matmul(W[lane][:, :], c["cn_w1"], o_t[p][:, lane, :], start=True, stop=True).then_inc(s["c_net"], 1)
                        continue
                    pe.wait_ge(s["c_net_sb"], at(i, layer - 1, lane) + 1)
                    if layer == 1:
                        for b in range(2):
                            last = pe.matmul(W[lane][64 * b:64 * b + 64, 0:T], c["cn_w2"], net1[lane][:, b * T:(b + 1) * T],
                                             start=True, stop=True, tile_position=(0, 64 * b))
                    elif layer == 2:
                        last = pe.matmul(W[lane][0:64, 0:T], c["cn_w3"], net2[lane][:, :], start=True, stop=True)
                    else:
                        pe.sem_inc(s["passed"], 1)
                        for b in range(2):
                            last = pe.matmul(W[lane][:, b * T:(b + 1) * T], c["cn_w4"][0:64, b * P:(b + 1) * P], net3[lane][:, :],
                                             start=b == 0, stop=True, skip_group_check=True)
                    last.then_inc(s["c_net"], 1)

            def rotated(i, lanes):
                if not cycles:
                    return
                for lane in lanes:
                    pe.matmul(TW[lane][:, :], c["twist"], o_t[p][:, lane, :], start=True, stop=True).then_inc(s["c_rot"], 1)

            def context(i):
                if not turn_in:
                    return
                if i == 0:
                    pe.wait_ge(s["b_mean"], k)
                    pe.matmul(HB[0][0:64, 0:2 * LANES], c["gc_w1"], total[:, :], start=True, stop=True).then_inc(s["b_gc"], 1)
                    return
                pe.wait_ge(s["b_gc_sb"], f * GCN + i)
                pe.sem_inc(s["passed"], 1)
                if i == 1:
                    pe.matmul(HB[0][0:32, 0:2 * LANES], c["gc_w2"][0:64, :], gc1[:, :], start=True, stop=True).then_inc(s["b_gc"], 1)
                else:
                    pe.matmul(HB[0][:, 0:2 * LANES], c["gc_w3"][0:32, :], gc2[:, :], start=True, stop=True).then_inc(s["b_gc"], 1)

            net(0, 0)
            rotated(0, (0,))
            net(0, 1)
            rotated(0, (1,))
            if turn_in:
                for lane in range(LANES):
                    pe.wait_ge(s["b_xl"], f * LANES + lane + 1)
                    for j in range(TS):
                        last = pe.transpose(HB[lane][:, j * P:(j + 1) * P], xl[:, lane * TS + j, :], c["ident"])
                    last.then_inc(s["b_t"], 1)
            net(0, 2)
            net(0, 3)
            if turn_back:
                for lane in range(LANES):
                    if finish:
                        pe.wait_ge(s["e_on"], (k - 4) * LANES + lane + 1)
                    for j in range(TS):
                        last = pe.transpose(DB[lane][:, j * P:(j + 1) * P], o_f[1 - p][:, lane, j * P:(j + 1) * P], c["ident"])
                    last.then_inc(s["d_t"], 1)
            for i in range(1, CYCLES):
                net(i, 0)
                rotated(i, (0,))
                if i == 1:
                    context(0)
                net(i, 1)
                rotated(i, (1,))
                if i == 1:
                    context(1)
                net(i, 2)
                if i == 1:
                    context(2)
                net(i, 3)
            pe.drain().then_inc(s["end_pe"], 1)

        def act_step(act, k, p, norm, turn_in, cycles, turn_back, finish):
            begin(act, k)
            f, m = k - 1, k - 2

            def net(i, layer):
                if not cycles:
                    return
                for lane in range(LANES):
                    act.wait_ge(s["c_net"], ((m * CYCLES + i) * NET + layer) * LANES + lane + 1)
                    if layer == 0:
                        ins = act.activation(net1[lane][:, :], W[lane][:, :], ACT.Gelu, bias=c["cn_b1"])
                    elif layer == 1:
                        ins = act.activation(net2[lane][:, :], W[lane][:, 0:T], ACT.Gelu, bias=c["cn_b2"])
                    elif layer == 2:
                        ins = act.activation(net3[lane][:, :], W[lane][0:64, 0:T], ACT.Gelu, bias=c["cn_b3"][0:64, :])
                    else:
                        ins = act.activation(th[lane][:, :], W[lane][:, :], ACT.Tanh, bias=half_cn[:, :], scale=0.5)
                    ins.then_inc(s["c_net_sb"], 1)

            def context(i):
                if not turn_in:
                    return
                act.wait_ge(s["b_gc"], f * GCN + i + 1)
                if i == 0:
                    ins = act.activation(gc1[:, :], HB[0][0:64, 0:2 * LANES], ACT.Gelu, bias=c["gc_b1"][0:64, :], scale=1.0 / T)
                elif i == 1:
                    ins = act.activation(gc2[:, :], HB[0][0:32, 0:2 * LANES], ACT.Gelu, bias=c["gc_b2"][0:32, :])
                else:
                    ins = act.activation(gc3[:, :], HB[0][:, 0:2 * LANES], ACT.Tanh, bias=half_gc[:, :], scale=0.5)
                ins.then_inc(s["b_gc_sb"], 1)

            net(0, 0)
            if turn_in:
                for lane in range(LANES):
                    act.wait_ge(s["b_t"], f * LANES + lane + 1)
                    act.activation(o_t[1 - p][:, lane, :], HB[lane][:, :], ACT.Copy).then_inc(s["b_o"], 1)
            net(0, 1)
            net(0, 2)
            net(0, 3)
            for i in range(1, CYCLES):
                for layer in range(NET):
                    net(i, layer)
                    if i == 1 and layer < GCN:
                        context(layer)
            if norm or turn_back:
                act.preload_act_table_set(EXP_LN)
                lo, hi = 0 if norm else GT, 2 * GT if turn_back else GT
                steps_before = k
                if norm:
                    act.wait_ge(s["a_mv"], k + 1)
                if turn_back:
                    act.wait_ge(s["d_mv"], k - 2)
                act.activation(ln[:, lo:hi], mv[p][:, lo:hi, 1], ACT.Ln, bias=EPS).then_inc(s["ln"], 1)
                act.wait_ge(s["ln"], steps_before + 1)
                act.activation(rs[p][:, lo:hi], ln[:, lo:hi], ACT.Exp, scale=-0.5).then_inc(s["rs"], 1)
            else:
                act.sem_inc(s["ln"], 1)
            act.drain().then_inc(s["end_act"], 1)

        def dve_step(dve, k, p, norm, turn_in, cycles, turn_back, finish):
            begin(dve, k)
            f, m, e = k - 1, k - 2, k - 4

            def stats_of(src, lane, lo, s_st, s_mv, r, last_lane):
                for j in range(TS):
                    last = dve.bn_stats(stats[:, lo + j, :], src[:, j, :])
                last.then_inc(s_st, 1)
                dve.wait_ge(s_st, r)
                dve.memset(hold[:, :], 0.0)
                for j in range(TS):
                    last = dve.bn_aggr(mv[p][:, lo + j, :], stats[:, lo + j, :])
                if last_lane:
                    last.then_inc(s_mv, 1)

            def centred(dst, src, lane, lo, sem):
                for j in range(TS):
                    t = lo + lane * TS + j
                    last = dve.tensor_scalar(dst[:, lane * TS + j, :], src[:, j, :], mv[1 - p][:, t, 0:1], rs[1 - p][:, t:t + 1], ALU.subtract, ALU.mult)
                last.then_inc(sem, 1)

            def turn_base(i, lane):
                if not cycles:
                    return
                dve.wait_ge(s["c_rot"], (m * CYCLES + i) * LANES + lane + 1)
                for b in range(2):
                    o = o_t[p][:, lane, b * T:(b + 1) * T]
                    last = dve.scalar_tensor_tensor(o, TW[lane][:, b * T:(b + 1) * T], base[p][:, 2 * lane + b:2 * lane + b + 1], o, ALU.mult, ALU.add)
                last.then_inc(s["c_cp"], 1)

            def turn(i, lane):
                if not cycles:
                    return
                n = (m * CYCLES + i) * LANES + lane + 1
                dve.wait_ge(s["c_net_sb"], ((m * CYCLES + i) * NET + NET - 1) * LANES + lane + 1)
                dve.scalar_tensor_tensor(cp[lane][:, :], th[lane][:, :], ar3[:, :], TW[lane][:, :], ALU.mult, ALU.mult).then_inc(s["c_turn"], 1)
                dve.wait_ge(s["c_turn"], n)
                dve.wait_ge(s["c_cp"], n)
                dst = o_t if i < CYCLES - 1 else o_f
                dve.tensor_tensor(dst[p][:, lane, :], o_t[p][:, lane, :], cp[lane][:, :], ALU.add).then_inc(s["c_o"], 1)

            if turn_in:
                for lane in range(LANES):
                    centred(xl, y3[1 - p][:, lane * TS:(lane + 1) * TS, :], lane, 0, s["b_xl"])
            if finish:
                for lane in range(LANES):
                    centred(fin, tok(DB[lane]), lane, GT, s["e_on"])
                dve.wait_ge(s["e_on"], e * LANES + LANES)
                dve.wait_ge(s["e_loaded"], 16 * e + 16)
                dve.wait_ge(s["e_stored"], 16 * e + 1)
                dve.tensor_tensor(res[:, :, :], fin[:, :, :], y3_e[:, :, :], ALU.add).then_inc(s["e_sum"], 1)
            turn_base(0, 0)
            turn_base(0, 1)
            turn(0, 0)
            turn(0, 1)
            if turn_in:
                dve.wait_ge(s["b_o"], f * LANES + LANES)
                dve.tensor_reduce(total[:, :], o_t[1 - p].rearrange("p l (b t) -> p (l b) t", b=2), AX.X, ALU.add).then_inc(s["b_mean"], 1)
            if norm:
                dve.wait_ge(s["a_loaded"], 16 * k + 16)
                for lane in range(LANES):
                    stats_of(y3[p][:, lane * TS:(lane + 1) * TS, :], lane, lane * TS, s["a_st"], s["a_mv"], k * LANES + lane + 1, lane == LANES - 1)
            turn_base(1, 0)
            turn_base(1, 1)
            turn(1, 0)
            turn(1, 1)
            if turn_back:
                for lane in range(LANES):
                    dve.wait_ge(s["d_t"], (k - 3) * LANES + lane + 1)
                    stats_of(tok(DB[lane]), lane, GT + lane * TS, s["d_st"], s["d_mv"], (k - 3) * LANES + lane + 1, lane == LANES - 1)
            if turn_in:
                dve.wait_ge(s["b_gc_sb"], f * GCN + GCN)
                dve.tensor_scalar(base[1 - p][:, :], gc3[:, :], ar7[:, :], 0.1, ALU.mult, ALU.add).then_inc(s["b_base"], 1)
            turn_base(2, 0)
            turn_base(2, 1)
            turn(2, 0)
            turn(2, 1)
            dve.drain().then_inc(s["end_dve"], 1)

        def steps(eng, step):
            for k in range(4):
                step(eng, k, k % 2, True, k > 0, k > 1, k > 2, False)
            with eng.Fori(0, (GROUPS - 4) // 2) as n:
                for p in range(2):
                    step(eng, n * 2 + (4 + p), p, True, True, True, True, True)
            for k in range(GROUPS, GROUPS + 4):
                step(eng, k, k % 2, False, k < GROUPS + 1, k < GROUPS + 2, k < GROUPS + 3, True)

        block = ctx.enter_context(nc.Block())

        @block.sync
        def _(sp):
            steps(sp, sp_step)
            sp.wait_ge(s["e_stored"], 16 * GROUPS + 1)

        @block.tensor
        def _(pe):
            steps(pe, pe_step)

        @block.scalar
        def _(act):
            steps(act, act_step)

        @block.vector
        def _(dve):
            dve.sem_inc(s["e_stored"], 1)
            dve.tensor_scalar(half_cn[:, :], c["cn_b4"], 0.5, None, ALU.mult)
            dve.tensor_scalar(half_gc[:, :], c["gc_b3"], 0.5, None, ALU.mult)
            dve.tensor_scalar(ar3[:, :], c["arange"], 0.3, None, ALU.mult)
            dve.tensor_scalar(ar7[:, :], c["arange"], 0.7, None, ALU.mult)
            steps(dve, dve_step)


CONSTS = [("ident", P), ("mask", P), ("ones_blk", P), ("strict", P), ("ones", P), ("twist", P), ("cos", T), ("sin", T),
          ("head_mask", HS), ("sel_cols", 32), ("reset", STEP), ("eye8", E * E), ("tile_no", ETILES)]
VECS = [("gate_b", 1), ("clock_b", 1), ("p_b", 1), ("ln1_g", 1), ("ln1_b", 1), ("ln2_g", 1), ("ln2_b", 1), ("mlp_b1", FC),
        ("conv_b", DHV), ("b_dt", DHV), ("skip", DHV), ("cn_b1", 1), ("cn_b2", 1), ("cn_b3", 1), ("cn_b4", 1),
        ("gc_b1", 1), ("gc_b2", 1), ("gc_b3", 1), ("arange", 1)]
W_A = [("w_gate", D), ("w_clock", D), ("w_p", D), ("w_q", D), ("w_qs", D), ("w_k", D), ("w_ks", D), ("w_v", D), ("w_o", D),
       ("w_up", F), ("w_down", F)]
W_C = [("w_in", DI), ("w_x", DHV * P), ("w_out", DHV * D), ("cn_w1", 128), ("cn_w2", 64), ("cn_w3", 64), ("cn_w4", 2 * P),
       ("gc_w1", 64), ("gc_w2", 32), ("gc_w3", P)]


def constants():
    f = np.float32
    row, col = np.arange(P)[:, None], np.arange(P)[None, :]
    half = DH // 2
    freqs = np.exp(-np.arange(half, dtype=f) * f(np.log(10000.0) / half)).astype(f)
    theta = np.arange(T, dtype=f)[None, :] * freqs[:, None]
    angle = theta[(np.arange(P) % DH) // 2]
    sign = np.where(np.arange(P) % 2 == 0, -1.0, 1.0)[:, None]
    quarter = P // 4
    twist = np.zeros((P, P), f)
    for to, of, by in ((0, 2, 1), (1, 3, -1), (2, 0, -1), (3, 1, 1)):
        twist[of * quarter + np.arange(quarter), to * quarter + np.arange(quarter)] = by
    parts = dict(
        ident=row == col, mask=np.where(row > col, -BIG, 0.0), ones_blk=row // DH == col // DH, strict=row < col,
        ones=np.ones((P, P)), twist=twist, cos=np.cos(angle), sin=np.sin(angle) * sign,
        head_mask=(np.arange(P)[:, None] // DH) % HS == np.arange(HS)[None, :],
        sel_cols=(row % 32 == np.arange(32)[None, :]) & (row // 32 != 1),
        reset=np.broadcast_to(np.arange(STEP)[None, :] % T != 0, (P, STEP)),
        eye8=np.broadcast_to(np.eye(E).reshape(1, E * E), (P, E * E)),
        tile_no=np.broadcast_to(np.arange(ETILES)[None, :], (P, ETILES)))
    return np.concatenate([np.asarray(parts[n], f) for n, _ in CONSTS], axis=1)


def laid_out(i):
    def column(v, rows=P):
        v = np.asarray(v).reshape(-1)
        if v.size < rows:
            v = np.concatenate([v, np.zeros(rows - v.size, v.dtype)])
        return v.reshape(-1, rows).T

    def down(w):
        w = np.asarray(w)
        return np.concatenate([w, np.zeros((P - w.shape[0], w.shape[1]), w.dtype)]) if w.shape[0] < P else w

    a = lambda n: np.asarray(i["L0_attn_" + n])
    e = lambda n: np.asarray(i["L0_ffn_" + n])
    m = lambda n: np.asarray(i["L1_attn_" + n])
    n_ = lambda n: np.asarray(i["L1_ffn_" + n])
    swap = np.arange(D) ^ 1
    heads = lambda w: np.repeat(w, DH, axis=-1)
    all_rows = lambda w: np.repeat(w, P, axis=1)
    blocks = lambda w: np.block([[w, np.zeros_like(w)], [np.zeros_like(w), w]])
    wx = m("W_x")
    bc, gap = wx[:, DR:], np.zeros((DI, 32 - DR), wx.dtype)
    bcd = np.concatenate([bc, wx[:, :DR], gap, bc, bc], axis=1)
    w_a = dict(w_gate=a("gate_w"), w_clock=heads(a("clock_w")), w_p=a("p_w"), w_q=a("Wq"), w_qs=a("Wq")[:, swap],
               w_k=a("Wk"), w_ks=a("Wk")[:, swap], w_v=a("Wv"), w_o=a("out_w"), w_up=a("mlp_w1"),
               w_down=a("mlp_w2").reshape(FC, P, D).transpose(1, 0, 2).reshape(P, -1))
    w_c = dict(w_in=m("W_in"), w_x=bcd.reshape(DHV, P, -1).transpose(1, 0, 2).reshape(P, -1),
               w_out=m("W_out").reshape(DHV, P, D).transpose(1, 0, 2).reshape(P, -1),
               cn_w1=n_("cn_w1"), cn_w2=n_("cn_w2"), cn_w3=blocks(n_("cn_w3")), cn_w4=blocks(all_rows(n_("cn_w4"))),
               gc_w1=n_("gc_w1"), gc_w2=n_("gc_w2"), gc_w3=all_rows(n_("gc_w3")))
    vec = dict(gate_b=a("gate_b"), clock_b=heads(a("clock_b")), p_b=a("p_b"), ln1_g=a("ln1_g"), ln1_b=a("ln1_b"),
               ln2_g=a("ln2_g"), ln2_b=a("ln2_b"), mlp_b1=a("mlp_b1"), conv_b=m("conv_b"), b_dt=m("b_dt"), skip=m("D"),
               cn_b1=n_("cn_b1"), cn_b2=np.tile(n_("cn_b2"), 2), cn_b3=np.tile(n_("cn_b3"), 2), cn_b4=np.repeat(n_("cn_b4"), P),
               gc_b1=n_("gc_b1"), gc_b2=n_("gc_b2"), gc_b3=np.repeat(n_("gc_b3"), P), arange=np.repeat(n_("adaptive_range"), P))
    return dict(
        x=a("x").reshape(N, D),
        consts=constants(),
        w_a=np.concatenate([w_a[n] for n, _ in W_A], axis=1),
        w_c=np.concatenate([down(w_c[n]) for n, _ in W_C], axis=1),
        vec=np.concatenate([column(vec[n]) for n, _ in VECS], axis=1),
        rows=np.repeat(np.stack([a("out_b"), a("mlp_b2")])[None], P, axis=0),
        cent=e("centroids").T,
        e_vec=np.concatenate([e("ln_g").T, e("ln_b").T], axis=1),
        w_1=e("w1").transpose(1, 0, 2).reshape(D, E * F),
        w_2=e("w2").reshape(E, FC, P, D).transpose(2, 0, 1, 3).reshape(P, E * F),
        b_1=e("b1"), b_2=e("b2"),
        a_log=m("A_log").reshape(DHV, P, NS).transpose(1, 0, 2),
        conv_w=np.repeat(m("conv_w")[:, 0, :].T[None], P, axis=0),
        w_dt=m("W_dt"),
    )


def kernel(**inputs):
    import concourse.bacc as _bacc
    from concourse import mybir as _mybir
    from concourse.bass_utils import run_bass_kernel_spmd as _run

    nc = _bacc.Bacc("TRN2", target_bir_lowering=False, num_devices=1)
    arrays, dram = {}, {}
    for name, a in laid_out(inputs).items():
        a = np.ascontiguousarray(a)
        arrays[f"in_{name}_dram"] = a
        dram[name] = nc.dram_tensor(f"in_{name}_dram", a.shape, _mybir.dt.from_np(a.dtype), kind="ExternalInput").ap()
    out = nc.dram_tensor("out_dram", (N, D), fp32, kind="ExternalOutput").ap()
    program(nc, dram, out)
    r = _run(nc, [arrays], core_ids=[0])
    return r.results[0]["out_dram"].reshape(SEQS, T, D)
```
